# Optimizing a Trainium2 kernel written in Bass

```python
import numpy as np
import jax
import jax.numpy as jnp

def _softmax(x, axis=-1):
    return jax.nn.softmax(x, axis=axis)

def _gelu(x):
    return jax.nn.gelu(x, approximate=True)

def _silu(x):
    return jax.nn.silu(x)

def _sigmoid(x):
    return jax.nn.sigmoid(x)

def _layernorm(x, axis=-1, eps=1e-05):
    m = jnp.mean(x, axis=axis, keepdims=True)
    v = jnp.var(x, axis=axis, keepdims=True)
    return (x - m) / jnp.sqrt(v + eps)

def _scatter_add(tgt, idx, src, axis=0):
    return tgt.at[idx].add(src)

def _segment_sum(src, seg, n):
    return jax.ops.segment_sum(src, seg, n)
kernel_name = 'mk_early_fusion_d1_tok_img768_r4_9ab775'

def setup_inputs(seed: int=0):
    np.random.seed(seed)
    _w = jnp.asarray

    def _rec_inputs():
        import jax
        import jax.numpy as jnp
        _rk = jax.random.key(seed)
        x = 1.64766e-05 + 1.00005 * jax.random.normal(jax.random.fold_in(_rk, 1), (8, 3, 512, 192), jnp.float32)
        txt = -0.000331106 + 0.408041 * jax.random.normal(jax.random.fold_in(_rk, 2), (8, 128, 192), jnp.float32)
        return (x, txt)
    x, txt = _rec_inputs()

    def _L0_tok_setup():
        import jax, jax.numpy as jnp
        import numpy as np
        NUM_BANDS = 6
        D_MODEL = 192
        B, N = (2, 512)
        IN_FEATURES = 3 * NUM_BANDS * 2 * D_MODEL
        key = jax.random.key(seed)
        k_xyz, k_w = jax.random.split(key)
        xyz = jax.random.normal(k_xyz, (B, 3, N, D_MODEL), dtype=jnp.float32)
        freq_bands = 2.0 ** jnp.linspace(0.0, NUM_BANDS - 1, NUM_BANDS).astype(jnp.float32)
        bound = 1.0 / np.sqrt(IN_FEATURES)
        W = jax.random.uniform(k_w, (D_MODEL, IN_FEATURES), dtype=jnp.float32, minval=-bound, maxval=bound)
        return {'xyz': xyz, 'freq_bands': freq_bands, 'W': W}
    _L0_tok_all = _L0_tok_setup()
    _L0_tok_in = {k: v for k, v in _L0_tok_all.items() if k in ('freq_bands', 'W')}
    del _L0_tok_all

    def _L0_attn_setup():
        import math
        import jax, jax.numpy as jnp
        import numpy as np
        D_MODEL = 192
        N_HEAD = 12
        HEAD_DIM = D_MODEL // N_HEAD
        ROPE_BASE = 10000.0
        EPS = 1e-06

        def rotary_cache(seq_len, head_dim, base=ROPE_BASE):
            half = head_dim // 2
            freq = 1.0 / base ** (jnp.arange(half, dtype=jnp.float32) / half)
            freqs = jnp.arange(seq_len, dtype=jnp.float32)[:, None] * freq[None, :]
            return (jnp.cos(freqs), jnp.sin(freqs))

        def apply_rope(x, cos, sin):
            cos = cos.astype(x.dtype)
            sin = sin.astype(x.dtype)
            x1 = x[..., ::2]
            x2 = x[..., 1::2]
            out = jnp.stack((x1 * cos - x2 * sin, x1 * sin + x2 * cos), axis=-1)
            return out.reshape(x.shape)
        key = jax.random.key(seed)
        kx, kq, kk, kv, kp = jax.random.split(key, 5)
        B, S, D = (2, 512, D_MODEL)
        x = jax.random.normal(kx, (B, S, D), dtype=jnp.float32)
        scale = 0.02
        Wq = jax.random.normal(kq, (D, D), dtype=jnp.float32) * scale
        Wk = jax.random.normal(kk, (D, D), dtype=jnp.float32) * scale
        Wv = jax.random.normal(kv, (D, D), dtype=jnp.float32) * scale
        Wproj = jax.random.normal(kp, (D, D), dtype=jnp.float32) * scale
        return {'x': x, 'Wq': Wq, 'Wk': Wk, 'Wv': Wv, 'Wproj': Wproj}
    _L0_attn_all = _L0_attn_setup()
    _L0_attn_in = {k: v for k, v in _L0_attn_all.items() if k in ('Wq', 'Wk', 'Wv', 'Wproj')}
    del _L0_attn_all

    def _L0_ffn_setup():
        import jax, jax.numpy as jnp
        import numpy as np
        CAPACITY_FACTOR = 1.25
        key = jax.random.key(seed)
        ks = jax.random.split(key, 5)
        B, S, D, F, E = (8, 512, 192, 768, 8)
        return {'x': jax.random.normal(ks[0], (B, S, D), jnp.float32), 'switch_w': jax.random.normal(ks[1], (D, E), jnp.float32) * 0.02, 'switch_b': jnp.zeros((E,), jnp.float32), 'w1': jax.random.normal(ks[2], (E, D, F), jnp.float32) * 0.02, 'b1': jnp.zeros((E, F), jnp.float32), 'w2': jax.random.normal(ks[3], (E, F, D), jnp.float32) * 0.02, 'b2': jnp.zeros((E, D), jnp.float32)}
    _L0_ffn_all = _L0_ffn_setup()
    _L0_ffn_in = {k: v for k, v in _L0_ffn_all.items() if k in ('switch_w', 'switch_b', 'w1', 'b1', 'w2', 'b2')}
    del _L0_ffn_all
    return {'x': x, 'txt': txt, 'L0_tok_freq_bands': _L0_tok_in['freq_bands'], 'L0_tok_W': _L0_tok_in['W'], 'L0_attn_Wq': _L0_attn_in['Wq'], 'L0_attn_Wk': _L0_attn_in['Wk'], 'L0_attn_Wv': _L0_attn_in['Wv'], 'L0_attn_Wproj': _L0_attn_in['Wproj'], 'L0_ffn_switch_w': _L0_ffn_in['switch_w'], 'L0_ffn_switch_b': _L0_ffn_in['switch_b'], 'L0_ffn_w1': _L0_ffn_in['w1'], 'L0_ffn_b1': _L0_ffn_in['b1'], 'L0_ffn_w2': _L0_ffn_in['w2'], 'L0_ffn_b2': _L0_ffn_in['b2']}

def reference(x, txt, L0_tok_freq_bands, L0_tok_W, L0_attn_Wq, L0_attn_Wk, L0_attn_Wv, L0_attn_Wproj, L0_ffn_switch_w, L0_ffn_switch_b, L0_ffn_w1, L0_ffn_b1, L0_ffn_w2, L0_ffn_b2):
    import jax
    import jax.numpy as jnp

    def _L0_tok_ref(xyz, freq_bands, W):
        import jax, jax.numpy as jnp
        import numpy as np
        NUM_BANDS = 6
        D_MODEL = 192
        B, N = (2, 512)
        IN_FEATURES = 3 * NUM_BANDS * 2 * D_MODEL
        b, c, n, d = xyz.shape
        xb = 2.0 * jnp.pi * xyz[..., None] * freq_bands
        feat = jnp.concatenate([jnp.sin(xb), jnp.cos(xb)], axis=-1)
        feat = feat.reshape(b, n, -1)
        return jnp.einsum('bnf,of->bno', feat, W)

    def _L0_attn_ref(x, Wq, Wk, Wv, Wproj):
        import math
        import jax, jax.numpy as jnp
        import numpy as np
        D_MODEL = 192
        N_HEAD = 12
        HEAD_DIM = D_MODEL // N_HEAD
        ROPE_BASE = 10000.0
        EPS = 1e-06

        def rotary_cache(seq_len, head_dim, base=ROPE_BASE):
            half = head_dim // 2
            freq = 1.0 / base ** (jnp.arange(half, dtype=jnp.float32) / half)
            freqs = jnp.arange(seq_len, dtype=jnp.float32)[:, None] * freq[None, :]
            return (jnp.cos(freqs), jnp.sin(freqs))

        def apply_rope(x, cos, sin):
            cos = cos.astype(x.dtype)
            sin = sin.astype(x.dtype)
            x1 = x[..., ::2]
            x2 = x[..., 1::2]
            out = jnp.stack((x1 * cos - x2 * sin, x1 * sin + x2 * cos), axis=-1)
            return out.reshape(x.shape)
        B, S, D = x.shape
        H, hd = (N_HEAD, HEAD_DIM)

        def heads(W):
            return (x @ W.T).reshape(B, S, H, hd).transpose(0, 2, 1, 3)
        q, k, v = (heads(Wq), heads(Wk), heads(Wv))
        cos, sin = rotary_cache(S, hd)
        cos = cos[None, None]
        sin = sin[None, None]
        q = apply_rope(q, cos, sin)
        k = apply_rope(k, cos, sin)
        scores = jnp.einsum('bhsd,bhtd->bhst', q.astype(jnp.float32), k.astype(jnp.float32))
        scores = scores / math.sqrt(hd)
        weights = jax.lax.erf(scores) + 1.0
        mask = jnp.tril(jnp.ones((S, S), dtype=bool))[None, None]
        weights = jnp.where(mask, weights, 0.0)
        denom = jnp.maximum(weights.sum(axis=-1, keepdims=True), EPS)
        y = jnp.einsum('bhst,bhtd->bhsd', weights, v.astype(jnp.float32)) / denom
        y = y.astype(v.dtype)
        y = y.transpose(0, 2, 1, 3).reshape(B, S, D)
        return y @ Wproj.T

    def _L0_ffn_ref(x, switch_w, switch_b, w1, b1, w2, b2):
        import jax, jax.numpy as jnp
        import numpy as np
        CAPACITY_FACTOR = 1.25
        B, S, D = x.shape
        E = w1.shape[0]
        xf = x.reshape(-1, D)
        N = xf.shape[0]
        capacity = int(CAPACITY_FACTOR * N / E)
        probs = jax.nn.softmax(xf @ switch_w + switch_b, axis=-1)
        prob_max = jnp.max(probs, axis=-1)
        routes = jnp.argmax(probs, axis=-1)
        sort_idx = jnp.lexsort((-prob_max, routes))
        counts = jnp.bincount(routes, length=E)
        starts = jnp.concatenate([jnp.zeros((1,), counts.dtype), jnp.cumsum(counts)[:-1]])
        rank_sorted = jnp.arange(N) - starts[routes[sort_idx]]
        rank = jnp.zeros((N,), jnp.int32).at[sort_idx].set(rank_sorted.astype(jnp.int32))
        keep = rank < capacity
        dest_e = jnp.where(keep, routes, E)
        dest_c = jnp.where(keep, rank, 0)
        buf = jnp.zeros((E + 1, capacity, D), xf.dtype).at[dest_e, dest_c].set(xf)
        h = jax.nn.gelu(jnp.einsum('ecd,edf->ecf', buf[:E], w1) + b1[:, None, :], approximate=False)
        o = jnp.einsum('ecf,efd->ecd', h, w2) + b2[:, None, :]
        y_exp = o[routes, dest_c]
        y = jnp.where(keep[:, None], y_exp, xf)
        out = y * prob_max[:, None]
        return out.reshape(B, S, D)
    h = _L0_tok_ref(x, L0_tok_freq_bands, L0_tok_W)
    h = jnp.concatenate([h, txt], axis=1)
    h = h + _L0_attn_ref(_layernorm(h, axis=-1), L0_attn_Wq, L0_attn_Wk, L0_attn_Wv, L0_attn_Wproj)
    h = h + _L0_ffn_ref(_layernorm(h, axis=-1), L0_ffn_switch_w, L0_ffn_switch_b, L0_ffn_w1, L0_ffn_b1, L0_ffn_w2, L0_ffn_b2)
    return h

_drawn_inputs = setup_inputs


def setup_inputs(seed=0):
    import zlib

    import numpy as np

    out = dict(_drawn_inputs(seed))
    spreads = {'L0_ffn_switch_b': (0.0, 0.1), 'L0_ffn_b1': (0.0, 0.633), 'L0_ffn_b2': (0.0, 0.1)}
    factors = {'L0_attn_Wq': 5.649, 'L0_attn_Wk': 4.803}
    for name, (base, spread) in spreads.items():
        noise = np.random.default_rng([zlib.crc32(name.encode()), seed]).standard_normal(out[name].shape)
        drawn = base * np.exp(spread * noise) if base else spread * noise
        out[name] = jnp.asarray(drawn.astype(out[name].dtype))
    for name, factor in factors.items():
        out[name] = (out[name] * factor).astype(out[name].dtype)
    return out
```

```python
from contextlib import ExitStack

import concourse.bass as bass
from concourse import mybir

F32, F16, I32, U32 = mybir.dt.float32, mybir.dt.float16, mybir.dt.int32, mybir.dt.uint32
ALU = mybir.AluOpType
ACT = mybir.ActivationFunctionType
AX_X = mybir.AxisListType.X

P = 128
BATCHES, IMG, TXT, D = 8, 512, 128, 192
SEQ = IMG + TXT
TILES = SEQ // P
IMG_TILES = IMG // P
ALL_TILES = BATCHES * TILES
CH = 3 * D
BANDS = 6
FEATURES = CH * 2 * BANDS
HEADS, HD = 12, 16
HALF = D // 2
EXPERTS, HIDDEN = 8, 768
TOKENS = BATCHES * SEQ
CAPACITY = int(1.25 * TOKENS / EXPERTS)
SLOTS = EXPERTS * CAPACITY
ROWS = 4
BLOCK = 400
BLOCK_P = BLOCK // ROWS
PER_EXPERT = CAPACITY // BLOCK
BLOCKS = EXPERTS * PER_EXPERT
F_TILES = HIDDEN // P
TWO_PI = 6.283185307179586
HALF_PI = 1.5707963267948966
ROUND = 1.5 * 2.0 ** 23

SUB = 3
CHUNKS = 9
CHUNK = SUB * IMG
RING = 3
X_BLOCKS = 5

PIECES = [(128 * t, t, 128 * t, 128) for t in range(TILES)] + [
    (640, 0, 128, 384), (1024, 1, 256, 384), (1408, 0, 512, 128), (1536, 2, 384, 256), (1792, 3, 512, 128)]
TRI = 1920
HALVES = [(0, 1024), (1024, TRI)]
A_RING = 6
GROUP = 4

ERF_C = 3.224444918595032e-05
ERF_H1, ERF_K1 = -14.605611022253761, 152.92954269725462
ERF_H2, ERF_K2 = 8.168209826141505, 28.825868754761615


def chunk_block(c):
    return c // 2


class Walk:

    FILLS = dict(XT=1, ZT=1, QK=1, V=1, TPQ=1, TPK=1, YT=1, PT=1, PJ=1, Z2T=1, RT=1)

    def __init__(self, steps, base, batch):
        self.steps, self.base, self.batch = steps, base, batch

    def __iter__(self):
        n = 0
        for name, off, *args in self.steps:
            yield name, self.batch + off, self.base + n, args
            n += self.FILLS.get(name, 0)


def fills(steps):
    return sum(Walk.FILLS.get(s[0], 0) for s in steps)


def chunk_ahead(off, c, last):
    k = c + 2
    if k >= CHUNKS:
        if last:
            return []
        off, k = off + 1, k - CHUNKS
    out = [("XT", off, chunk_block(k))] if k % 2 == 0 else []
    return out + [("YN", off, k)]


def trig_ahead(off, c, last):
    k = c + 1
    if k >= CHUNKS:
        if last:
            return []
        off, k = off + 1, 0
    return [("TR", off, k)]


def first_steps():
    s = [("XT", 0, 0), ("YN", 0, 0), ("YN", 0, 1), ("TR", 0, 0)]
    for c in range(CHUNKS):
        s += chunk_ahead(0, c, False) + trig_ahead(0, c, False) + [("MM", 0, c, 0), ("MM", 0, c, 1)]
    return s + [("HEVAC", 0), ("LN1", 0)]


def head_steps(off, tokens, last):
    s = []
    for c in range(3, CHUNKS):
        h = 2 * (c - 3)
        s += [("S", off, h)]
        if tokens:
            s += chunk_ahead(off + 1, c, last)
        s += [("E", off, h)]
        if c - 2 < HEADS // 2:
            s += [("TPQ", off, c - 2), ("TPK", off, c - 2)]
        if tokens:
            s += [("MM", off + 1, c, 0)]
        s += [("S", off, h + 1)]
        if tokens:
            s += trig_ahead(off + 1, c, last)
        s += [("E", off, h + 1)]
        if c == 6:
            s += [("YT", off, 0, 0), ("YT", off, 0, 1)]
        if c == 8:
            s += [("YT", off, 1, 0), ("YT", off, 1, 1)]
        if tokens:
            s += [("MM", off + 1, c, 1)]
        if c == 5:
            s += [("AV", off, 0, 0), ("AV", off, 0, 1)]
        if c == 7:
            s += [("AV", off, 1, 0), ("AV", off, 1, 1)]
    s += [("ELAST", off)]
    if tokens:
        s += [("HEVAC", off + 1), ("LN1", off + 1)]
    return s + [("AV", off, 2, 0), ("AV", off, 2, 1)]


def turn_steps(post, prep, tokens):
    def if_post(*steps):
        return [(s[0], -1, *s[1:]) for s in steps] if post else []

    def if_prep(*steps):
        return [(s[0], 0, *s[1:]) for s in steps] if prep else []

    def mm(c, half):
        return [("MM", 1, c, half)] if tokens else []

    def ahead(c):
        return chunk_ahead(1, c, False) + trig_ahead(1, c, False) if tokens else []

    s = mm(0, 0) + if_post(("YT", 2, 0), ("YT", 2, 1)) + ahead(0) + if_post(("PT", 0), ("PT", 1), ("PT", 2)) + mm(0, 1)
    s += if_post(("PJ", 0), ("PJ", 1), ("PJ", 2)) + if_prep(("ZT", 0), ("ZT", 1), ("ZT", 2)) + if_post(("LN2",))
    s += if_prep(("QK", 0), ("QK", 1)) + mm(1, 0) + if_prep(("QK", 2), ("QK", 3), ("QK", 4)) + ahead(1)
    s += if_prep(("ROPE",), ("V", 0), ("V", 1), ("V", 2)) + mm(1, 1) + if_prep(("V", 3), ("V", 4))
    s += if_post(("Z2T", 0), ("Z2T", 1), ("Z2T", 2)) + if_prep(("SPLIT",)) + mm(2, 0)
    s += if_post(("RT",)) + if_prep(("COPYH",)) + ahead(2) + if_prep(("TPQ", 0), ("TPK", 0)) + mm(2, 1)
    return s


def transformer_block(nc, ctx, io, keep):
    def sb(name, shape, dt=F32):
        return ctx.enter_context(nc.sbuf_tensor(name, shape, dt))

    def sem(name):
        return ctx.enter_context(nc.semaphore(name))

    ident, logits = keep["ident"], keep["logits"]
    xraw = sb("xraw", [P, IMG_TILES, P])
    xT = sb("xT", [P, IMG])
    turns = [sb(f"turns{i}", [P, CHUNK]) for i in range(RING)]
    whole = [sb(f"whole{i}", [P, CHUNK]) for i in range(RING)]
    WT = sb("WT", [P, CHUNKS * SUB * 2, D])
    freq = sb("freq", [P, BANDS + SUB])
    hacc = sb("hacc", [P, TILES, D])
    h = sb("h", [P, TILES, D])
    z = sb("z", [P, TILES, D])
    stats = sb("stats", [P, TILES, 6])
    moments = sb("moments", [P, TILES, 2])
    var_eps = sb("var_eps", [P, TILES])
    rstd = sb("rstd", [P, TILES])
    gate = sb("gate", [P, 1])
    minus_half = sb("minus_half", [P, TILES])
    zT = sb("zT", [HALF, 2, SEQ])
    qk = sb("qk", [P, TILES, 2 * D])
    v32 = sb("v32", [P, TILES, HEADS, 32])
    split = sb("split", [P, TILES, 2 * HEADS, 64], F16)
    qT = sb("qT", [P, 2, SEQ], F16)
    kT = sb("kT", [P, 2, SEQ], F16)
    work = sb("work", [P, max((A_RING + 1) * TRI, 2 * FEATURES)])
    yraw = sb("yraw", [P, SEQ])
    y_sb = qk[:, :, 0:D]
    den = sb("den", [P, TILES * GROUP])
    rden = sb("rden", [P, TILES * GROUP])
    ident16 = sb("ident16", [P, P], F16)
    causal = sb("causal", [P, P])
    rope_cos = sb("rope_cos", [P, TILES, HD])
    rope_sin = sb("rope_sin", [P, TILES, HD])
    wqkvT = sb("wqkvT", [HALF, 2, 3 * D])
    wpT = sb("wpT", [HALF, 2, D])
    switch_w = sb("switch_w", [HALF, 2, EXPERTS])
    switch_b = sb("switch_b", [P, EXPERTS])

    weight = [work[:, s * TRI:(s + 1) * TRI] for s in range(A_RING)]
    factor = work[:, A_RING * TRI:(A_RING + 1) * TRI]
    rope_a = factor.rearrange("p (t n) -> p t n", t=TILES)
    rope_b = weight[-1].rearrange("p (t n) -> p t n", t=TILES)
    w_raw = work[0:HALF, 0:2 * FEATURES].rearrange("p (o f) -> p o f", o=2)
    w_pairs = split[0:HALF].rearrange("p t h i -> p (t h i)").bitcast(F32)[:, 0:2 * 2 * SUB * P]\
        .rearrange("p (o s i n) -> p o s i n", o=2, s=2, i=SUB)
    attn_raw = [hacc[0:HALF, 0:2, :], hacc[0:HALF, 2:4, :], z[0:HALF, 0:2, :], z[0:HALF, 2:4, :]]

    acc = ctx.enter_context(nc.psum_tensor("acc", [P, 2, 512], F32))
    score = ctx.enter_context(nc.psum_tensor("score", [P, 4 * 512], F32))
    av = ctx.enter_context(nc.psum_tensor("av", [P, 512], F32))
    misc = ctx.enter_context(nc.psum_tensor("misc", [P, 512], F32))
    misc16 = misc[:].bitcast(F16)

    w_loaded, small_loaded, x_loaded, txt_loaded = sem("w_loaded"), sem("small_loaded"), sem("x_loaded"), sem("txt_loaded")
    h_stored, z2_stored = sem("h_stored"), sem("z2_stored")
    zero_ready, const_ready, pairs_ready, ones_ready = sem("zero_ready"), sem("const_ready"), sem("pairs_ready"), sem("ones_ready")
    wt_full, wt_act, wt_dve, at_full, at_free = sem("wt_full"), sem("wt_act"), sem("wt_dve"), sem("at_full"), sem("at_free")
    misc_full, misc_free = sem("misc_full"), sem("misc_free")
    turns_made, turns_ready, frac_ready, abs_ready, trig_ready, chunk_used = (
        sem("turns_made"), sem("turns_ready"), sem("frac_ready"), sem("abs_ready"), sem("trig_ready"), sem("chunk_used"))
    hacc_ready, h_copied = sem("hacc_ready"), sem("h_copied")
    ln_stats, ln_aggr, ln_var, ln_rstd = sem("ln_stats"), sem("ln_aggr"), sem("ln_var"), sem("ln_rstd")
    z_ready, z2_ready = sem("z_ready"), sem("z2_ready")
    rope_parts, rope_done, hi_ready, lo_ready = sem("rope_parts"), sem("rope_done"), sem("hi_ready"), sem("lo_ready")
    score_full, square_done, factor_ready, y_done, y2_done = (
        sem("score_full"), sem("square_done"), sem("factor_ready"), sem("y_done"), sem("y2_done"))
    tanh_done, weight_ready, av_full, av_free, den_step = (
        sem("tanh_done"), sem("weight_ready"), sem("av_full"), sem("av_free"), sem("den_step"))

    begin = first_steps() + turn_steps(False, True, True)
    looped = head_steps(-1, True, False) + turn_steps(True, True, True)
    ending = head_steps(-1, True, True) + turn_steps(True, True, False)
    final = head_steps(0, False, True) + [(s[0], 0, *s[2:]) for s in turn_steps(True, False, False)]
    LOOPS = BATCHES - 2
    f_begin, f_loop, f_end = fills(begin), fills(looped), fills(ending)

    def program(eng, emit):
        for name, n, f, args in Walk(begin, 0, 0):
            emit(name, n, f, args)
        for name, n, f, args in Walk(looped, f_begin, 1):
            emit(name, n, f, args)
        with eng.Fori(2, 1 + LOOPS) as b:
            for name, n, f, args in Walk(looped, (b - 1) * f_loop + f_begin, b):
                emit(name, n, f, args)
        for name, n, f, args in Walk(ending, f_begin + LOOPS * f_loop, BATCHES - 1):
            emit(name, n, f, args)
        for name, n, f, args in Walk(final, f_begin + LOOPS * f_loop + f_end, BATCHES - 1):
            emit(name, n, f, args)

    def wait(eng, s, value):
        if isinstance(value, int) and value <= 0:
            return
        eng.wait_ge(s, value)

    def norms_before(name, n):
        if name == "LN1":
            return 0 if isinstance(n, int) and n == 0 else n * 2 - 1
        return n * 2 + 1 if isinstance(n, int) and n == BATCHES - 1 else n * 2 + 2

    def group_of(head):
        return head // GROUP

    W_FILLS = CHUNKS * SUB
    block = ctx.enter_context(nc.Block())

    @block.sync
    def _(sp):
        sp.dma_start(w_raw, io["W"].rearrange("(o p) f -> p o f", p=HALF)).then_inc(w_loaded, 16)
        for raw, name in zip(attn_raw, ("Wq", "Wk", "Wv", "Wproj")):
            sp.dma_start(raw, io[name].rearrange("(o p) f -> p o f", p=HALF)).then_inc(small_loaded, 16)
        with nc.allow_non_contiguous_dma(reason="a few words of frequencies"):
            sp.dma_start(freq[:, 0:BANDS], io["freq"][None, :].to_broadcast([P, BANDS])).then_inc(small_loaded, 16)
            for side in range(2):
                sp.dma_start(freq[64 * side:64 * side + 64, BANDS:BANDS + SUB],
                             io["freq"].rearrange("(i s) -> s i", s=2)[side:side + 1, :].to_broadcast([64, SUB]))\
                    .then_inc(small_loaded, 16)
        sp.dma_start(rope_cos[:], io["cos"]).then_inc(small_loaded, 16)
        sp.dma_start(rope_sin[:], io["sin"]).then_inc(small_loaded, 16)
        sp.dma_start(switch_w[:], io["switch_w"].rearrange("(k p) e -> p k e", p=HALF)).then_inc(small_loaded, 16)
        sp.dma_start(switch_b[:], io["switch_b"][None, :].to_broadcast([P, EXPERTS])).then_inc(small_loaded, 16)

        def load_x(n, q):
            src = io["x"][bass.ds(n, 1)].rearrange("o (t p) c -> p (o t) c", p=P)
            if q < X_BLOCKS - 1:
                sp.dma_start(xraw[:], src[:, :, q * P:(q + 1) * P]).then_inc(x_loaded, 32)
            else:
                for side in range(2):
                    sp.dma_start(xraw[:, :, side * 64:(side + 1) * 64], src[:, :, CH - 64:CH]).then_inc(x_loaded, 16)

        load_x(0, 0)
        sp.wait_ge(at_free, 4)
        sp.dma_start(hacc[:, IMG_TILES, :], io["txt"][0]).then_inc(txt_loaded, 16)

        def emit(name, n, f, args):
            if name == "XT":
                q = (args[0] + 1) % X_BLOCKS
                if q == 0 and isinstance(n, int) and n == BATCHES - 1:
                    return
                sp.wait_ge(misc_full, f + 1)
                load_x(n + (q == 0), q)
            elif name == "COPYH":
                if isinstance(n, int) and n == BATCHES - 1:
                    return
                sp.wait_ge(h_copied, n + 1)
                sp.dma_start(hacc[:, IMG_TILES, :], io["txt"][bass.ds(n + 1, 1)].rearrange("o p d -> p (o d)"))\
                    .then_inc(txt_loaded, 16)
            elif name == "LN2":
                sp.wait_ge(misc_free, f)
                sp.dma_start(io["h_dram"][bass.ds(n, 1)].rearrange("o p t d -> p (o t) d"), h[:]).then_inc(h_stored, 16)
                sp.wait_ge(z2_ready, n + 1)
                sp.dma_start(io["z2_dram"][bass.ds(n, 1)].rearrange("o p t d -> p (o t) d"), z[:]).then_inc(z2_stored, 16)

        program(sp, emit)
        sp.wait_ge(h_stored, 16 * BATCHES)
        sp.wait_ge(z2_stored, 16 * BATCHES)

    @block.gpsimd
    def _(pool):
        pool.memset(ident[:], 0.0).then_inc(zero_ready, 1)
        pool.memset(ident16[:], 0.0).then_inc(zero_ready, 1)
        pool.memset(causal[:], 1.0).then_inc(zero_ready, 1)
        pool.memset(minus_half[:], -0.5).then_inc(const_ready, 1)
        pool.wait_ge(zero_ready, 3)
        for m in (ident, ident16):
            pool.affine_select(out=m[:], in_=m[:], compare_op=ALU.not_equal, fill=1.0, base=0,
                               pattern=[[-1, P]], channel_multiplier=1).then_inc(const_ready, 1)
        pool.affine_select(out=causal[:], in_=causal[:], compare_op=ALU.is_ge, fill=0.0, base=0,
                           pattern=[[1, P]], channel_multiplier=-1).then_inc(const_ready, 1)

        def emit(name, n, f, args):
            if name == "YN":
                c, = args
                pool.wait_ge(turns_ready, n * CHUNKS + c + 1)
                pool.tensor_tensor(turns[c % RING][:], turns[c % RING][:], whole[c % RING][:],
                                   ALU.subtract).then_inc(frac_ready, 1)
            elif name in ("LN1", "LN2"):
                m = norms_before(name, n)
                pool.wait_ge(ln_var, m + 1)
                pool.tensor_tensor(rstd[:], var_eps[:], minus_half[:], ALU.pow).then_inc(ln_rstd, 1)
            elif name == "ROPE":
                pool.wait_ge(misc_free, f)
                wait(pool, y2_done, n * HEADS)
                wait(pool, av_full, n * 2 * (HEADS // GROUP))
                shape = [P, TILES, 2 * HEADS, HD]
                q4 = qk[:].rearrange("p t (h i) -> p t h i", i=HD)
                b4 = rope_b.rearrange("p t (h i) -> p t h i", i=HD)
                a4 = rope_a.rearrange("p t (h i) -> p t h i", i=HD)
                pool.tensor_tensor(a4, q4, rope_cos[:, :, None, :].to_broadcast(shape), ALU.mult).then_inc(rope_parts, 1)
                half = [P, TILES, 2 * HEADS, HD // 2]
                for e in range(2):
                    pool.tensor_tensor(b4[:, :, :, e::2], q4[:, :, :, 1 - e::2],
                                       rope_sin[:, :, None, e::2].to_broadcast(half), ALU.mult).then_inc(rope_parts, 1)
                pool.wait_ge(rope_parts, 3 * n + 3)
                pool.tensor_tensor(rope_a, rope_a, rope_b, ALU.add).then_inc(rope_done, 1)
            elif name == "SPLIT":
                pool.wait_ge(hi_ready, 2 * n + 2)
                a4 = rope_a.rearrange("p t (h i) -> p (t h) i", i=HD).rearrange("p (t h) i -> p t h i", t=TILES)
                for w, at in ((0, 32), (1, 16)):
                    hs = slice(w * HEADS, (w + 1) * HEADS)
                    pool.tensor_tensor(split[:, :, hs, at:at + HD], a4[:, :, hs, :], split[:, :, hs, 0:HD],
                                       ALU.subtract).then_inc(lo_ready, 1)

        program(pool, emit)

    @block.scalar
    def _(act):
        act.wait_ge(const_ready, 1)
        act.activation(den[:, 0:1], minus_half[:, 0:1], ACT.Silu).then_inc(ones_ready, 1)
        for k in range(0, W_FILLS, 2):
            act.wait_ge(wt_full, k + 1)
            act.activation(WT[:, 2 * k:2 * k + 2, :], score[:, (k % 4) * 512:(k % 4) * 512 + 2 * D], ACT.Copy).then_inc(wt_act, 1)

        act.wait_ge(ones_ready, 7)

        def emit(name, n, f, args):
            def evac(out, in_):
                act.wait_ge(misc_full, f + 1)
                act.activation(out, in_, ACT.Copy).then_inc(misc_free, 1)

            if name == "XT":
                q, = args
                wait(act, turns_ready, n * CHUNKS + 2 * q)
                evac(xT[:], misc[:])
            elif name == "TR":
                c, = args
                act.wait_ge(abs_ready, n * CHUNKS + c + 1)
                act.activation(turns[c % RING][:], turns[c % RING][:], ACT.Sin, scale=TWO_PI).then_inc(trig_ready, 1)
                act.activation(whole[c % RING][:], whole[c % RING][:], ACT.Sin, scale=-TWO_PI,
                               bias=keep["half_pi"][:, 0:1]).then_inc(trig_ready, 1)
            elif name in ("ZT", "PT", "Z2T"):
                i, = args
                w = min(2, TILES - 2 * i)
                evac(zT[:, :, 2 * i * P:(2 * i + w) * P].rearrange("p k (t n) -> p t k n", n=P),
                     misc[0:HALF, 0:w * 2 * P].rearrange("p (t k n) -> p t k n", t=w, k=2))
            elif name == "QK":
                if args[0] == 0:
                    wait(act, rope_done, n)
                evac(qk[:, args[0], :], misc[:, 0:2 * D])
            elif name == "V":
                evac(v32[:, args[0], :, 0:HD], misc[:, 0:D].rearrange("p (h i) -> p h i", i=HD))
            elif name == "TPQ":
                evac(qT[:, args[0] % 2, :], misc16[:, 0:SEQ])
            elif name == "E":
                i, = args
                H = n * HEADS + i
                A, B = weight[i % A_RING], factor
                for j, (a, b) in enumerate(HALVES):
                    act.wait_ge(score_full, 2 * H + j + 1)
                    if j == 0:
                        wait(act, av_full, 2 * (n * (HEADS // GROUP) + group_of(i - A_RING) + 1))
                    act.activation(A[:, a:b], score[:, a:b], ACT.Square, scale=HD ** -0.5).then_inc(square_done, 1)
                if i:
                    tanh(n, i - 1)
                act.wait_ge(square_done, 2 * H + 2)
                wait(act, y2_done, H)
                if i == 0:
                    act.wait_ge(lo_ready, 2 * n + 2)
                act.activation(B, A, ACT.Square, bias=keep["erf_h1"][:, 0:1]).then_inc(factor_ready, 1)
                act.activation(A, A, ACT.Square, bias=keep["erf_h2"][:, 0:1]).then_inc(factor_ready, 1)
            elif name == "ELAST":
                tanh(n, HEADS - 1)
            elif name == "AV":
                g, part = args
                G = 2 * (n * (HEADS // GROUP) + g) + part
                act.wait_ge(av_full, G + 1)
                a, w = (0, 512) if part == 0 else (512, SEQ - 512)
                act.activation(yraw[:, a:a + w], av[:, 0:w], ACT.Copy).then_inc(av_free, 1)

        def tanh(n, i):
            act.wait_ge(y2_done, n * HEADS + i + 1)
            A = weight[i % A_RING]
            act.activation(A, A, ACT.Tanh, scale=ERF_C * HD ** -0.5).then_inc(tanh_done, 1)

        program(act, emit)

    @block.vector
    def _(dve):
        dve.memset(keep["half_pi"][:], HALF_PI).then_inc(ones_ready, 1)
        dve.memset(keep["erf_h1"][:], ERF_H1).then_inc(ones_ready, 1)
        dve.memset(keep["erf_h2"][:], ERF_H2).then_inc(ones_ready, 1)
        dve.memset(v32[:], 0.0).then_inc(ones_ready, 1)
        dve.wait_ge(ones_ready, 5)
        dve.memset(v32[:, :, :, HD:HD + 1], 1.0).then_inc(ones_ready, 1)
        dve.wait_ge(w_loaded, 16)
        for o in range(2):
            for s in range(2):
                for i in range(SUB):
                    src = w_raw[:, o, (CH - 64) * 12:].rearrange("p (j k) -> p k j", k=12)[:, s * BANDS + 2 * i:s * BANDS + 2 * i + 2, :]
                    last = dve.tensor_copy(w_pairs[:, o, s, i, :].rearrange("p (k j) -> p k j", k=2), src)
        last.then_inc(pairs_ready, 1)
        for k in range(1, W_FILLS, 2):
            dve.wait_ge(wt_full, k + 1)
            dve.tensor_copy(WT[:, 2 * k:2 * k + 2, :],
                            score[:, (k % 4) * 512:(k % 4) * 512 + 2 * D].rearrange("p (t n) -> p t n", t=2)).then_inc(wt_dve, 1)
        dve.wait_ge(wt_full, W_FILLS)
        dve.memset(split[:], 0.0).then_inc(ones_ready, 1)
        for m in range(4):
            dve.wait_ge(at_full, m + 1)
            src = misc[0:HALF, 0:2 * D].rearrange("p (k n) -> p k n", k=2)
            dst = wqkvT[:, :, m * D:(m + 1) * D] if m < 3 else wpT[:]
            dve.tensor_copy(dst, src).then_inc(at_free, 1)
        dve.wait_ge(small_loaded, 16 * 11)
        dve.wait_ge(const_ready, 4)

        def norm(n, m, src, dst, done):
            for t in range(TILES):
                dve.bn_stats(stats[:, t, :], src[:, t, :]).then_inc(ln_stats, 1)
            dve.wait_ge(ln_stats, TILES * m + TILES)
            dve.memset(gate[:], 0.0)
            for t in range(TILES):
                dve.bn_aggr(moments[:, t, :], stats[:, t, :]).then_inc(ln_aggr, 1)
            dve.wait_ge(ln_aggr, TILES * m + TILES)
            dve.tensor_scalar(var_eps[:], moments[:, :, 1], 1e-5, None, ALU.add).then_inc(ln_var, 1)
            dve.wait_ge(ln_rstd, m + 1)
            for t in range(TILES):
                last = dve.tensor_scalar(dst[:, t, :], src[:, t, :], moments[:, t, 0:1], rstd[:, t:t + 1],
                                         ALU.subtract, ALU.mult)
            last.then_inc(done, 1)

        def emit(name, n, f, args):
            if name == "YN":
                c, = args
                K = n * CHUNKS + c
                if c % 2 == 0:
                    dve.wait_ge(misc_free, f)
                wait(dve, chunk_used, K - RING + 1)
                for i in range(SUB):
                    col = freq[:, BANDS + i:BANDS + i + 1] if c == CHUNKS - 1 else freq[:, SUB * (c % 2) + i:SUB * (c % 2) + i + 1]
                    src = xT[:]
                    cols = slice(i * IMG, (i + 1) * IMG)
                    last = dve.tensor_scalar(turns[c % RING][:, cols], src, col, None, ALU.mult)
                last.then_inc(turns_made, 1)
                dve.wait_ge(turns_made, K + 1)
                dve.tensor_scalar(whole[c % RING][:], turns[c % RING][:], ROUND, ROUND, ALU.add, ALU.subtract).then_inc(turns_ready, 1)
            elif name == "TR":
                c, = args
                dve.wait_ge(frac_ready, n * CHUNKS + c + 1)
                dve.tensor_scalar(whole[c % RING][:].bitcast(I32), turns[c % RING][:].bitcast(I32), 0x7FFFFFFF, None,
                                  ALU.bitwise_and).then_inc(abs_ready, 1)
            elif name == "HEVAC":
                dve.wait_ge(chunk_used, (n + 1) * CHUNKS)
                for j in range(2):
                    last = dve.tensor_copy(hacc[:, 2 * j:2 * j + 2, :], acc[:, j, 0:2 * D].rearrange("p (t n) -> p t n", t=2))
                last.then_inc(hacc_ready, 1)
            elif name == "LN1":
                dve.wait_ge(txt_loaded, 16 * (n + 1))
                dve.wait_ge(hacc_ready, n + 1)
                if not (isinstance(n, int) and n <= 1):
                    dve.wait_ge(z2_stored, 16 * (n - 1))
                norm(n, norms_before(name, n), hacc, z, z_ready)
            elif name == "LN2":
                dve.wait_ge(misc_free, f)
                if isinstance(n, int) and n == BATCHES - 1:
                    dve.wait_ge(z2_stored, 16 * n)
                norm(n, norms_before(name, n), h, z, z2_ready)
            elif name == "SPLIT":
                dve.wait_ge(rope_done, n + 1)
                a4 = rope_a.rearrange("p t (h i) -> p t h i", i=HD)
                for w in range(2):
                    hs = slice(w * HEADS, (w + 1) * HEADS)
                    for e in range(2):
                        at = 16 * e if w == 0 else 32 * e
                        last = dve.tensor_copy(split[:, :, hs, at:at + HD], a4[:, :, hs, :])
                    last.then_inc(hi_ready, 1)
            elif name == "TPK":
                dve.wait_ge(misc_full, f + 1)
                dve.tensor_copy(kT[:, args[0] % 2, :], misc16[:, 0:SEQ]).then_inc(misc_free, 1)
            elif name == "E":
                i, = args
                H = n * HEADS + i
                A, B = weight[i % A_RING], factor
                dve.wait_ge(factor_ready, 2 * H + 1)
                for a, b in HALVES:
                    dve.scalar_tensor_tensor(B[:, a:b], B[:, a:b], ERF_K1, score[:, a:b], ALU.add, ALU.mult).then_inc(y_done, 1)
                if i:
                    weights(n, i - 1)
                dve.wait_ge(factor_ready, 2 * H + 2)
                dve.wait_ge(y_done, 2 * H + 2)
                dve.scalar_tensor_tensor(A, A, ERF_K2, B, ALU.add, ALU.mult).then_inc(y2_done, 1)
            elif name == "ELAST":
                weights(n, HEADS - 1)
            elif name == "YT":
                g, part = args
                w = 4 if part == 0 else 1
                k = 2 * (2 * (n * (HEADS // GROUP) + g) + part)
                src = misc[:, 0:w * P].rearrange("p (t h i) -> p t h i", t=w, i=32)
                dn = den[:, 0:w * GROUP].rearrange("p (t h) -> p t h", t=w)
                dve.wait_ge(misc_full, f + 1)
                dve.tensor_scalar(dn, src[:, :, :, HD], 1e-6, None, ALU.max).then_inc(den_step, 1)
                dve.wait_ge(den_step, k + 1)
                dve.reciprocal(rden[:, 0:w * GROUP], den[:, 0:w * GROUP]).then_inc(den_step, 1)
                dve.wait_ge(den_step, k + 2)
                rd = rden[:, 0:w * GROUP].rearrange("p (t h) -> p t h", t=w)
                out = y_sb[:, 4 * part:4 * part + w, g * GROUP * HD:(g + 1) * GROUP * HD].rearrange("p t (h i) -> p t h i", i=HD)
                dve.tensor_tensor(out, src[:, :, :, 0:HD], rd[:, :, :, None].to_broadcast([P, w, GROUP, HD]),
                                  ALU.mult).then_inc(misc_free, 1)
            elif name == "PJ":
                i, = args
                w = min(2, TILES - 2 * i)
                dve.wait_ge(misc_full, f + 1)
                if i == 0:
                    dve.wait_ge(h_copied, n + 1)
                ins = dve.tensor_tensor(h[:, 2 * i:2 * i + w, :], misc[:, 0:w * D].rearrange("p (t n) -> p t n", t=w),
                                        h[:, 2 * i:2 * i + w, :], ALU.add)
                ins.then_inc(misc_free, 1)
            elif name == "RT":
                dve.wait_ge(misc_full, f + 1)
                dve.tensor_tensor(logits[:, bass.ds(n * TILES, TILES), :], misc[:, 0:TILES * EXPERTS].rearrange("p (t e) -> p t e", t=TILES),
                                  switch_b[:, None, :].to_broadcast([P, TILES, EXPERTS]), ALU.add).then_inc(misc_free, 1)
            elif name == "COPYH":
                wait(dve, h_stored, 16 * n)
                dve.tensor_copy(h[:], hacc[:]).then_inc(h_copied, 1)

        def weights(n, i):
            A = weight[i % A_RING]
            dve.wait_ge(tanh_done, n * HEADS + i + 1)
            dg = A[:, 0:TILES * P].rearrange("p (t n) -> p t n", t=TILES)
            dve.scalar_tensor_tensor(dg, dg, 1.0, causal[:, None, :].to_broadcast([P, TILES, P]), ALU.add, ALU.mult)
            dve.tensor_scalar(A[:, TILES * P:TRI], A[:, TILES * P:TRI], 1.0, None, ALU.add).then_inc(weight_ready, 1)

        program(dve, emit)

    @block.tensor
    def _(pe):
        pe.wait_ge(const_ready, 4)
        pe.wait_ge(w_loaded, 16)
        for k in range(W_FILLS):
            if k >= 4:
                pe.wait_ge(wt_dve if k % 2 else wt_act, (k - 4) // 2 + 1)
            if k == 0:
                pe.wait_ge(pairs_ready, 1)
            c, i = divmod(k, SUB)
            for s in range(2):
                for o in range(2):
                    if c < CHUNKS - 1:
                        band = SUB * (c % 2) + i
                        at = chunk_block(c) * P * 12 + s * BANDS + band
                        src = w_raw[:, o, at:at + 127 * 12 + 1:12]
                    else:
                        src = w_pairs[:, o, s, i, :]
                    at = (k % 4) * 512 + s * D + o * HALF
                    last = pe.transpose(score[:, at:at + HALF], src, ident[0:HALF, 0:HALF])
            last.then_inc(wt_full, 1)
        pe.wait_ge(small_loaded, 16 * 11)
        for m, raw in enumerate(attn_raw):
            if m:
                pe.wait_ge(at_free, m)
            for k in range(2):
                for o in range(2):
                    last = pe.transpose(misc[0:HALF, k * D + o * HALF:k * D + (o + 1) * HALF],
                                        raw[:, o, k * HALF:(k + 1) * HALF], ident[0:HALF, 0:HALF])
            last.then_inc(at_full, 1)
        pe.wait_ge(at_free, 4)
        pe.wait_ge(wt_act, (W_FILLS + 1) // 2)
        pe.wait_ge(wt_dve, W_FILLS // 2)
        pe.wait_ge(ones_ready, 7)

        def emit(name, n, f, args):
            if name in Walk.FILLS:
                wait(pe, misc_free, f)
            if name == "XT":
                q, = args
                pe.wait_ge(x_loaded, 32 * (n * X_BLOCKS + q + 1))
                for t in range(IMG_TILES):
                    last = pe.transpose(misc[:, t * P:(t + 1) * P], xraw[:, t, :], ident[:])
                last.then_inc(misc_full, 1)
            elif name == "MM":
                c, s = args
                K = n * CHUNKS + c
                if c == 0 and s == 0:
                    wait(pe, hacc_ready, n)
                pe.wait_ge(trig_ready, 2 * K + s + 1)
                feat = (turns, whole)[s][c % RING]
                for i in range(SUB):
                    for t in range(IMG_TILES):
                        first = c == 0 and s == 0 and i == 0 and t % 2 == 0
                        end = c == CHUNKS - 1 and s == 1 and i == SUB - 1 and t % 2 == 1
                        last = pe.matmul(acc[:, t // 2, (t % 2) * D:(t % 2 + 1) * D],
                                         feat[:, i * IMG + t * P:i * IMG + (t + 1) * P],
                                         WT[:, 2 * (c * SUB + i) + s, :], start=first, stop=end)
                if s == 1:
                    last.then_inc(chunk_used, 1)
            elif name in ("ZT", "PT", "Z2T"):
                i, = args
                if name == "ZT" and i == 0:
                    pe.wait_ge(z_ready, n + 1)
                if name == "Z2T" and i == 0:
                    pe.wait_ge(z2_ready, n + 1)
                src = y_sb if name == "PT" else z
                for t in range(min(2, TILES - 2 * i)):
                    for k in range(2):
                        last = pe.transpose(misc[0:HALF, (2 * t + k) * P:(2 * t + k + 1) * P],
                                            src[:, 2 * i + t, k * HALF:(k + 1) * HALF], ident[:])
                last.then_inc(misc_full, 1)
            elif name in ("QK", "V"):
                t, = args
                cols = slice(0, 2 * D) if name == "QK" else slice(2 * D, 3 * D)
                w = cols.stop - cols.start
                for k in range(2):
                    last = pe.matmul(misc[:, 0:w], zT[:, k, t * P:(t + 1) * P], wqkvT[:, k, cols], start=k == 0, stop=k == 1)
                last.then_inc(misc_full, 1)
            elif name in ("TPQ", "TPK"):
                hp, = args
                pe.wait_ge(lo_ready, 2 * n + 2)
                at = 2 * hp + (HEADS if name == "TPK" else 0)
                for t in range(TILES):
                    last = pe.transpose(misc16[:, t * P:(t + 1) * P],
                                        split[:, t, at:at + 2, :].rearrange("p h i -> p (h i)"), ident16[:])
                last.then_inc(misc_full, 1)
            elif name == "S":
                i, = args
                H = n * HEADS + i
                pe.wait_ge(misc_free, f)
                rows = slice(64 * (i % 2), 64 * (i % 2) + 64)
                for j, (a, b) in enumerate(HALVES):
                    wait(pe, y_done, 2 * (H - 1) + j + 1)
                    for at, t, q0, w in PIECES:
                        if not a <= at < b:
                            continue
                        last = pe.matmul(score[:, at:at + w], kT[rows, i // 2 % 2, t * P:(t + 1) * P],
                                         qT[rows, i // 2 % 2, q0:q0 + w], start=True, stop=True)
                    last.then_inc(score_full, 1)
            elif name == "AV":
                g, part = args
                G = 2 * (n * (HEADS // GROUP) + g) + part
                pe.wait_ge(weight_ready, n * HEADS + GROUP * (g + 1))
                wait(pe, av_free, G)
                lo, hi = (0, 512) if part == 0 else (512, SEQ)
                todo = []
                for at, t, q0, w in sorted(PIECES, key=lambda p: (p[1], p[2])):
                    a, b = max(lo, q0), min(hi, q0 + w)
                    if a < b:
                        todo.append((at + a - q0, t, a, b - a))
                for m, (at, t, q0, w) in enumerate(todo):
                    for r in range(GROUP):
                        head = GROUP * g + r
                        last = pe.matmul(av[32 * r:32 * r + 32, q0 - lo:q0 - lo + w], v32[:, t, head, :],
                                         weight[head % A_RING][:, at:at + w], start=m == 0, stop=m == len(todo) - 1)
                last.then_inc(av_full, 1)
            elif name == "YT":
                g, part = args
                pe.wait_ge(av_free, 2 * (n * (HEADS // GROUP) + g) + 2)
                for t in range(4 if part == 0 else 1):
                    last = pe.transpose(misc[:, t * P:(t + 1) * P], yraw[:, (4 * part + t) * P:(4 * part + t + 1) * P], ident[:])
                last.then_inc(misc_full, 1)
            elif name == "PJ":
                i, = args
                for t in range(min(2, TILES - 2 * i)):
                    for k in range(2):
                        last = pe.matmul(misc[:, t * D:(t + 1) * D], zT[:, k, (2 * i + t) * P:(2 * i + t + 1) * P],
                                         wpT[:, k, :], start=k == 0, stop=k == 1)
                last.then_inc(misc_full, 1)
            elif name == "RT":
                for t in range(TILES):
                    for k in range(2):
                        last = pe.matmul(misc[:, t * EXPERTS:(t + 1) * EXPERTS], zT[:, k, t * P:(t + 1) * P],
                                         switch_w[:, k, :], start=k == 0, stop=k == 1)
                last.then_inc(misc_full, 1)

        program(pe, emit)


def experts(nc, ctx, io, keep):
    def sb(name, shape, dt=F32):
        return ctx.enter_context(nc.sbuf_tensor(name, shape, dt))

    def sem(name):
        return ctx.enter_context(nc.semaphore(name))

    ident, logits = keep["ident"], keep["logits"]
    h_all = sb("h_all", [P, ALL_TILES, D])
    z_all = sb("z_all", [P, ALL_TILES, D])
    zeros = sb("zeros", [P, 5 * D])
    zero16 = sb("zero16", [P, 512], F16)
    top = sb("top", [P, ALL_TILES])
    below = sb("below", [P, ALL_TILES, EXPERTS])
    expo = sb("expo", [P, ALL_TILES, EXPERTS])
    number = sb("number", [P, EXPERTS])
    is_top = sb("is_top", [P, ALL_TILES, EXPERTS])
    route = sb("route", [P, ALL_TILES])
    onehot = sb("onehot", [P, ALL_TILES, EXPERTS])
    onehot16 = sb("onehot16", [P, ALL_TILES, EXPERTS], F16)
    total = sb("total", [P, ALL_TILES])
    prob = sb("prob", [P, ALL_TILES])
    spread = sb("spread", [P, ALL_TILES, P])
    bars = sb("bars", [P, 2 * TOKENS])
    ahead = [sb(f"ahead{i}", [P, TOKENS], F16) for i in range(2)]
    earlier = sb("earlier", [P, P])
    tie = [sb(f"tie{i}", [P, P]) for i in range(2)]
    rank_e = sb("rank_e", [P, ALL_TILES, EXPERTS])
    rank = sb("rank", [P, ALL_TILES])
    place = sb("place", [P, ALL_TILES])
    slots = sb("slots", [P, ALL_TILES], U32)
    b1_raw = sb("b1_raw", [EXPERTS * F_TILES, P])
    b1 = sb("b1", [P, EXPERTS * F_TILES])
    b2 = sb("b2", [BLOCK_P, EXPERTS, D])
    bias = [sb(f"bias{i}", [P, F_TILES]) for i in range(2)]
    w1 = [sb(f"w1_{i}", [HALF, 2, HIDDEN]) for i in range(2)]
    w2 = [sb(f"w2_{i}", [P, F_TILES, D]) for i in range(2)]
    rows = [sb(f"rows{i}", [BLOCK_P, ROWS, D]) for i in range(2)]
    rowsT = sb("rowsT", [HALF, 2, BLOCK])
    hid = sb("hid", [P, F_TILES, BLOCK])
    made = [ahead[i][0:BLOCK_P, 0:2 * ROWS * D].bitcast(F32).rearrange("p (r d) -> p r d", r=ROWS) for i in range(2)]

    HB = 4
    hid_ps = ctx.enter_context(nc.psum_tensor("hid_ps", [P, HB, 512], F32))
    rowsT_ps = ctx.enter_context(nc.psum_tensor("rowsT_ps", [P, 2, 512], F32))
    pair = ctx.enter_context(nc.psum_tensor("pair", [P, 2 * 512], F32))
    rank_ps = pair[:, 0:2 * ALL_TILES * EXPERTS]
    made_ps = pair[:].rearrange("p (j n) -> p j n", j=2)

    z_loaded, h_loaded, b1_loaded, b2_loaded = sem("z_loaded"), sem("h_loaded"), sem("b1_loaded"), sem("b2_loaded")
    zeros_ready, buffer_zeroed, sent, fetched, out_stored = (
        sem("zeros_ready"), sem("buffer_zeroed"), sem("sent"), sem("fetched"), sem("out_stored"))
    masks_ready, route_step, expo_ready, spread_ready, bars_full, bars_copied, bars_ready = (
        sem("masks_ready"), sem("route_step"), sem("expo_ready"), sem("spread_ready"), sem("bars_full"), sem("bars_copied"), sem("bars_ready"))
    tie_ready, ahead_ready, ahead_used, slots_ready, b1_full, b1_ready = (
        sem("tie_ready"), sem("ahead_ready"), sem("ahead_used"), sem("slots_ready"), sem("b1_full"), sem("b1_ready"))
    weights_loaded = [sem("weights_loaded0"), sem("weights_loaded1")]
    rows_loaded = [sem("rows_loaded0"), sem("rows_loaded1")]
    made_stored = [sem("made_stored0"), sem("made_stored1")]
    rows_full, rows_half0, rows_half1 = sem("rows_full"), sem("rows_half0"), sem("rows_half1")
    hid_full, gelu_done, made_full, made_ready = sem("hid_full"), sem("gelu_done"), sem("made_full"), sem("made_ready")
    out_ready = sem("out_ready")

    block = ctx.enter_context(nc.Block())
    xs_blocks = io["xs_dram"].rearrange("(b p r) d -> b p r d", p=BLOCK_P, r=ROWS)
    ys_blocks = io["ys_dram"].rearrange("(b p r) d -> b p r d", p=BLOCK_P, r=ROWS)
    STEP = 2 * PER_EXPERT
    TURNS = BLOCKS // STEP

    def wait(eng, s, value):
        if isinstance(value, int) and value <= 0:
            return
        eng.wait_ge(s, value)

    def program(eng, emit):
        for u in range(STEP):
            emit(0, u, False)
        with eng.Fori(1, TURNS - 1) as i:
            for u in range(STEP):
                emit(i, u, False)
        for u in range(STEP):
            emit(TURNS - 1, u, u == STEP - 1)

    @block.sync
    def _(sp):
        sp.dma_start(b1_raw[:], io["b1"].rearrange("e (f p) -> (e f) p", p=P)).then_inc(b1_loaded, 16)
        sp.dma_start(z_all[:].rearrange("p (b t) d -> p b t d", b=BATCHES), io["z2_dram"].rearrange("b p t d -> p b t d"))\
            .then_inc(z_loaded, 16)
        sp.wait_ge(zeros_ready, 1)
        sp.dma_start(io["xs_dram"].rearrange("(p k n) d -> p k (n d)", p=P, n=5),
                     zeros[:, None, :].to_broadcast([P, SLOTS // P // 5, 5 * D])).then_inc(buffer_zeroed, 16)
        sp.dma_start(b2[:], io["b2"].rearrange("(o e) d -> o e d", o=1).to_broadcast([BLOCK_P, EXPERTS, D])).then_inc(b2_loaded, 16)

        def load_weights(e, side):
            sp.dma_start(w1[side][:], io["w1"][bass.ds(e, 1)].rearrange("o (k p) f -> p (o k) f", p=HALF)).then_inc(weights_loaded[side], 16)
            sp.dma_start(bias[side][:], b1[:, bass.ds(e * F_TILES, F_TILES)]).then_inc(weights_loaded[side], 16)
            sp.dma_start(w2[side][:], io["w2"][bass.ds(e, 1)].rearrange("o (f p) d -> p (o f) d", p=P)).then_inc(weights_loaded[side], 16)

        def load_rows(b, side):
            sp.dma_start(rows[side][:], xs_blocks[bass.ds(b, 1)].rearrange("o p r d -> p (o r) d")).then_inc(rows_loaded[side], 16)

        sp.wait_ge(b1_ready, 1)
        for e in range(2):
            load_weights(e, e)
        sp.dma_start(h_all[:].rearrange("p (b t) d -> p b t d", b=BATCHES), io["h_dram"].rearrange("b p t d -> p b t d"))\
            .then_inc(h_loaded, 16)
        sp.wait_ge(sent, 16 * ALL_TILES)
        for b in range(2):
            load_rows(b, b)

        def emit(i, u, last):
            b = i * STEP + u
            ends = isinstance(i, int) and i == TURNS - 1
            if not (ends and u >= STEP - 2):
                sp.wait_ge(rows_full, b + 1)
                load_rows(b + 2, u % 2)
            sp.wait_ge(made_ready, 2 * b + 2)
            sp.dma_start(ys_blocks[bass.ds(b, 1)].rearrange("o p r d -> p (o r) d"), made[u % 2]).then_inc(made_stored[u % 2], 16)
            if u % PER_EXPERT == PER_EXPERT - 1 and not ends:
                load_weights(i * 2 + u // PER_EXPERT + 2, u // PER_EXPERT)

        program(sp, emit)
        for b in range(BATCHES):
            sp.wait_ge(out_ready, b + 1)
            sp.dma_start(io["out"][b].rearrange("(t p) d -> p t d", p=P), h_all[:, b * TILES:(b + 1) * TILES, :]).then_inc(out_stored, 16)
        sp.wait_ge(out_stored, 16 * BATCHES)

    @block.gpsimd
    def _(pool):
        pool.memset(zeros[:], 0.0).then_inc(zeros_ready, 1)
        pool.memset(zero16[:], 0.0).then_inc(masks_ready, 1)
        for e in range(EXPERTS):
            pool.memset(number[:, e:e + 1], float(e - EXPERTS)).then_inc(masks_ready, 1)
        pool.memset(earlier[:], 1.0).then_inc(masks_ready, 1)
        pool.wait_ge(masks_ready, EXPERTS + 2)
        pool.affine_select(out=earlier[:], in_=earlier[:], compare_op=ALU.is_ge, fill=0.0, base=-1,
                           pattern=[[1, P]], channel_multiplier=-1).then_inc(masks_ready, 1)
        pool.wait_ge(slots_ready, 1)
        pool.wait_ge(buffer_zeroed, 16)
        pool.wait_ge(z_loaded, 16)
        for t in range(ALL_TILES):
            pool.indirect_dma_start(out=io["xs_dram"], out_offset=bass.IndirectOffsetOnAxis(ap=slots[:, t:t + 1], axis=0),
                                    in_=z_all[:, t, :], in_offset=None, bounds_check=SLOTS - 1, oob_is_err=False).then_inc(sent, 16)
        pool.wait_ge(sent, 16 * ALL_TILES)
        for side in range(2):
            pool.wait_ge(made_stored[side], 16 * BLOCKS // 2)
        for t in range(ALL_TILES):
            pool.indirect_dma_start(out=z_all[:, t, :], out_offset=None, in_=io["ys_dram"],
                                    in_offset=bass.IndirectOffsetOnAxis(ap=slots[:, t:t + 1], axis=0),
                                    bounds_check=SLOTS - 1, oob_is_err=False).then_inc(fetched, 16)
        pool.wait_ge(fetched, 16 * ALL_TILES)

    @block.scalar
    def _(act):
        act.wait_ge(route_step, 2)
        act.activation(expo[:], below[:], ACT.Exp).then_inc(expo_ready, 1)
        for k in range(ALL_TILES // 4):
            act.wait_ge(bars_full, k + 1)
            act.activation(bars[:, 512 * k:512 * (k + 1)], hid_ps[:, k % HB, :], ACT.Copy).then_inc(bars_copied, 1)
        act.wait_ge(b1_full, 1)
        act.activation(b1[:], rowsT_ps[:, 0, 0:EXPERTS * F_TILES], ACT.Copy).then_inc(b1_ready, 1)

        def emit(i, u, last):
            b = i * STEP + u
            if isinstance(i, int) and b == 0:
                first_rows()
            for f in range(F_TILES):
                G = b * F_TILES + f
                act.wait_ge(hid_full, G + 1)
                if f == 0:
                    wait(act, made_full, 2 * b)
                act.activation(hid[:, f, :], hid_ps[:, (u * F_TILES + f) % HB, 0:BLOCK], ACT.Gelu,
                               bias=bias[u // PER_EXPERT][:, f:f + 1]).then_inc(gelu_done, 1)
            if not last:
                act.wait_ge(rows_full, b + 2)
                act.activation(rowsT[:, 0, :], rowsT_ps[0:HALF, 0, 0:BLOCK], ACT.Copy).then_inc(rows_half0, 1)

        def first_rows():
            act.wait_ge(rows_full, 1)
            act.activation(rowsT[:, 0, :], rowsT_ps[0:HALF, 0, 0:BLOCK], ACT.Copy).then_inc(rows_half0, 1)

        program(act, emit)

    @block.vector
    def _(dve):
        each = [P, ALL_TILES, EXPERTS]
        n = 0

        def step(ins):
            nonlocal n
            ins.then_inc(route_step, 1)
            n += 1
            dve.wait_ge(route_step, n)

        dve.wait_ge(masks_ready, EXPERTS + 3)
        step(dve.tensor_reduce(top[:], logits[:], AX_X, ALU.max))
        step(dve.tensor_tensor(below[:], logits[:], top[:, :, None].to_broadcast(each), ALU.subtract))
        step(dve.scalar_tensor_tensor(is_top[:], below[:], 0.0, number[:, None, :].to_broadcast(each), ALU.is_ge, ALU.mult))
        step(dve.tensor_reduce(route[:], is_top[:], AX_X, ALU.min))
        step(dve.tensor_tensor(onehot[:], number[:, None, :].to_broadcast(each), route[:, :, None].to_broadcast(each), ALU.is_equal))
        step(dve.tensor_copy(onehot16[:], onehot[:]))
        dve.wait_ge(expo_ready, 1)
        step(dve.tensor_reduce(total[:], expo[:], AX_X, ALU.add))
        step(dve.reciprocal(prob[:], total[:]))
        dve.tensor_copy(spread[:], prob[:, :, None].to_broadcast([P, ALL_TILES, P])).then_inc(spread_ready, 1)
        dve.wait_ge(bars_copied, ALL_TILES // 4)
        dve.scalar_tensor_tensor(bars[:, TOKENS:2 * TOKENS], bars[:, 0:TOKENS], 0.75 * 2.0 ** -23, bars[:, 0:TOKENS],
                                 ALU.mult, ALU.add).then_inc(bars_ready, 1)
        dve.wait_ge(bars_ready, 1)

        def compare(i, u):
            j = 2 * i + u
            pj = prob[:, bass.ds(j, 1)]
            own = bars[:, bass.ds(j * P, P)]
            wait(dve, ahead_used, 2 * i + u - 1)
            dve.tensor_scalar(ahead[u][:, P:TOKENS], bars[:, bass.ds((j + 1) * P, TOKENS - P)], pj, None, ALU.is_le)
            dve.scalar_tensor_tensor(tie[u][:], own, pj, earlier[:], ALU.is_equal, ALU.mult).then_inc(tie_ready, 1)
            dve.wait_ge(tie_ready, 2 * i + u + 1)
            dve.scalar_tensor_tensor(ahead[u][:, 0:P], own, pj, tie[u][:], ALU.is_lt, ALU.add).then_inc(ahead_ready, 1)

        for u in range(2):
            compare(0, u)
        with dve.Fori(1, ALL_TILES // 2) as i:
            for u in range(2):
                compare(i, u)

        dve.wait_ge(ahead_used, ALL_TILES + 1)
        step(dve.tensor_copy(rank_e[:], rank_ps[:, 0:ALL_TILES * EXPERTS].rearrange("p (t e) -> p t e", e=EXPERTS)))
        step(dve.tensor_tensor(rank_e[:], rank_e[:], rank_ps[:, ALL_TILES * EXPERTS:].rearrange("p (t e) -> p t e", e=EXPERTS), ALU.add))
        step(dve.tensor_tensor(rank_e[:], rank_e[:], onehot[:], ALU.mult))
        step(dve.tensor_reduce(rank[:], rank_e[:], AX_X, ALU.add))
        step(dve.tensor_scalar(place[:], rank[:], float(CAPACITY), float(4 * SLOTS), ALU.is_ge, ALU.mult))
        step(dve.tensor_tensor(place[:], place[:], rank[:], ALU.add))
        step(dve.tensor_scalar(route[:], route[:], float(EXPERTS), float(CAPACITY), ALU.add, ALU.mult))
        dve.tensor_tensor(slots[:], place[:], route[:], ALU.add).then_inc(slots_ready, 1)
        dve.wait_ge(b2_loaded, 16)

        def second_half(b):
            dve.wait_ge(rows_full, b + 1)
            dve.tensor_copy(rowsT[:, 1, :], rowsT_ps[0:HALF, 1, 0:BLOCK]).then_inc(rows_half1, 1)

        def emit(i, u, last):
            b = i * STEP + u
            if isinstance(i, int) and b == 0:
                second_half(0)
            if not last:
                second_half(b + 1)
            for j in range(2):
                dve.wait_ge(made_full, 2 * b + j + 1)
                if j == 0:
                    wait(dve, made_stored[u % 2], (i * 2 + u // 2) * 16)
                dve.tensor_tensor(made[u % 2][:, 2 * j:2 * j + 2, :],
                                  made_ps[0:BLOCK_P, j, 0:2 * D].rearrange("p (r d) -> p r d", r=2),
                                  b2[:, bass.ds(i * 2 + u // PER_EXPERT, 1), :].to_broadcast([BLOCK_P, 2, D]), ALU.add)\
                    .then_inc(made_ready, 1)

        program(dve, emit)
        dve.wait_ge(h_loaded, 16)
        for t in range(ALL_TILES):
            dve.wait_ge(fetched, 16 * ALL_TILES) if t == 0 else None
            ins = dve.scalar_tensor_tensor(h_all[:, t, :], z_all[:, t, :], prob[:, t:t + 1], h_all[:, t, :], ALU.mult, ALU.add)
            if t % TILES == TILES - 1:
                ins.then_inc(out_ready, 1)

    @block.tensor
    def _(pe):
        pe.wait_ge(b1_loaded, 16)
        pe.transpose(rowsT_ps[:, 0, 0:EXPERTS * F_TILES], b1_raw[:], ident[0:EXPERTS * F_TILES, 0:EXPERTS * F_TILES]).then_inc(b1_full, 1)
        pe.wait_ge(spread_ready, 1)
        for k in range(ALL_TILES // 4):
            if k >= HB:
                pe.wait_ge(bars_copied, k - HB + 1)
            for t in range(4):
                last = pe.transpose(hid_ps[:, k % HB, t * P:(t + 1) * P], spread[:, 4 * k + t, :], ident[:])
            last.then_inc(bars_full, 1)
        pe.wait_ge(masks_ready, EXPERTS + 3)
        for j in range(2):
            pe.matmul(pair[:, j * 512:(j + 1) * 512], zero16[:, 0:P], zero16[:], start=True, stop=False)

        def count(i, u):
            j = 2 * i + u
            pe.wait_ge(ahead_ready, 2 * i + u + 1)
            for k in range(ALL_TILES):
                last = pe.matmul(pair[:, bass.ds((j + k) * EXPERTS, EXPERTS)], ahead[u][:, k * P:(k + 1) * P],
                                 onehot16[:, bass.ds(j, 1), :].rearrange("p o e -> p (o e)"), start=False, stop=False)
            last.then_inc(ahead_used, 1)

        with pe.Fori(0, ALL_TILES // 2) as i:
            for u in range(2):
                count(i, u)
        for j in range(2):
            last = pe.matmul(pair[:, j * 512:(j + 1) * 512], zero16[:, 0:P], zero16[:], start=False, stop=True)
        last.then_inc(ahead_used, 1)
        pe.wait_ge(slots_ready, 1)

        def transpose_rows(b, side, round_, first):
            pe.wait_ge(rows_loaded[side], 16 * round_)
            if first:
                pe.wait_ge(b1_ready, 1)
            for r in range(ROWS):
                for k in range(2):
                    last = pe.transpose(rowsT_ps[0:HALF, k, r * BLOCK_P:(r + 1) * BLOCK_P],
                                        rows[side][:, r, k * HALF:(k + 1) * HALF], ident[0:BLOCK_P, 0:BLOCK_P])
            last.then_inc(rows_full, 1)

        def emit(i, u, last):
            b = i * STEP + u
            side = u // PER_EXPERT
            if isinstance(i, int) and b == 0:
                transpose_rows(0, 0, 1, True)
            pe.wait_ge(rows_half0, b + 1)
            pe.wait_ge(rows_half1, b + 1)
            if u % PER_EXPERT == 0:
                pe.wait_ge(weights_loaded[side], 48 * (i + 1))
            for f in range(F_TILES):
                G = b * F_TILES + f
                wait(pe, gelu_done, G - HB + 1)
                for k in range(2):
                    ins = pe.matmul(hid_ps[:, (u * F_TILES + f) % HB, 0:BLOCK], w1[side][:, k, f * P:(f + 1) * P],
                                    rowsT[:, k, :], start=k == 0, stop=k == 1)
                ins.then_inc(hid_full, 1)
            if not last:
                transpose_rows(b + 1, (u + 1) % 2, i * 2 + (u + 1) // 2 + 1, False)
            wait(pe, made_ready, 2 * b)
            pe.wait_ge(gelu_done, (b + 1) * F_TILES)
            for r in range(ROWS):
                for f in range(F_TILES):
                    ins = pe.matmul(made_ps[0:BLOCK_P, r // 2, (r % 2) * D:(r % 2 + 1) * D],
                                    hid[:, f, r * BLOCK_P:(r + 1) * BLOCK_P], w2[side][:, f, :],
                                    start=r % 2 == 0 and f == 0, stop=r % 2 == 1 and f == F_TILES - 1)
                if r % 2 == 1:
                    ins.then_inc(made_full, 1)

        program(pe, emit)


def early_fusion_block(nc, x, txt, freq, W, Wq, Wk, Wv, Wproj, switch_w, switch_b, w1, b1, w2, b2, cos, sin, out):
    io = dict(x=x, txt=txt, freq=freq, W=W, Wq=Wq, Wk=Wk, Wv=Wv, Wproj=Wproj, switch_w=switch_w, switch_b=switch_b,
              w1=w1, b1=b1, w2=w2, b2=b2, cos=cos, sin=sin, out=out)
    io["h_dram"] = nc.dram_tensor("h_dram", [BATCHES, P, TILES, D], F32, kind="Internal").ap()
    io["z2_dram"] = nc.dram_tensor("z2_dram", [BATCHES, P, TILES, D], F32, kind="Internal").ap()
    io["xs_dram"] = nc.dram_tensor("xs_dram", [SLOTS, D], F32, kind="Internal").ap()
    io["ys_dram"] = nc.dram_tensor("ys_dram", [SLOTS, D], F32, kind="Internal").ap()
    with ExitStack() as outer:
        def sb(name, shape):
            return outer.enter_context(nc.sbuf_tensor(name, shape, F32))
        keep = dict(ident=sb("ident", [P, P]), logits=sb("logits", [P, ALL_TILES, EXPERTS]),
                    half_pi=sb("half_pi", [P, 1]), erf_h1=sb("erf_h1", [P, 1]), erf_h2=sb("erf_h2", [P, 1]))
        with ExitStack() as ctx:
            transformer_block(nc, ctx, io, keep)
        with ExitStack() as ctx:
            experts(nc, ctx, io, keep)


def kernel(x, txt, L0_tok_freq_bands, L0_tok_W, L0_attn_Wq, L0_attn_Wk, L0_attn_Wv, L0_attn_Wproj, L0_ffn_switch_w,
           L0_ffn_switch_b, L0_ffn_w1, L0_ffn_b1, L0_ffn_w2, L0_ffn_b2):
    import numpy as _np
    import concourse.bacc as _bacc
    from concourse import mybir as _mybir
    from concourse.bass_utils import run_bass_kernel_spmd as _run

    half = HD // 2
    rate = _np.float32(1.0) / _np.float32(10000.0) ** (_np.arange(half, dtype=_np.float32) / _np.float32(half))
    angle = _np.arange(SEQ, dtype=_np.float32)[:, None] * rate[None, :]
    c, s = _np.cos(angle), _np.sin(angle)

    def tiled(a):
        return a.reshape(TILES, P, HD).transpose(1, 0, 2)

    arrays = [("x", x.reshape(BATCHES, IMG, CH)), ("txt", txt), ("freq", L0_tok_freq_bands), ("W", L0_tok_W),
              ("Wq", L0_attn_Wq), ("Wk", L0_attn_Wk), ("Wv", L0_attn_Wv), ("Wproj", L0_attn_Wproj),
              ("switch_w", L0_ffn_switch_w), ("switch_b", L0_ffn_switch_b),
              ("w1", L0_ffn_w1), ("b1", L0_ffn_b1), ("w2", L0_ffn_w2), ("b2", L0_ffn_b2),
              ("cos", tiled(_np.repeat(c, 2, axis=1))), ("sin", tiled(_np.stack([-s, s], axis=-1)))]
    nc = _bacc.Bacc("TRN2", target_bir_lowering=False, num_devices=1)
    feed, args = {}, []
    for name, a in arrays:
        a = _np.ascontiguousarray(a)
        feed[f"in_{name}"] = a
        args.append(nc.dram_tensor(f"in_{name}", a.shape, _mybir.dt.from_np(a.dtype), kind="ExternalInput").ap())
    args.append(nc.dram_tensor("out_0", (BATCHES, SEQ, D), _mybir.dt.float32, kind="ExternalOutput").ap())
    early_fusion_block(nc, *args)
    r = _run(nc, [feed], core_ids=[0])
    return r.results[0]["out_0"]
```

```python
from contextlib import ExitStack

import concourse.bass as bass
from concourse import mybir

F32, F16, I32, U32 = mybir.dt.float32, mybir.dt.float16, mybir.dt.int32, mybir.dt.uint32
ALU = mybir.AluOpType
ACT = mybir.ActivationFunctionType
AX_X = mybir.AxisListType.X

P = 128
BATCHES, IMG, TXT, D = 8, 512, 128, 192
SEQ = IMG + TXT
TILES = SEQ // P
IMG_TILES = IMG // P
ALL_TILES = BATCHES * TILES
CH = 3 * D
BANDS = 6
FEATURES = CH * 2 * BANDS
HEADS, HD = 12, 16
HALF = D // 2
EXPERTS, HIDDEN = 8, 768
TOKENS = BATCHES * SEQ
CAPACITY = int(1.25 * TOKENS / EXPERTS)
SLOTS = EXPERTS * CAPACITY
ROWS = 4
BLOCK = 400
BLOCK_P = BLOCK // ROWS
PER_EXPERT = CAPACITY // BLOCK
BLOCKS = EXPERTS * PER_EXPERT
F_TILES = HIDDEN // P
AT_H, AT_PROB, AT_TOKEN, WIDE = D, 2 * D, 2 * D + 1, 2 * D + 2
ROWS_RING = 4
LEVELS = 3
ROUNDS = 14
TWO_PI = 6.283185307179586
HALF_PI = 1.5707963267948966
ROUND = 1.5 * 2.0 ** 23

SUB = 3
CHUNKS = 9
CHUNK = SUB * IMG
RING = 3
X_BLOCKS = 5

PIECES = [(128 * t, t, 128 * t, 128) for t in range(TILES)] + [
    (640, 0, 128, 384), (1024, 1, 256, 384), (1408, 0, 512, 128), (1536, 2, 384, 256), (1792, 3, 512, 128)]
TRI = 1920
HALVES = [(0, 1024), (1024, TRI)]
A_RING = 6
PAIR_RING = 3
GROUP = 4

ERF_C = 3.224444918595032e-05
ERF_H1, ERF_K1 = -14.605611022253761, 152.92954269725462
ERF_H2, ERF_K2 = 8.168209826141505, 28.825868754761615


def chunk_block(c):
    return c // 2


class Fills:

    def __init__(self, half, n):
        self.half, self.n = half, n
        self.bank = n % 2
        self.total = half * 2 + n

    def of(self, bank):
        return self.half + (self.n + 1 - bank) // 2


FILLS = dict(XT=1, ZT=1, QK=1, V=1, TPQ=1, TPK=1, YT=1, PT=1, PJ=1, Z2T=1, RT=1, AV=1)
PIECES_OF_CHUNK = 2 * SUB


def walk(steps, half, odd, batch):
    n = odd
    for name, off, *args in steps:
        yield name, batch + off, Fills(half, n), args
        n += FILLS.get(name, 0)


def fills(steps):
    return sum(FILLS.get(s[0], 0) for s in steps)


SPAN = 3 * HEADS
HEAD_AT = dict(E1=0, E2=1, S=-1.2, E3=2)
PAIR_AT = {0: -2, 1: 2, 2: 3.7, 3: 9, 4: 13, 5: 21}
SUM_AT = {0: (16, 17), 1: (28, 29), 2: (40.3, 40.79)}
TURN_AT = {0: (18.1, 21.5), 1: (32.1, 32.92), 2: (43, 44)}
TILE_AT = dict(ZT=(-14, -14, -13), QK=(-12, -12, -10.7, -10.3, -10), ROPE=(-11, -10.92, -10.15, -9.3,
               -9.21), V=(6, 6.7, 7.4, 8, 8.1), PT=(46, 47, 47), PJ=(48.7, 48.7, 49.7), Z2T=(53, 54.3, 54.4))
ONCE_AT = dict(LN1=-15.7, SPLIT=-7.5, COPYH=18, LN2=51, RT=56.3)
CHUNK_SPAN = SPAN / CHUNKS
CHUNK_AT = dict(XT=-10.1, YN=-8, AB=-6.9, TR=-2.2, MM=-0.7)
CHUNKS_BEFORE = CHUNKS + 4


def timetable():
    at = []

    def add(time, name, batch, *args):
        at.append((time, len(at), (name, batch, *args)))

    for k in range(BATCHES * CHUNKS):
        batch, c = divmod(k, CHUNKS)
        start = (k - CHUNKS_BEFORE) * CHUNK_SPAN
        if c % 2 == 0:
            add(start + CHUNK_AT["XT"], "XT", batch, c // 2)
        for name in ("YN", "AB", "TR"):
            add(start + CHUNK_AT[name], name, batch, c)
        for m in range(PIECES_OF_CHUNK):
            add(start + CHUNK_AT["MM"] + m * CHUNK_SPAN / PIECES_OF_CHUNK, "MM", batch, c, m)
        if c == CHUNKS - 1:
            add(start + CHUNK_AT["MM"] + (PIECES_OF_CHUNK - 1) * CHUNK_SPAN / PIECES_OF_CHUNK, "HEVAC", batch)
    for batch in range(BATCHES):
        start = batch * SPAN
        for h in range(HEADS):
            for name in ("E1", "E2", "S", "E3"):
                add(start + 3 * h + HEAD_AT[name], name, batch, h)
        for hp, time in PAIR_AT.items():
            add(start + time, "TPQ", batch, hp)
            add(start + time, "TPK", batch, hp)
        for name, table in (("AV", SUM_AT), ("YT", TURN_AT)):
            for g, times in table.items():
                for part, time in enumerate(times):
                    add(start + time, name, batch, g, part)
        for name, times in TILE_AT.items():
            for k, time in enumerate(times):
                add(start + time, name, batch, k)
        for name, time in ONCE_AT.items():
            add(start + time, name, batch)
    add(BATCHES * SPAN, "ELAST", BATCHES - 1)
    return sorted(at)


def steps_between(table, first, last, batch):
    return [(name, b - batch, *args) for time, _, (name, b, *args) in table if first <= time < last]


def transformer_block(nc, ctx, io, keep):
    def sb(name, shape, dt=F32):
        return ctx.enter_context(nc.sbuf_tensor(name, shape, dt))

    def sem(name):
        return ctx.enter_context(nc.semaphore(name))

    ident, logits = keep["ident"], keep["logits"]
    xraw = sb("xraw", [P, IMG_TILES, P])
    xT = sb("xT", [P, IMG])
    turns = [sb(f"turns{i}", [P, CHUNK]) for i in range(RING)]
    whole = [sb(f"whole{i}", [P, CHUNK]) for i in range(RING)]
    WT = sb("WT", [P, CHUNKS * SUB * 2, D])
    freq = sb("freq", [P, BANDS + SUB])
    hacc = sb("hacc", [P, TILES, D])
    h = sb("h", [P, TILES, D])
    z = sb("z", [P, TILES, D])
    stats = sb("stats", [P, TILES, 6])
    moments = sb("moments", [P, TILES, 2])
    var_eps = sb("var_eps", [P, TILES])
    rstd = sb("rstd", [P, TILES])
    gate = sb("gate", [P, 1])
    minus_half = sb("minus_half", [P, TILES])
    zT = sb("zT", [HALF, 2, SEQ])
    qk = sb("qk", [P, TILES, 2 * D])
    v32 = sb("v32", [P, TILES, HEADS, 32])
    split = sb("split", [P, TILES, 2 * HEADS, 64], F16)
    qT = sb("qT", [P, PAIR_RING, SEQ], F16)
    kT = sb("kT", [P, PAIR_RING, SEQ], F16)
    work = sb("work", [P, max((A_RING + 1) * TRI, 2 * FEATURES)])
    yraw = sb("yraw", [P, SEQ])
    y_sb = sb("y_sb", [P, TILES, D])
    rope_a = sb("rope_a", [P, 2 * D])
    rope_b = sb("rope_b", [P, 2 * D])
    den = sb("den", [P, TILES * GROUP])
    rden = sb("rden", [P, TILES * GROUP])
    ident16 = sb("ident16", [P, P], F16)
    causal = sb("causal", [P, P])
    rope_cos = sb("rope_cos", [P, TILES, HD])
    rope_sin = sb("rope_sin", [P, TILES, HD])
    wqkvT = sb("wqkvT", [HALF, 2, 3 * D])
    wpT = sb("wpT", [HALF, 2, D])
    switch_w = sb("switch_w", [HALF, 2, EXPERTS])
    switch_b = sb("switch_b", [P, EXPERTS])

    weight = [work[:, s * TRI:(s + 1) * TRI] for s in range(A_RING)]
    factor = work[:, A_RING * TRI:(A_RING + 1) * TRI]
    w_raw = work[0:HALF, 0:2 * FEATURES].rearrange("p (o f) -> p o f", o=2)
    w_pairs = split[0:HALF].rearrange("p t h i -> p (t h i)").bitcast(F32)[:, 0:2 * 2 * SUB * P]\
        .rearrange("p (o s i n) -> p o s i n", o=2, s=2, i=SUB)
    attn_raw = [hacc[0:HALF, 0:2, :], hacc[0:HALF, 2:4, :], z[0:HALF, 0:2, :], z[0:HALF, 2:4, :]]

    acc = ctx.enter_context(nc.psum_tensor("acc", [P, 2, 512], F32))
    score = ctx.enter_context(nc.psum_tensor("score", [P, 4 * 512], F32))
    shared = [ctx.enter_context(nc.psum_tensor(f"shared{i}", [P, 512], F32)) for i in range(2)]

    w_loaded, small_loaded, x_loaded, txt_loaded = sem("w_loaded"), sem("small_loaded"), sem("x_loaded"), sem("txt_loaded")
    h_stored, z2_stored, fill_ready, slots_filled = sem("h_stored"), sem("z2_stored"), sem("fill_ready"), sem("slots_filled")
    zero_ready, const_ready, pairs_ready, ones_ready = sem("zero_ready"), sem("const_ready"), sem("pairs_ready"), sem("ones_ready")
    wt_full, wt_act, wt_dve, at_full, at_free = sem("wt_full"), sem("wt_act"), sem("wt_dve"), sem("at_full"), sem("at_free")
    misc_full, misc_free = sem("misc_full"), [sem("misc_free0"), sem("misc_free1")]
    turns_made, turns_ready, frac_ready, abs_ready, trig_ready, chunk_used = (
        sem("turns_made"), sem("turns_ready"), sem("frac_ready"), sem("abs_ready"), sem("trig_ready"), sem("chunk_used"))
    hacc_ready, h_copied = sem("hacc_ready"), sem("h_copied")
    ln_stats, ln_aggr, ln_var, ln_rstd = sem("ln_stats"), sem("ln_aggr"), sem("ln_var"), sem("ln_rstd")
    z_ready, z2_ready = sem("z_ready"), sem("z2_ready")
    rope_parts, rope_done, hi_ready, lo_ready = sem("rope_parts"), sem("rope_done"), sem("hi_ready"), sem("lo_ready")
    score_full, square_done, factor_ready, y_done, y2_done = (
        sem("score_full"), sem("square_done"), sem("factor_ready"), sem("y_done"), sem("y2_done"))
    tanh_done, weight_ready, den_step = sem("tanh_done"), sem("weight_ready"), sem("den_step")

    table = timetable()
    spans = [steps_between(table, b * SPAN, (b + 1) * SPAN, b) for b in range(BATCHES)]
    begin, first, looped, before_last, last = (
        steps_between(table, -4 * SPAN, 0, 0), spans[0], spans[1], spans[-2], spans[-1])
    end = steps_between(table, BATCHES * SPAN, (BATCHES + 2) * SPAN, BATCHES - 1)
    LOOPS = BATCHES - 3
    assert all(span == looped for span in spans[1:1 + LOOPS])
    f_begin = fills(begin)
    f_first = f_begin + fills(first)
    f_loop = fills(looped)
    assert f_loop % 2 == 0
    f_before_last = f_first + LOOPS * f_loop
    f_last = f_before_last + fills(before_last)
    f_end = f_last + fills(last)

    def program(eng, emit):
        def run(steps, half, odd, batch):
            for name, n, f, args in walk(steps, half, odd, batch):
                emit(name, n, f, args)

        run(begin, 0, 0, 0)
        run(first, *divmod(f_begin, 2), 0)
        with eng.Fori(1, 1 + LOOPS) as b:
            run(looped, (b - 1) * (f_loop // 2) + f_first // 2, f_first % 2, b)
        run(before_last, *divmod(f_before_last, 2), BATCHES - 2)
        run(last, *divmod(f_last, 2), BATCHES - 1)
        run(end, *divmod(f_end, 2), BATCHES - 1)

    def wait_free(eng, f):
        for bank in range(2):
            wait(eng, misc_free[bank], f.of(bank))

    def wait(eng, s, value):
        if isinstance(value, int) and value <= 0:
            return
        eng.wait_ge(s, value)

    def norms_before(name, n):
        if name == "LN1":
            return 0 if isinstance(n, int) and n == 0 else n * 2 - 1
        return n * 2 + 1 if isinstance(n, int) and n == BATCHES - 1 else n * 2 + 2

    W_FILLS = CHUNKS * SUB
    block = ctx.enter_context(nc.Block())

    @block.sync
    def _(sp):
        sp.dma_start(w_raw, io["W"].rearrange("(o p) f -> p o f", p=HALF)).then_inc(w_loaded, 16)
        for raw, name in zip(attn_raw, ("Wq", "Wk", "Wv", "Wproj")):
            sp.dma_start(raw, io[name].rearrange("(o p) f -> p o f", p=HALF)).then_inc(small_loaded, 16)
        with nc.allow_non_contiguous_dma(reason="a few words of frequencies"):
            sp.dma_start(freq[:, 0:BANDS], io["freq"][None, :].to_broadcast([P, BANDS])).then_inc(small_loaded, 16)
            for side in range(2):
                sp.dma_start(freq[64 * side:64 * side + 64, BANDS:BANDS + SUB],
                             io["freq"].rearrange("(i s) -> s i", s=2)[side:side + 1, :].to_broadcast([64, SUB]))\
                    .then_inc(small_loaded, 16)
        sp.dma_start(rope_cos[:], io["cos"]).then_inc(small_loaded, 16)
        sp.dma_start(rope_sin[:], io["sin"]).then_inc(small_loaded, 16)
        sp.dma_start(switch_w[:], io["switch_w"].rearrange("(k p) e -> p k e", p=HALF)).then_inc(small_loaded, 16)
        sp.dma_start(switch_b[:], io["switch_b"][None, :].to_broadcast([P, EXPERTS])).then_inc(small_loaded, 16)

        def load_x(n, q):
            src = io["x"][bass.ds(n, 1)].rearrange("o (t p) c -> p (o t) c", p=P)
            if q < X_BLOCKS - 1:
                sp.dma_start(xraw[:], src[:, :, q * P:(q + 1) * P]).then_inc(x_loaded, 32)
            else:
                for side in range(2):
                    sp.dma_start(xraw[:, :, side * 64:(side + 1) * 64], src[:, :, CH - 64:CH]).then_inc(x_loaded, 16)

        load_x(0, 0)
        sp.wait_ge(at_free, 4)
        sp.dma_start(hacc[:, IMG_TILES, :], io["txt"][0]).then_inc(txt_loaded, 16)

        def emit(name, n, f, args):
            if name == "XT":
                q = (args[0] + 1) % X_BLOCKS
                if q == 0 and isinstance(n, int) and n == BATCHES - 1:
                    return
                sp.wait_ge(misc_full, f.total + 1)
                load_x(n + (q == 0), q)
            elif name == "COPYH":
                if isinstance(n, int) and n == BATCHES - 1:
                    return
                sp.wait_ge(h_copied, n + 1)
                sp.dma_start(hacc[:, IMG_TILES, :], io["txt"][bass.ds(n + 1, 1)].rearrange("o p d -> p (o d)"))\
                    .then_inc(txt_loaded, 16)
            elif name == "LN2":
                wait_free(sp, f)
                sp.dma_start(io["h_dram"][:, bass.ds(n * TILES, TILES), :], h[:]).then_inc(h_stored, 16)
                sp.wait_ge(z2_ready, n + 1)
                sp.dma_start(io["z2_dram"][:, bass.ds(n * TILES, TILES), :], z[:]).then_inc(z2_stored, 16)

        program(sp, emit)
        sp.wait_ge(h_stored, 16 * BATCHES)
        sp.wait_ge(z2_stored, 16 * BATCHES)

    @block.gpsimd
    def _(pool):
        pool.memset(h[:], 1.0).then_inc(fill_ready, 1)
        pool.memset(ident[:], 0.0).then_inc(zero_ready, 1)
        pool.memset(ident16[:], 0.0).then_inc(zero_ready, 1)
        pool.memset(causal[:], 1.0).then_inc(zero_ready, 1)
        pool.memset(minus_half[:], -0.5).then_inc(const_ready, 1)
        pool.wait_ge(zero_ready, 3)
        for m in (ident, ident16):
            pool.affine_select(out=m[:], in_=m[:], compare_op=ALU.not_equal, fill=1.0, base=0,
                               pattern=[[-1, P]], channel_multiplier=1).then_inc(const_ready, 1)
        pool.affine_select(out=causal[:], in_=causal[:], compare_op=ALU.is_ge, fill=0.0, base=0,
                           pattern=[[1, P]], channel_multiplier=-1).then_inc(const_ready, 1)

        def emit(name, n, f, args):
            if name == "YN":
                c, = args
                pool.wait_ge(turns_ready, n * CHUNKS + c + 1)
                pool.tensor_tensor(turns[c % RING][:], turns[c % RING][:], whole[c % RING][:],
                                   ALU.subtract).then_inc(frac_ready, 1)
            elif name in ("LN1", "LN2"):
                m = norms_before(name, n)
                pool.wait_ge(ln_var, m + 1)
                pool.tensor_tensor(rstd[:], var_eps[:], minus_half[:], ALU.pow).then_inc(ln_rstd, 1)
            elif name == "ROPE":
                t, = args
                done = n * TILES + t
                wait_free(pool, f)
                wait(pool, rope_done, done)
                shape = [P, 2 * HEADS, HD]
                q3, a3, b3 = (m.rearrange("p (h i) -> p h i", i=HD) for m in (qk[:, t, :], rope_a[:], rope_b[:]))
                pool.tensor_tensor(a3, q3, rope_cos[:, t, None, :].to_broadcast(shape), ALU.mult).then_inc(rope_parts, 1)
                half = [P, 2 * HEADS, HD // 2]
                for e in range(2):
                    pool.tensor_tensor(b3[:, :, e::2], q3[:, :, 1 - e::2],
                                       rope_sin[:, t, None, e::2].to_broadcast(half), ALU.mult).then_inc(rope_parts, 1)
                pool.wait_ge(rope_parts, 3 * done + 3)
                pool.tensor_tensor(qk[:, t, :], rope_a[:], rope_b[:], ALU.add).then_inc(rope_done, 1)
            elif name == "SPLIT":
                pool.wait_ge(hi_ready, 2 * n + 2)
                a4 = qk[:].rearrange("p t (h i) -> p t h i", i=HD)
                for w, at in ((0, 32), (1, 16)):
                    hs = slice(w * HEADS, (w + 1) * HEADS)
                    pool.tensor_tensor(split[:, :, hs, at:at + HD], a4[:, :, hs, :], split[:, :, hs, 0:HD],
                                       ALU.subtract).then_inc(lo_ready, 1)

        program(pool, emit)

    @block.scalar
    def _(act):
        act.wait_ge(fill_ready, 1)
        act.dma_start(io["xs_dram"].rearrange("(p k n) d -> p k (n d)", p=P, n=2),
                      h[:].rearrange("p t d -> p (t d)")[:, None, 0:2 * WIDE].to_broadcast([P, SLOTS // P // 2, 2 * WIDE]))\
            .then_inc(slots_filled, 16)
        act.wait_ge(const_ready, 1)
        act.activation(den[:, 0:1], minus_half[:, 0:1], ACT.Silu).then_inc(ones_ready, 1)
        for k in range(0, W_FILLS, 2):
            act.wait_ge(wt_full, k + 1)
            act.activation(WT[:, 2 * k:2 * k + 2, :], score[:, (k % 4) * 512:(k % 4) * 512 + 2 * D], ACT.Copy).then_inc(wt_act, 1)

        act.wait_ge(ones_ready, 7)

        def emit(name, n, f, args):
            misc = shared[f.bank]

            def evac(out, in_):
                act.wait_ge(misc_full, f.total + 1)
                act.activation(out, in_, ACT.Copy).then_inc(misc_free[f.bank], 1)

            if name == "XT":
                q, = args
                wait(act, turns_ready, n * CHUNKS + 2 * q)
                evac(xT[:], misc[:])
            elif name == "TR":
                c, = args
                act.wait_ge(abs_ready, n * CHUNKS + c + 1)
                act.activation(turns[c % RING][:], turns[c % RING][:], ACT.Sin, scale=TWO_PI).then_inc(trig_ready, 1)
                act.activation(whole[c % RING][:], whole[c % RING][:], ACT.Sin, scale=-TWO_PI,
                               bias=keep["half_pi"][:, 0:1]).then_inc(trig_ready, 1)
            elif name in ("ZT", "PT", "Z2T"):
                i, = args
                w = min(2, TILES - 2 * i)
                evac(zT[:, :, 2 * i * P:(2 * i + w) * P].rearrange("p k (t n) -> p t k n", n=P),
                     misc[0:HALF, 0:w * 2 * P].rearrange("p (t k n) -> p t k n", t=w, k=2))
            elif name == "QK":
                if args[0] == 0:
                    wait(act, lo_ready, 2 * n)
                evac(qk[:, args[0], :], misc[:, 0:2 * D])
            elif name == "V":
                evac(v32[:, args[0], :, 0:HD], misc[:, 0:D].rearrange("p (h i) -> p h i", i=HD))
            elif name == "TPQ":
                evac(qT[:, args[0] % PAIR_RING, :], misc[:].bitcast(F16)[:, 0:SEQ])
            elif name == "E1":
                i, = args
                H = n * HEADS + i
                A, B = weight[i % A_RING], factor
                for j, (a, b) in enumerate(HALVES):
                    act.wait_ge(score_full, 2 * H + j + 1)
                    act.activation(A[:, a:b], score[:, a:b], ACT.Square, scale=HD ** -0.5).then_inc(square_done, 1)
                act.wait_ge(square_done, 2 * H + 2)
                wait(act, y2_done, H)
                act.activation(B, A, ACT.Square, bias=keep["erf_h1"][:, 0:1]).then_inc(factor_ready, 1)
            elif name == "E2":
                i, = args
                A = weight[i % A_RING]
                act.activation(A, A, ACT.Square, bias=keep["erf_h2"][:, 0:1]).then_inc(factor_ready, 1)
                if not (isinstance(n, int) and n == 0 and i == 0):
                    tanh(n, i - 1)
            elif name == "ELAST":
                tanh(n, HEADS - 1)
            elif name == "AV":
                g, part = args
                a, w = (0, 512) if part == 0 else (512, SEQ - 512)
                evac(yraw[:, a:a + w], misc[:, 0:w])

        def tanh(n, i):
            act.wait_ge(y2_done, n * HEADS + i + 1)
            A = weight[i % A_RING]
            act.activation(A, A, ACT.Tanh, scale=ERF_C * HD ** -0.5).then_inc(tanh_done, 1)

        program(act, emit)

    @block.vector
    def _(dve):
        dve.memset(keep["half_pi"][:], HALF_PI).then_inc(ones_ready, 1)
        dve.memset(keep["erf_h1"][:], ERF_H1).then_inc(ones_ready, 1)
        dve.memset(keep["erf_h2"][:], ERF_H2).then_inc(ones_ready, 1)
        dve.memset(v32[:], 0.0).then_inc(ones_ready, 1)
        dve.wait_ge(ones_ready, 5)
        dve.memset(v32[:, :, :, HD:HD + 1], 1.0).then_inc(ones_ready, 1)
        dve.wait_ge(w_loaded, 16)
        for o in range(2):
            for s in range(2):
                for i in range(SUB):
                    src = w_raw[:, o, (CH - 64) * 12:].rearrange("p (j k) -> p k j", k=12)[:, s * BANDS + 2 * i:s * BANDS + 2 * i + 2, :]
                    last = dve.tensor_copy(w_pairs[:, o, s, i, :].rearrange("p (k j) -> p k j", k=2), src)
        last.then_inc(pairs_ready, 1)
        for k in range(1, W_FILLS, 2):
            dve.wait_ge(wt_full, k + 1)
            dve.tensor_copy(WT[:, 2 * k:2 * k + 2, :],
                            score[:, (k % 4) * 512:(k % 4) * 512 + 2 * D].rearrange("p (t n) -> p t n", t=2)).then_inc(wt_dve, 1)
        dve.wait_ge(wt_full, W_FILLS)
        dve.memset(split[:], 0.0).then_inc(ones_ready, 1)
        for m in range(4):
            dve.wait_ge(at_full, m + 1)
            src = shared[0][0:HALF, 0:2 * D].rearrange("p (k n) -> p k n", k=2)
            dst = wqkvT[:, :, m * D:(m + 1) * D] if m < 3 else wpT[:]
            dve.tensor_copy(dst, src).then_inc(at_free, 1)
        dve.wait_ge(small_loaded, 16 * 11)
        dve.wait_ge(const_ready, 4)

        def norm(n, m, src, dst, done):
            for t in range(TILES):
                dve.bn_stats(stats[:, t, :], src[:, t, :]).then_inc(ln_stats, 1)
            dve.wait_ge(ln_stats, TILES * m + TILES)
            dve.memset(gate[:], 0.0)
            for t in range(TILES):
                dve.bn_aggr(moments[:, t, :], stats[:, t, :]).then_inc(ln_aggr, 1)
            dve.wait_ge(ln_aggr, TILES * m + TILES)
            dve.tensor_scalar(var_eps[:], moments[:, :, 1], 1e-5, None, ALU.add).then_inc(ln_var, 1)
            dve.wait_ge(ln_rstd, m + 1)
            for t in range(TILES):
                last = dve.tensor_scalar(dst[:, t, :], src[:, t, :], moments[:, t, 0:1], rstd[:, t:t + 1],
                                         ALU.subtract, ALU.mult)
            last.then_inc(done, 1)

        def emit(name, n, f, args):
            misc, free = shared[f.bank], misc_free[f.bank]
            if name == "YN":
                c, = args
                K = n * CHUNKS + c
                if c % 2 == 0:
                    wait_free(dve, f)
                wait(dve, chunk_used, K - RING + 1)
                for i in range(SUB):
                    col = freq[:, BANDS + i:BANDS + i + 1] if c == CHUNKS - 1 else freq[:, SUB * (c % 2) + i:SUB * (c % 2) + i + 1]
                    src = xT[:]
                    cols = slice(i * IMG, (i + 1) * IMG)
                    last = dve.tensor_scalar(turns[c % RING][:, cols], src, col, None, ALU.mult)
                last.then_inc(turns_made, 1)
                dve.wait_ge(turns_made, K + 1)
                dve.tensor_scalar(whole[c % RING][:], turns[c % RING][:], ROUND, ROUND, ALU.add, ALU.subtract).then_inc(turns_ready, 1)
            elif name == "AB":
                c, = args
                dve.wait_ge(frac_ready, n * CHUNKS + c + 1)
                dve.tensor_scalar(whole[c % RING][:].bitcast(I32), turns[c % RING][:].bitcast(I32), 0x7FFFFFFF, None,
                                  ALU.bitwise_and).then_inc(abs_ready, 1)
            elif name == "HEVAC":
                dve.wait_ge(chunk_used, (n + 1) * CHUNKS)
                wait(dve, h_copied, n)
                for j in range(2):
                    last = dve.tensor_copy(hacc[:, 2 * j:2 * j + 2, :], acc[:, j, 0:2 * D].rearrange("p (t n) -> p t n", t=2))
                last.then_inc(hacc_ready, 1)
            elif name == "LN1":
                dve.wait_ge(txt_loaded, 16 * (n + 1))
                dve.wait_ge(hacc_ready, n + 1)
                if not (isinstance(n, int) and n <= 1):
                    dve.wait_ge(z2_stored, 16 * (n - 1))
                norm(n, norms_before(name, n), hacc, z, z_ready)
            elif name == "LN2":
                wait_free(dve, f)
                if isinstance(n, int) and n == BATCHES - 1:
                    dve.wait_ge(z2_stored, 16 * n)
                norm(n, norms_before(name, n), h, z, z2_ready)
            elif name == "SPLIT":
                dve.wait_ge(rope_done, (n + 1) * TILES)
                dve.wait_ge(misc_full, f.total)
                a4 = qk[:].rearrange("p t (h i) -> p t h i", i=HD)
                for w in range(2):
                    hs = slice(w * HEADS, (w + 1) * HEADS)
                    for e in range(2):
                        at = 16 * e if w == 0 else 32 * e
                        last = dve.tensor_copy(split[:, :, hs, at:at + HD], a4[:, :, hs, :])
                    last.then_inc(hi_ready, 1)
            elif name == "TPK":
                dve.wait_ge(misc_full, f.total + 1)
                dve.tensor_copy(kT[:, args[0] % PAIR_RING, :], misc[:].bitcast(F16)[:, 0:SEQ]).then_inc(free, 1)
            elif name == "E2":
                i, = args
                H = n * HEADS + i
                B = factor
                dve.wait_ge(factor_ready, 2 * H + 1)
                for a, b in HALVES:
                    dve.scalar_tensor_tensor(B[:, a:b], B[:, a:b], ERF_K1, score[:, a:b], ALU.add, ALU.mult).then_inc(y_done, 1)
            elif name == "E3":
                i, = args
                H = n * HEADS + i
                A, B = weight[i % A_RING], factor
                dve.wait_ge(factor_ready, 2 * H + 2)
                dve.wait_ge(y_done, 2 * H + 2)
                dve.scalar_tensor_tensor(A, A, ERF_K2, B, ALU.add, ALU.mult).then_inc(y2_done, 1)
                if not (isinstance(n, int) and n == 0 and i == 0):
                    weights(n, i - 1)
            elif name == "ELAST":
                weights(n, HEADS - 1)
            elif name == "YT":
                g, part = args
                w = 4 if part == 0 else 1
                k = 2 * (2 * (n * (HEADS // GROUP) + g) + part)
                src = misc[:, 0:w * P].rearrange("p (t h i) -> p t h i", t=w, i=32)
                dn = den[:, 0:w * GROUP].rearrange("p (t h) -> p t h", t=w)
                dve.wait_ge(misc_full, f.total + 1)
                dve.tensor_scalar(dn, src[:, :, :, HD], 1e-6, None, ALU.max).then_inc(den_step, 1)
                dve.wait_ge(den_step, k + 1)
                dve.reciprocal(rden[:, 0:w * GROUP], den[:, 0:w * GROUP]).then_inc(den_step, 1)
                dve.wait_ge(den_step, k + 2)
                rd = rden[:, 0:w * GROUP].rearrange("p (t h) -> p t h", t=w)
                out = y_sb[:, 4 * part:4 * part + w, g * GROUP * HD:(g + 1) * GROUP * HD].rearrange("p t (h i) -> p t h i", i=HD)
                dve.tensor_tensor(out, src[:, :, :, 0:HD], rd[:, :, :, None].to_broadcast([P, w, GROUP, HD]),
                                  ALU.mult).then_inc(free, 1)
            elif name == "PJ":
                i, = args
                w = min(2, TILES - 2 * i)
                dve.wait_ge(misc_full, f.total + 1)
                if i == 0:
                    dve.wait_ge(h_copied, n + 1)
                ins = dve.tensor_tensor(h[:, 2 * i:2 * i + w, :], misc[:, 0:w * D].rearrange("p (t n) -> p t n", t=w),
                                        h[:, 2 * i:2 * i + w, :], ALU.add)
                ins.then_inc(free, 1)
            elif name == "RT":
                dve.wait_ge(misc_full, f.total + 1)
                dve.tensor_tensor(logits[:, bass.ds(n * TILES, TILES), :], misc[:, 0:TILES * EXPERTS].rearrange("p (t e) -> p t e", t=TILES),
                                  switch_b[:, None, :].to_broadcast([P, TILES, EXPERTS]), ALU.add).then_inc(free, 1)
            elif name == "COPYH":
                dve.wait_ge(slots_filled, 16)
                wait(dve, h_stored, 16 * n)
                wait(dve, z2_ready, n)
                dve.tensor_copy(h[:], hacc[:]).then_inc(h_copied, 1)

        def weights(n, i):
            A = weight[i % A_RING]
            dve.wait_ge(tanh_done, n * HEADS + i + 1)
            dg = A[:, 0:TILES * P].rearrange("p (t n) -> p t n", t=TILES)
            dve.scalar_tensor_tensor(dg, dg, 1.0, causal[:, None, :].to_broadcast([P, TILES, P]), ALU.add, ALU.mult)
            dve.tensor_scalar(A[:, TILES * P:TRI], A[:, TILES * P:TRI], 1.0, None, ALU.add).then_inc(weight_ready, 1)

        program(dve, emit)

    @block.tensor
    def _(pe):
        pe.wait_ge(const_ready, 4)
        pe.wait_ge(w_loaded, 16)
        for k in range(W_FILLS):
            if k >= 4:
                pe.wait_ge(wt_dve if k % 2 else wt_act, (k - 4) // 2 + 1)
            if k == 0:
                pe.wait_ge(pairs_ready, 1)
            c, i = divmod(k, SUB)
            for s in range(2):
                for o in range(2):
                    if c < CHUNKS - 1:
                        band = SUB * (c % 2) + i
                        at = chunk_block(c) * P * 12 + s * BANDS + band
                        src = w_raw[:, o, at:at + 127 * 12 + 1:12]
                    else:
                        src = w_pairs[:, o, s, i, :]
                    at = (k % 4) * 512 + s * D + o * HALF
                    last = pe.transpose(score[:, at:at + HALF], src, ident[0:HALF, 0:HALF])
            last.then_inc(wt_full, 1)
        pe.wait_ge(small_loaded, 16 * 11)
        for m, raw in enumerate(attn_raw):
            if m:
                pe.wait_ge(at_free, m)
            for k in range(2):
                for o in range(2):
                    last = pe.transpose(shared[0][0:HALF, k * D + o * HALF:k * D + (o + 1) * HALF],
                                        raw[:, o, k * HALF:(k + 1) * HALF], ident[0:HALF, 0:HALF])
            last.then_inc(at_full, 1)
        pe.wait_ge(at_free, 4)
        pe.wait_ge(wt_act, (W_FILLS + 1) // 2)
        pe.wait_ge(wt_dve, W_FILLS // 2)
        pe.wait_ge(ones_ready, 7)

        def emit(name, n, f, args):
            misc = shared[f.bank]
            if name in FILLS:
                wait(pe, misc_free[f.bank], f.of(f.bank))
            if name == "XT":
                q, = args
                pe.wait_ge(x_loaded, 32 * (n * X_BLOCKS + q + 1))
                for t in range(IMG_TILES):
                    last = pe.transpose(misc[:, t * P:(t + 1) * P], xraw[:, t, :], ident[:])
                last.then_inc(misc_full, 1)
            elif name == "MM":
                c, m = args
                s, i = divmod(m, SUB)
                K = n * CHUNKS + c
                if c == 0 and m == 0:
                    wait(pe, hacc_ready, n)
                if i == 0:
                    pe.wait_ge(trig_ready, 2 * K + s + 1)
                feat = (turns, whole)[s][c % RING]
                for t in range(IMG_TILES):
                    first = c == 0 and m == 0 and t % 2 == 0
                    end = c == CHUNKS - 1 and m == PIECES_OF_CHUNK - 1 and t % 2 == 1
                    last = pe.matmul(acc[:, t // 2, (t % 2) * D:(t % 2 + 1) * D],
                                     feat[:, i * IMG + t * P:i * IMG + (t + 1) * P],
                                     WT[:, 2 * (c * SUB + i) + s, :], start=first, stop=end)
                if m == PIECES_OF_CHUNK - 1:
                    last.then_inc(chunk_used, 1)
            elif name in ("ZT", "PT", "Z2T"):
                i, = args
                if name == "ZT" and i == 0:
                    pe.wait_ge(z_ready, n + 1)
                if name == "Z2T" and i == 0:
                    pe.wait_ge(z2_ready, n + 1)
                if name == "PT" and i == 0:
                    wait_free(pe, f)
                src = y_sb if name == "PT" else z
                for t in range(min(2, TILES - 2 * i)):
                    for k in range(2):
                        last = pe.transpose(misc[0:HALF, (2 * t + k) * P:(2 * t + k + 1) * P],
                                            src[:, 2 * i + t, k * HALF:(k + 1) * HALF], ident[:])
                last.then_inc(misc_full, 1)
            elif name in ("QK", "V"):
                t, = args
                cols = slice(0, 2 * D) if name == "QK" else slice(2 * D, 3 * D)
                w = cols.stop - cols.start
                if name == "QK":
                    wait_free(pe, f)
                for k in range(2):
                    last = pe.matmul(misc[:, 0:w], zT[:, k, t * P:(t + 1) * P], wqkvT[:, k, cols], start=k == 0, stop=k == 1)
                last.then_inc(misc_full, 1)
            elif name in ("TPQ", "TPK"):
                hp, = args
                pe.wait_ge(lo_ready, 2 * n + 2)
                at = 2 * hp + (HEADS if name == "TPK" else 0)
                for t in range(TILES):
                    last = pe.transpose(misc[:].bitcast(F16)[:, t * P:(t + 1) * P],
                                        split[:, t, at:at + 2, :].rearrange("p h i -> p (h i)"), ident16[:])
                last.then_inc(misc_full, 1)
            elif name == "S":
                i, = args
                H = n * HEADS + i
                wait_free(pe, f)
                rows = slice(64 * (i % 2), 64 * (i % 2) + 64)
                for j, (a, b) in enumerate(HALVES):
                    wait(pe, y_done, 2 * (H - 1) + j + 1)
                    for at, t, q0, w in PIECES:
                        if not a <= at < b:
                            continue
                        last = pe.matmul(score[:, at:at + w], kT[rows, i // 2 % PAIR_RING, t * P:(t + 1) * P],
                                         qT[rows, i // 2 % PAIR_RING, q0:q0 + w], start=True, stop=True)
                    last.then_inc(score_full, 1)
            elif name == "AV":
                g, part = args
                pe.wait_ge(weight_ready, n * HEADS + GROUP * (g + 1))
                if g == 0 and part == 0:
                    wait_free(pe, f)
                lo, hi = (0, 512) if part == 0 else (512, SEQ)
                todo = []
                for at, t, q0, w in sorted(PIECES, key=lambda p: (p[1], p[2])):
                    a, b = max(lo, q0), min(hi, q0 + w)
                    if a < b:
                        todo.append((at + a - q0, t, a, b - a))
                for m, (at, t, q0, w) in enumerate(todo):
                    for r in range(GROUP):
                        head = GROUP * g + r
                        last = pe.matmul(misc[32 * r:32 * r + 32, q0 - lo:q0 - lo + w], v32[:, t, head, :],
                                         weight[head % A_RING][:, at:at + w], start=m == 0, stop=m == len(todo) - 1)
                last.then_inc(misc_full, 1)
            elif name == "YT":
                g, part = args
                if part == 0:
                    wait_free(pe, f)
                for t in range(4 if part == 0 else 1):
                    last = pe.transpose(misc[:, t * P:(t + 1) * P], yraw[:, (4 * part + t) * P:(4 * part + t + 1) * P], ident[:])
                last.then_inc(misc_full, 1)
            elif name == "PJ":
                i, = args
                wait_free(pe, f)
                for t in range(min(2, TILES - 2 * i)):
                    for k in range(2):
                        last = pe.matmul(misc[:, t * D:(t + 1) * D], zT[:, k, (2 * i + t) * P:(2 * i + t + 1) * P],
                                         wpT[:, k, :], start=k == 0, stop=k == 1)
                last.then_inc(misc_full, 1)
            elif name == "RT":
                wait_free(pe, f)
                for t in range(TILES):
                    for k in range(2):
                        last = pe.matmul(misc[:, t * EXPERTS:(t + 1) * EXPERTS], zT[:, k, t * P:(t + 1) * P],
                                         switch_w[:, k, :], start=k == 0, stop=k == 1)
                last.then_inc(misc_full, 1)

        program(pe, emit)


def experts(nc, ctx, io, keep):
    def sb(name, shape, dt=F32):
        return ctx.enter_context(nc.sbuf_tensor(name, shape, dt))

    def sem(name):
        return ctx.enter_context(nc.semaphore(name))

    ident, logits = keep["ident"], keep["logits"]
    sending = sb("sending", [P, ALL_TILES, WIDE])
    plain = sb("plain", [P, ALL_TILES, D])
    token = sb("token", [P, ALL_TILES], I32)
    top = sb("top", [P, ALL_TILES])
    below = sb("below", [P, ALL_TILES, EXPERTS])
    expo = sb("expo", [P, ALL_TILES, EXPERTS])
    number = sb("number", [P, EXPERTS])
    is_top = sb("is_top", [P, ALL_TILES, EXPERTS])
    route = sb("route", [P, ALL_TILES])
    onehot = sb("onehot", [P, ALL_TILES, EXPERTS])
    total = sb("total", [P, ALL_TILES])
    prob = sb("prob", [P, ALL_TILES])
    prob_e = sb("prob_e", [P, ALL_TILES, EXPERTS])
    level = sb("level", [P, LEVELS, EXPERTS])
    step_size = sb("step_size", [P, 1])
    tried = sb("tried", [P, LEVELS, EXPERTS])
    reached = sb("reached", [P, ALL_TILES, LEVELS * EXPERTS], F16)
    counts = sb("counts", [P, LEVELS * EXPERTS])
    passed = sb("passed", [P, LEVELS, EXPERTS])
    gain = sb("gain", [P, EXPERTS])
    threshold = sb("threshold", [P, EXPERTS])
    above = sb("above", [P, ALL_TILES, EXPERTS], F16)
    equal = sb("equal", [P, ALL_TILES, EXPERTS])
    tied = sb("tied", [P, ALL_TILES, EXPERTS], F16)
    room = sb("room", [P, EXPERTS])
    fits = sb("fits", [P, ALL_TILES, EXPERTS])
    kept = sb("kept", [P, ALL_TILES, EXPERTS], F16)
    first_slot = sb("first_slot", [P, EXPERTS])
    slot_e = sb("slot_e", [P, ALL_TILES, EXPERTS])
    place = sb("place", [P, ALL_TILES])
    gate = sb("pool_gate", [P, 2])
    lost = sb("lost", [P, ALL_TILES])
    slots = sb("slots", [P, ALL_TILES], U32)
    ones16 = sb("ones16", [P, P], F16)
    earlier = sb("earlier", [P, P], F16)
    b1_raw = sb("b1_raw", [EXPERTS * F_TILES, P])
    b1 = sb("b1", [P, EXPERTS * F_TILES])
    b2 = sb("b2", [BLOCK_P, EXPERTS, D])
    bias = [sb(f"bias{i}", [P, F_TILES]) for i in range(2)]
    w1 = [sb(f"w1_{i}", [HALF, 2, HIDDEN]) for i in range(2)]
    w2 = [sb(f"w2_{i}", [P, F_TILES, D]) for i in range(2)]
    rows = [sb(f"rows{i}", [BLOCK_P, ROWS, WIDE]) for i in range(ROWS_RING)]
    rowsT = sb("rowsT", [HALF, 2, BLOCK])
    hid = sb("hid", [P, F_TILES, BLOCK])
    made = [sb(f"made{i}", [BLOCK_P, ROWS, D]) for i in range(2)]

    HB = 4
    hid_ps = ctx.enter_context(nc.psum_tensor("hid_ps", [P, HB, 512], F32))
    rowsT_ps = ctx.enter_context(nc.psum_tensor("rowsT_ps", [P, 2, 512], F32))
    made_ps = ctx.enter_context(nc.psum_tensor("made_ps", [P, 2, 512], F32))

    z_loaded, h_loaded, b1_loaded, b2_loaded = sem("z_loaded"), sem("h_loaded"), sem("b1_loaded"), sem("b2_loaded")
    token_loaded, sending_ready, sent, plain_ready, plain_stored = (
        sem("token_loaded"), sem("sending_ready"), sem("sent"), sem("plain_ready"), sem("plain_stored"))
    masks_ready, route_step, expo_ready = sem("masks_ready"), sem("route_step"), sem("expo_ready")
    try_ready, reached_ready, counted, count_read, passed_ready, gain_ready, threshold_ready, step_ready = (
        sem("try_ready"), sem("reached_ready"), sem("counted"), sem("count_read"), sem("passed_ready"),
        sem("gain_ready"), sem("threshold_ready"), sem("step_ready"))
    above_ready, tied_ready, above_counted, tied_before, kept_ready, kept_before = (
        sem("above_ready"), sem("tied_ready"), sem("above_counted"), sem("tied_before"), sem("kept_ready"), sem("kept_before"))
    slots_ready, b1_full, b1_ready = sem("slots_ready"), sem("b1_full"), sem("b1_ready")
    weights_loaded = [sem("weights_loaded0"), sem("weights_loaded1")]
    rows_loaded = [sem(f"rows_loaded{i}") for i in range(ROWS_RING)]
    made_stored = [sem("made_stored0"), sem("made_stored1")]
    rows_full, rows_half0, rows_half1 = sem("rows_full"), sem("rows_half0"), sem("rows_half1")
    hid_full, gelu_done, made_full, made_ready = sem("hid_full"), sem("gelu_done"), sem("made_full"), sem("made_ready")
    sum_ready, gate_ready = sem("sum_ready"), sem("gate_ready")

    SUMMED = 8
    MASKS = 2 * EXPERTS + LEVELS + 6
    block = ctx.enter_context(nc.Block())
    xs_blocks = io["xs_dram"].rearrange("(b p r) d -> b p r d", p=BLOCK_P, r=ROWS)
    out_rows = io["out"].rearrange("b s d -> (b s) d")
    STEP = 2 * PER_EXPERT
    TURNS = BLOCKS // STEP

    def wait(eng, s, value):
        if isinstance(value, int) and value <= 0:
            return
        eng.wait_ge(s, value)

    def program(eng, emit):
        for u in range(STEP):
            emit(0, u, False)
        with eng.Fori(1, TURNS - 1) as i:
            for u in range(STEP):
                emit(i, u, False)
        for u in range(STEP):
            emit(TURNS - 1, u, u == STEP - 1)

    @block.sync
    def _(sp):
        sp.dma_start(token[:], io["token"]).then_inc(token_loaded, 16)
        sp.dma_start(b1_raw[:], io["b1"].rearrange("e (f p) -> (e f) p", p=P)).then_inc(b1_loaded, 16)
        sp.dma_start(sending[:, :, 0:D], io["z2_dram"]).then_inc(z_loaded, 16)
        sp.dma_start(sending[:, :, AT_H:AT_H + D], io["h_dram"]).then_inc(h_loaded, 16)
        sp.dma_start(b2[:], io["b2"].rearrange("(o e) d -> o e d", o=1).to_broadcast([BLOCK_P, EXPERTS, D])).then_inc(b2_loaded, 16)

        def load_weights(e, side):
            sp.dma_start(w1[side][:], io["w1"][bass.ds(e, 1)].rearrange("o (k p) f -> p (o k) f", p=HALF)).then_inc(weights_loaded[side], 16)
            sp.dma_start(bias[side][:], b1[:, bass.ds(e * F_TILES, F_TILES)]).then_inc(weights_loaded[side], 16)
            sp.dma_start(w2[side][:], io["w2"][bass.ds(e, 1)].rearrange("o (f p) d -> p (o f) d", p=P)).then_inc(weights_loaded[side], 16)

        def load_rows(b, side):
            sp.dma_start(rows[side][:], xs_blocks[bass.ds(b, 1)].rearrange("o p r d -> p (o r) d")).then_inc(rows_loaded[side], 16)

        sp.wait_ge(b1_ready, 1)
        for e in range(2):
            load_weights(e, e)
        sp.wait_ge(sent, 16 * ALL_TILES)
        for b in range(2):
            load_rows(b, b)
        for b in range(BATCHES):
            sp.wait_ge(plain_ready, b + 1)
            sp.dma_start(io["out"][b].rearrange("(t p) d -> p t d", p=P), plain[:, b * TILES:(b + 1) * TILES, :]).then_inc(plain_stored, 16)

        def emit(i, u, last):
            b = i * STEP + u
            ends = isinstance(i, int) and i == TURNS - 1
            if not (ends and u >= STEP - 2):
                wait(sp, made_stored[u % 2], 16 * ROWS * (i * 2 + u // 2))
                load_rows(b + 2, (u + 2) % ROWS_RING)
            if u % PER_EXPERT == PER_EXPERT - 1 and not ends:
                sp.wait_ge(made_ready, 2 * b + 2)
                load_weights(i * 2 + u // PER_EXPERT + 2, u // PER_EXPERT)

        program(sp, emit)

    @block.gpsimd
    def _(pool):
        for e in range(EXPERTS):
            pool.memset(number[:, e:e + 1], float(e - EXPERTS)).then_inc(masks_ready, 1)
        pool.memset(earlier[:], 1.0).then_inc(masks_ready, 1)
        pool.wait_ge(masks_ready, EXPERTS + 1)
        pool.affine_select(out=earlier[:], in_=earlier[:], compare_op=ALU.is_ge, fill=0.0, base=-1,
                           pattern=[[1, P]], channel_multiplier=-1).then_inc(masks_ready, 1)
        pool.memset(ones16[:], 1.0).then_inc(masks_ready, 1)
        for e in range(EXPERTS):
            pool.memset(first_slot[:, e:e + 1], float(e * CAPACITY)).then_inc(masks_ready, 1)
        for k in range(LEVELS):
            pool.memset(level[:, k, :], float(k + 1)).then_inc(masks_ready, 1)
        pool.memset(step_size[:], 0.5).then_inc(masks_ready, 1)
        pool.memset(threshold[:], 0.0).then_inc(masks_ready, 1)
        pool.memset(gate[:], 0.0).then_inc(masks_ready, 1)
        pool.wait_ge(slots_ready, 1)
        pool.wait_ge(z_loaded, 16)
        pool.wait_ge(h_loaded, 16)
        pool.wait_ge(sending_ready, 2)
        for t in range(ALL_TILES):
            pool.indirect_dma_start(out=io["xs_dram"], out_offset=bass.IndirectOffsetOnAxis(ap=slots[:, t:t + 1], axis=0),
                                    in_=sending[:, t, :], in_offset=None, bounds_check=SLOTS - 1, oob_is_err=False).then_inc(sent, 16)
        pool.wait_ge(plain_stored, 16 * BATCHES)

        def emit(i, u, last):
            b = i * STEP + u
            wait(pool, gate_ready, b)
            pool.wait_ge(made_ready, 2 * b + 2)
            pool.tensor_tensor(gate[:, 1:2], gate[:, 0:1], gate[:, 0:1], ALU.mult).then_inc(gate_ready, 1)
            for r in range(ROWS):
                where = rows[u % ROWS_RING][:, r, AT_TOKEN:AT_TOKEN + 1].bitcast(U32)
                pool.indirect_dma_start(out=out_rows, out_offset=bass.IndirectOffsetOnAxis(ap=where, axis=0),
                                        in_=made[u % 2][:, r, :], in_offset=None, bounds_check=TOKENS - 1,
                                        oob_is_err=False).then_inc(made_stored[u % 2], 16)

        program(pool, emit)
        for side in range(2):
            pool.wait_ge(made_stored[side], 16 * ROWS * BLOCKS // 2)

    @block.scalar
    def _(act):
        act.wait_ge(route_step, 2)
        act.activation(expo[:], below[:], ACT.Exp).then_inc(expo_ready, 1)
        act.wait_ge(b1_full, 1)
        act.activation(b1[:], rowsT_ps[:, 0, 0:EXPERTS * F_TILES], ACT.Copy).then_inc(b1_ready, 1)

        def emit(i, u, last):
            b = i * STEP + u
            if isinstance(i, int) and b == 0:
                first_rows()
            for f in range(F_TILES):
                G = b * F_TILES + f
                act.wait_ge(hid_full, G + 1)
                if f == 0:
                    wait(act, made_full, 2 * b)
                act.activation(hid[:, f, :], hid_ps[:, (u * F_TILES + f) % HB, 0:BLOCK], ACT.Gelu,
                               bias=bias[u // PER_EXPERT][:, f:f + 1]).then_inc(gelu_done, 1)
            if not last:
                act.wait_ge(rows_full, b + 2)
                act.activation(rowsT[:, 0, :], rowsT_ps[0:HALF, 0, 0:BLOCK], ACT.Copy).then_inc(rows_half0, 1)

        def first_rows():
            act.wait_ge(rows_full, 1)
            act.activation(rowsT[:, 0, :], rowsT_ps[0:HALF, 0, 0:BLOCK], ACT.Copy).then_inc(rows_half0, 1)

        program(act, emit)

    @block.vector
    def _(dve):
        each = [P, ALL_TILES, EXPERTS]
        n = 0

        def step(ins):
            nonlocal n
            ins.then_inc(route_step, 1)
            n += 1
            dve.wait_ge(route_step, n)

        dve.wait_ge(masks_ready, MASKS)
        step(dve.tensor_reduce(top[:], logits[:], AX_X, ALU.max))
        step(dve.tensor_tensor(below[:], logits[:], top[:, :, None].to_broadcast(each), ALU.subtract))
        step(dve.scalar_tensor_tensor(is_top[:], below[:], 0.0, number[:, None, :].to_broadcast(each), ALU.is_ge, ALU.mult))
        step(dve.tensor_reduce(route[:], is_top[:], AX_X, ALU.min))
        step(dve.tensor_tensor(onehot[:], number[:, None, :].to_broadcast(each), route[:, :, None].to_broadcast(each), ALU.is_equal))
        dve.wait_ge(expo_ready, 1)
        step(dve.tensor_reduce(total[:], expo[:], AX_X, ALU.add))
        step(dve.reciprocal(prob[:], total[:]))
        step(dve.tensor_tensor(prob_e[:], onehot[:], prob[:, :, None].to_broadcast(each), ALU.mult))

        dve.wait_ge(token_loaded, 16)
        dve.tensor_copy(sending[:, :, AT_PROB], prob[:]).then_inc(sending_ready, 1)
        dve.tensor_copy(sending[:, :, AT_TOKEN].bitcast(I32), token[:]).then_inc(sending_ready, 1)

        def find(r):
            if not isinstance(r, int) or r > 0:
                dve.wait_ge(threshold_ready, r)
                dve.wait_ge(step_ready, r)
            dve.scalar_tensor_tensor(tried[:], level[:], step_size[:, 0:1],
                                     threshold[:, None, :].to_broadcast([P, LEVELS, EXPERTS]), ALU.mult, ALU.add)\
                .then_inc(try_ready, 1)
            dve.wait_ge(try_ready, r + 1)
            levels = [P, ALL_TILES, LEVELS, EXPERTS]
            dve.tensor_tensor(reached[:].rearrange("p t (k e) -> p t k e", e=EXPERTS),
                              prob_e[:, :, None, :].to_broadcast(levels), tried[:, None, :, :].to_broadcast(levels), ALU.is_ge)\
                .then_inc(reached_ready, 1)
            dve.wait_ge(counted, r + 1)
            dve.tensor_reduce(counts[:], made_ps[:, 0, 0:SUMMED * LEVELS * EXPERTS].rearrange("p (g m) -> p m g", g=SUMMED),
                              AX_X, ALU.add).then_inc(count_read, 1)
            dve.wait_ge(count_read, r + 1)
            dve.tensor_scalar(passed[:].rearrange("p k e -> p (k e)"), counts[:], float(CAPACITY), step_size[:, 0:1],
                              ALU.is_ge, ALU.mult).then_inc(passed_ready, 1)
            dve.wait_ge(passed_ready, r + 1)
            dve.tensor_scalar(step_size[:], step_size[:], 0.25, None, ALU.mult).then_inc(step_ready, 1)
            dve.tensor_reduce(gain[:], passed[:].rearrange("p k e -> p e k"), AX_X, ALU.add).then_inc(gain_ready, 1)
            dve.wait_ge(gain_ready, r + 1)
            dve.tensor_tensor(threshold[:], threshold[:], gain[:], ALU.add).then_inc(threshold_ready, 1)

        for u in range(2):
            find(u)
        with dve.Fori(1, ROUNDS // 2) as i:
            for u in range(2):
                find(2 * i + u)

        dve.wait_ge(threshold_ready, ROUNDS)
        limit = threshold[:, None, :].to_broadcast(each)
        dve.tensor_tensor(above[:], prob_e[:], limit, ALU.is_gt).then_inc(above_ready, 1)
        step(dve.tensor_tensor(equal[:], prob_e[:], limit, ALU.is_equal))
        dve.tensor_tensor(tied[:], equal[:], onehot[:], ALU.mult).then_inc(tied_ready, 1)
        dve.wait_ge(above_counted, 1)
        step(dve.tensor_reduce(room[:], made_ps[:, 0, 0:SUMMED * EXPERTS].rearrange("p (g e) -> p e g", g=SUMMED), AX_X, ALU.add))
        step(dve.tensor_scalar(room[:], room[:], -1.0, float(CAPACITY), ALU.mult, ALU.add))
        dve.wait_ge(tied_before, 1)
        before = made_ps[:, 1, 0:ALL_TILES * EXPERTS].rearrange("p (t e) -> p t e", e=EXPERTS)
        step(dve.tensor_tensor(fits[:], before, room[:, None, :].to_broadcast(each), ALU.is_lt))
        step(dve.tensor_tensor(fits[:], fits[:], tied[:], ALU.mult))
        dve.tensor_tensor(kept[:], fits[:], above[:], ALU.add).then_inc(kept_ready, 1)
        dve.wait_ge(kept_ready, 1)
        step(dve.tensor_reduce(lost[:], kept[:], AX_X, ALU.add))
        step(dve.tensor_scalar(lost[:], lost[:], -4.0 * SLOTS, 4.0 * SLOTS, ALU.mult, ALU.add))
        dve.wait_ge(kept_before, 1)
        before = made_ps[:, 0, 0:ALL_TILES * EXPERTS].rearrange("p (t e) -> p t e", e=EXPERTS)
        step(dve.tensor_tensor(slot_e[:], before, first_slot[:, None, :].to_broadcast(each), ALU.add))
        step(dve.tensor_tensor(slot_e[:], slot_e[:], kept[:], ALU.mult))
        step(dve.tensor_reduce(place[:], slot_e[:], AX_X, ALU.add))
        dve.tensor_tensor(slots[:], place[:], lost[:], ALU.add).then_inc(slots_ready, 1)
        dve.wait_ge(h_loaded, 16)
        dve.wait_ge(z_loaded, 16)
        for t in range(ALL_TILES):
            ins = dve.scalar_tensor_tensor(plain[:, t, :], sending[:, t, 0:D], prob[:, t:t + 1], sending[:, t, AT_H:AT_H + D],
                                           ALU.mult, ALU.add)
            if t % TILES == TILES - 1:
                ins.then_inc(plain_ready, 1)
        dve.wait_ge(b2_loaded, 16)

        def second_half(b):
            dve.wait_ge(rows_full, b + 1)
            dve.tensor_copy(rowsT[:, 1, :], rowsT_ps[0:HALF, 1, 0:BLOCK]).then_inc(rows_half1, 1)

        def emit(i, u, last):
            b = i * STEP + u
            if isinstance(i, int) and b == 0:
                second_half(0)
            if not last:
                second_half(b + 1)
            for j in range(2):
                dve.wait_ge(made_full, 2 * b + j + 1)
                if j == 0:
                    wait(dve, made_stored[u % 2], (i * 2 + u // 2) * 16 * ROWS)
                half = made[u % 2][:, 2 * j:2 * j + 2, :]
                dve.tensor_tensor(half, made_ps[0:BLOCK_P, j, 0:2 * D].rearrange("p (r d) -> p r d", r=2),
                                  b2[:, bass.ds(i * 2 + u // PER_EXPERT, 1), :].to_broadcast([BLOCK_P, 2, D]), ALU.add)\
                    .then_inc(sum_ready, 1)
                dve.wait_ge(sum_ready, 2 * b + j + 1)
                for r in (2 * j, 2 * j + 1):
                    row, result = rows[u % ROWS_RING], made[u % 2][:, r, :]
                    last_row = dve.scalar_tensor_tensor(result, result, row[:, r, AT_PROB:AT_PROB + 1], row[:, r, AT_H:AT_H + D],
                                                        ALU.mult, ALU.add)
                last_row.then_inc(made_ready, 1)

        program(dve, emit)

    @block.tensor
    def _(pe):
        pe.wait_ge(b1_loaded, 16)
        pe.transpose(rowsT_ps[:, 0, 0:EXPERTS * F_TILES], b1_raw[:], ident[0:EXPERTS * F_TILES, 0:EXPERTS * F_TILES]).then_inc(b1_full, 1)
        pe.wait_ge(masks_ready, MASKS)

        def count(bank, flags):
            width = flags.shape[2] * SUMMED
            for k in range(ALL_TILES // SUMMED):
                last = pe.matmul(made_ps[:, bank, 0:width], ones16[:],
                                 flags[:, k * SUMMED:(k + 1) * SUMMED, :].rearrange("p t m -> p (t m)"),
                                 start=k == 0, stop=k == ALL_TILES // SUMMED - 1)
            return last

        def before(bank, flags):
            out = made_ps[:, bank, 0:ALL_TILES * EXPERTS]
            pe.matmul(out, earlier[:], flags[:].rearrange("p t e -> p (t e)"), start=True, stop=False)
            for t in range(ALL_TILES - 1):
                rest = ALL_TILES - 1 - t
                last = pe.matmul(out[:, (t + 1) * EXPERTS:], ones16[:],
                                 flags[:, t:t + 1, :].to_broadcast([P, rest, EXPERTS]),
                                 start=False, stop=t == ALL_TILES - 2)
            return last

        with pe.Fori(0, ROUNDS // 2) as i:
            for u in range(2):
                pe.wait_ge(reached_ready, 2 * i + u + 1)
                count(0, reached).then_inc(counted, 1)
        pe.wait_ge(above_ready, 1)
        count(0, above).then_inc(above_counted, 1)
        pe.wait_ge(tied_ready, 1)
        before(1, tied).then_inc(tied_before, 1)
        pe.wait_ge(kept_ready, 1)
        before(0, kept).then_inc(kept_before, 1)
        pe.wait_ge(slots_ready, 1)

        def transpose_rows(side, round_, first):
            pe.wait_ge(rows_loaded[side], 16 * round_)
            if first:
                pe.wait_ge(b1_ready, 1)
            for r in range(ROWS):
                for k in range(2):
                    last = pe.transpose(rowsT_ps[0:HALF, k, r * BLOCK_P:(r + 1) * BLOCK_P],
                                        rows[side][:, r, k * HALF:(k + 1) * HALF], ident[0:BLOCK_P, 0:BLOCK_P])
            last.then_inc(rows_full, 1)

        def emit(i, u, last):
            b = i * STEP + u
            side = u // PER_EXPERT
            if isinstance(i, int) and b == 0:
                transpose_rows(0, 1, True)
            pe.wait_ge(rows_half0, b + 1)
            pe.wait_ge(rows_half1, b + 1)
            if u % PER_EXPERT == 0:
                pe.wait_ge(weights_loaded[side], 48 * (i + 1))
            for f in range(F_TILES):
                G = b * F_TILES + f
                wait(pe, gelu_done, G - HB + 1)
                for k in range(2):
                    ins = pe.matmul(hid_ps[:, (u * F_TILES + f) % HB, 0:BLOCK], w1[side][:, k, f * P:(f + 1) * P],
                                    rowsT[:, k, :], start=k == 0, stop=k == 1)
                ins.then_inc(hid_full, 1)
            if not last:
                transpose_rows((u + 1) % ROWS_RING, i + (u + 1) // ROWS_RING + 1, False)
            wait(pe, sum_ready, 2 * b)
            pe.wait_ge(gelu_done, (b + 1) * F_TILES)
            for r in range(ROWS):
                for f in range(F_TILES):
                    ins = pe.matmul(made_ps[0:BLOCK_P, r // 2, (r % 2) * D:(r % 2 + 1) * D],
                                    hid[:, f, r * BLOCK_P:(r + 1) * BLOCK_P], w2[side][:, f, :],
                                    start=r % 2 == 0 and f == 0, stop=r % 2 == 1 and f == F_TILES - 1)
                if r % 2 == 1:
                    ins.then_inc(made_full, 1)

        program(pe, emit)


def early_fusion_block(nc, x, txt, freq, W, Wq, Wk, Wv, Wproj, switch_w, switch_b, w1, b1, w2, b2, cos, sin, token, out):
    io = dict(x=x, txt=txt, freq=freq, W=W, Wq=Wq, Wk=Wk, Wv=Wv, Wproj=Wproj, switch_w=switch_w, switch_b=switch_b,
              w1=w1, b1=b1, w2=w2, b2=b2, cos=cos, sin=sin, token=token, out=out)
    io["h_dram"] = nc.dram_tensor("h_dram", [P, ALL_TILES, D], F32, kind="Internal").ap()
    io["z2_dram"] = nc.dram_tensor("z2_dram", [P, ALL_TILES, D], F32, kind="Internal").ap()
    io["xs_dram"] = nc.dram_tensor("xs_dram", [SLOTS, WIDE], F32, kind="Internal").ap()
    with ExitStack() as outer:
        def sb(name, shape):
            return outer.enter_context(nc.sbuf_tensor(name, shape, F32))
        keep = dict(ident=sb("ident", [P, P]), logits=sb("logits", [P, ALL_TILES, EXPERTS]),
                    half_pi=sb("half_pi", [P, 1]), erf_h1=sb("erf_h1", [P, 1]), erf_h2=sb("erf_h2", [P, 1]))
        with ExitStack() as ctx:
            transformer_block(nc, ctx, io, keep)
        with ExitStack() as ctx:
            experts(nc, ctx, io, keep)


def kernel(x, txt, L0_tok_freq_bands, L0_tok_W, L0_attn_Wq, L0_attn_Wk, L0_attn_Wv, L0_attn_Wproj, L0_ffn_switch_w,
           L0_ffn_switch_b, L0_ffn_w1, L0_ffn_b1, L0_ffn_w2, L0_ffn_b2):
    import numpy as _np
    import concourse.bacc as _bacc
    from concourse import mybir as _mybir
    from concourse.bass_utils import run_bass_kernel_spmd as _run

    half = HD // 2
    rate = _np.float32(1.0) / _np.float32(10000.0) ** (_np.arange(half, dtype=_np.float32) / _np.float32(half))
    angle = _np.arange(SEQ, dtype=_np.float32)[:, None] * rate[None, :]
    c, s = _np.cos(angle), _np.sin(angle)

    def tiled(a):
        return a.reshape(TILES, P, HD).transpose(1, 0, 2)

    arrays = [("x", x.reshape(BATCHES, IMG, CH)), ("txt", txt), ("freq", L0_tok_freq_bands), ("W", L0_tok_W),
              ("Wq", L0_attn_Wq), ("Wk", L0_attn_Wk), ("Wv", L0_attn_Wv), ("Wproj", L0_attn_Wproj),
              ("switch_w", L0_ffn_switch_w), ("switch_b", L0_ffn_switch_b),
              ("w1", L0_ffn_w1), ("b1", L0_ffn_b1), ("w2", L0_ffn_w2), ("b2", L0_ffn_b2),
              ("cos", tiled(_np.repeat(c, 2, axis=1))), ("sin", tiled(_np.stack([-s, s], axis=-1))),
              ("token", _np.arange(TOKENS, dtype=_np.int32).reshape(ALL_TILES, P).T)]
    nc = _bacc.Bacc("TRN2", target_bir_lowering=False, num_devices=1)
    feed, args = {}, []
    for name, a in arrays:
        a = _np.ascontiguousarray(a)
        feed[f"in_{name}"] = a
        args.append(nc.dram_tensor(f"in_{name}", a.shape, _mybir.dt.from_np(a.dtype), kind="ExternalInput").ap())
    args.append(nc.dram_tensor("out_0", (BATCHES, SEQ, D), _mybir.dt.float32, kind="ExternalOutput").ap())
    early_fusion_block(nc, *args)
    r = _run(nc, [feed], core_ids=[0])
    return r.results[0]["out_0"]
```

```python
from contextlib import ExitStack

import concourse.bass as bass
from concourse import mybir

F32, F16, I32, U32 = mybir.dt.float32, mybir.dt.float16, mybir.dt.int32, mybir.dt.uint32
ALU = mybir.AluOpType
ACT = mybir.ActivationFunctionType
AX_X = mybir.AxisListType.X

P = 128
BATCHES, IMG, TXT, D = 8, 512, 128, 192
SEQ = IMG + TXT
TILES = SEQ // P
IMG_TILES = IMG // P
ALL_TILES = BATCHES * TILES
CH = 3 * D
BANDS = 6
FEATURES = CH * 2 * BANDS
HEADS, HD = 12, 16
HALF = D // 2
EXPERTS, HIDDEN = 8, 768
TOKENS = BATCHES * SEQ
CAPACITY = int(1.25 * TOKENS / EXPERTS)
SLOTS = EXPERTS * CAPACITY
ROWS = 4
BLOCK = 400
BLOCK_P = BLOCK // ROWS
PER_EXPERT = CAPACITY // BLOCK
BLOCKS = EXPERTS * PER_EXPERT
F_TILES = HIDDEN // P
AT_H, AT_PROB, AT_TOKEN, WIDE = D, 2 * D, 2 * D + 1, 2 * D + 2
ROWS_RING = 4
W_SCALE = 256.0
REST = D - P
LEVELS = 3
ROUNDS = 14
TWO_PI = 6.283185307179586
HALF_PI = 1.5707963267948966
ROUND = 1.5 * 2.0 ** 23

SUB = 3
CHUNKS = 9
CHUNK = SUB * IMG
RING = 3
X_BLOCKS = 5

PIECES = [(128 * t, t, 128 * t, 128) for t in range(TILES)] + [
    (640, 0, 128, 384), (1024, 1, 256, 384), (1408, 0, 512, 128), (1536, 2, 384, 256), (1792, 3, 512, 128)]
TRI = 1920
HALVES = [(0, 1024), (1024, TRI)]
A_RING = 6
PAIR_RING = 3
GROUP = 4

ERF_C = 3.224444918595032e-05
ERF_H1, ERF_K1 = -14.605611022253761, 152.92954269725462
ERF_H2, ERF_K2 = 8.168209826141505, 28.825868754761615


def chunk_block(c):
    return c // 2


class Fills:

    def __init__(self, half, n):
        self.half, self.n = half, n
        self.bank = n % 2
        self.total = half * 2 + n

    def of(self, bank):
        return self.half + (self.n + 1 - bank) // 2


FILLS = dict(XT=1, ZT=1, QK=1, V=1, TPQ=1, TPK=1, YT=1, PT=1, PJ=1, Z2T=1, RT=1, AV=1)
PIECES_OF_CHUNK = 2 * SUB


def walk(steps, half, odd, batch):
    n = odd
    for name, off, *args in steps:
        yield name, batch + off, Fills(half, n), args
        n += FILLS.get(name, 0)


def fills(steps):
    return sum(FILLS.get(s[0], 0) for s in steps)


SPAN = 3 * HEADS
HEAD_AT = dict(E1=0, E2=1, S=-1.05, E3=1.85)
PAIR_AT = {0: -2, 1: 1.7, 2: 0.2, 3: 10.2, 4: 15.4, 5: 23}
SUM_AT = {0: (15, 16), 1: (28.7, 28.9), 2: (39.1, 40.98)}
TURN_AT = {0: (18.1, 21.5), 1: (33.6, 33.87), 2: (41.85, 43.11)}
TILE_AT = dict(ZT=(-14, -13.76, -12.6), QK=(-11.7, -11.6, -9.94, -9.36, -8.9), ROPE=(-11, -10.8, -9.78,
               -8.66, -8.45), V=(6, 6.94, 7.88, 8.7, 8.92), PT=(46, 47, 47), PJ=(48.7, 49.4, 50.1), Z2T=(51.8, 54.4, 56.2))
ONCE_AT = dict(LN1=-15.4, SPLIT=-7.1, COPYH=16.1, LN2=51, RT=56.3)
CHUNK_SPAN = SPAN / CHUNKS
BY_DVE = dict(XT=(1, 0, 0, 0, 1), ZT=(0, 0, 0), PT=(0, 0, 0), Z2T=(1, 0, 0), QK=(1, 0, 0, 1, 1), V=(0, 0,
              0, 1, 1), TPQ=(1, 0, 0, 1, 0, 0), TPK=(1, 0, 1, 1, 1, 1))
CHUNK_AT = dict(XT=-10.1, YN=-8.4, AB=-5.7, TR=-2.2, TC=-3.3, MM=-0.7)
CHUNKS_BEFORE = CHUNKS + 4


def timetable():
    at = []

    def add(time, name, batch, *args):
        at.append((time, len(at), (name, batch, *args)))

    for k in range(BATCHES * CHUNKS):
        batch, c = divmod(k, CHUNKS)
        start = (k - CHUNKS_BEFORE) * CHUNK_SPAN
        if c % 2 == 0:
            add(start + CHUNK_AT["XT"], "XT", batch, c // 2)
        for name in ("YN", "AB", "TR", "TC"):
            add(start + CHUNK_AT[name], name, batch, c)
        for m in range(PIECES_OF_CHUNK):
            add(start + CHUNK_AT["MM"] + m * CHUNK_SPAN / PIECES_OF_CHUNK, "MM", batch, c, m)
        if c == CHUNKS - 1:
            add(start + CHUNK_AT["MM"] + (PIECES_OF_CHUNK - 1) * CHUNK_SPAN / PIECES_OF_CHUNK, "HEVAC", batch)
    for batch in range(BATCHES):
        start = batch * SPAN
        for h in range(HEADS):
            for name in ("E1", "E2", "S", "E3"):
                add(start + 3 * h + HEAD_AT[name], name, batch, h)
        for hp, time in PAIR_AT.items():
            add(start + time, "TPQ", batch, hp)
            add(start + time, "TPK", batch, hp)
        for name, table in (("AV", SUM_AT), ("YT", TURN_AT)):
            for g, times in table.items():
                for part, time in enumerate(times):
                    add(start + time, name, batch, g, part)
        for name, times in TILE_AT.items():
            for k, time in enumerate(times):
                add(start + time, name, batch, k)
        for name, time in ONCE_AT.items():
            add(start + time, name, batch)
    add(BATCHES * SPAN, "ELAST", BATCHES - 1)
    return sorted(at)


def steps_between(table, first, last, batch):
    return [(name, b - batch, *args) for time, _, (name, b, *args) in table if first <= time < last]


def transformer_block(nc, ctx, io, keep):
    def sb(name, shape, dt=F32):
        return ctx.enter_context(nc.sbuf_tensor(name, shape, dt))

    def sem(name):
        return ctx.enter_context(nc.semaphore(name))

    ident, logits = keep["ident"], keep["logits"]
    xraw = sb("xraw", [P, IMG_TILES, P])
    xT = sb("xT", [P, IMG])
    turns = [sb(f"turns{i}", [P, CHUNK]) for i in range(RING)]
    whole = [sb(f"whole{i}", [P, CHUNK]) for i in range(RING)]
    WT = sb("WT", [P, CHUNKS * SUB * 2, D])
    freq = sb("freq", [P, BANDS + SUB])
    hacc = sb("hacc", [P, TILES, D])
    h = sb("h", [P, TILES, D])
    z = sb("z", [P, TILES, D])
    stats = sb("stats", [P, TILES, 6])
    moments = sb("moments", [P, TILES, 2])
    var_eps = sb("var_eps", [P, TILES])
    rstd = sb("rstd", [P, TILES])
    gate = sb("gate", [P, 1])
    minus_half = sb("minus_half", [P, TILES])
    zT = sb("zT", [HALF, 2, SEQ])
    qk = sb("qk", [P, TILES, 2 * D])
    v32 = sb("v32", [P, TILES, HEADS, 32])
    split = sb("split", [P, TILES, 2 * HEADS, 64], F16)
    qT = sb("qT", [P, PAIR_RING, SEQ], F16)
    kT = sb("kT", [P, PAIR_RING, SEQ], F16)
    work = sb("work", [P, max((A_RING + 1) * TRI, 2 * FEATURES)])
    yraw = sb("yraw", [P, SEQ])
    y_sb = sb("y_sb", [P, TILES, D])
    rope_a = sb("rope_a", [P, 2 * D])
    rope_b = sb("rope_b", [P, 2 * D])
    den = sb("den", [P, TILES * GROUP])
    rden = sb("rden", [P, TILES * GROUP])
    ident16 = sb("ident16", [P, P], F16)
    causal = sb("causal", [P, P])
    rope_cos = sb("rope_cos", [P, TILES, HD])
    rope_sin = sb("rope_sin", [P, TILES, HD])
    wqkvT = sb("wqkvT", [HALF, 2, 3 * D])
    wpT = sb("wpT", [HALF, 2, D])
    switch_w = sb("switch_w", [HALF, 2, EXPERTS])
    switch_b = sb("switch_b", [P, EXPERTS])

    weight = [work[:, s * TRI:(s + 1) * TRI] for s in range(A_RING)]
    factor = work[:, A_RING * TRI:(A_RING + 1) * TRI]
    w_raw = work[0:HALF, 0:2 * FEATURES].rearrange("p (o f) -> p o f", o=2)
    w_pairs = split[0:HALF].rearrange("p t h i -> p (t h i)").bitcast(F32)[:, 0:2 * 2 * SUB * P]\
        .rearrange("p (o s i n) -> p o s i n", o=2, s=2, i=SUB)
    attn_raw = [hacc[0:HALF, 0:2, :], hacc[0:HALF, 2:4, :], z[0:HALF, 0:2, :], z[0:HALF, 2:4, :]]

    acc = ctx.enter_context(nc.psum_tensor("acc", [P, 2, 512], F32))
    score = ctx.enter_context(nc.psum_tensor("score", [P, 4 * 512], F32))
    shared = [ctx.enter_context(nc.psum_tensor(f"shared{i}", [P, 512], F32)) for i in range(2)]

    w_loaded, freq_loaded, small_loaded, x_loaded, txt_loaded = (
        sem("w_loaded"), sem("freq_loaded"), sem("small_loaded"), sem("x_loaded"), sem("txt_loaded"))
    h_stored, z2_stored, fill_ready, slots_filled = sem("h_stored"), sem("z2_stored"), sem("fill_ready"), sem("slots_filled")
    zero_ready, const_ready, pairs_ready, ones_ready = sem("zero_ready"), sem("const_ready"), sem("pairs_ready"), sem("ones_ready")
    wt_full, wt_act, wt_dve, at_full, at_free = sem("wt_full"), sem("wt_act"), sem("wt_dve"), sem("at_full"), sem("at_free")
    misc_full, misc_free = sem("misc_full"), [sem("misc_free0"), sem("misc_free1")]
    turns_made, turns_ready, frac_ready, abs_ready, sine_ready, cosine_ready, chunk_used = (
        sem("turns_made"), sem("turns_ready"), sem("frac_ready"), sem("abs_ready"), sem("sine_ready"), sem("cosine_ready"), sem("chunk_used"))
    hacc_ready, h_copied = sem("hacc_ready"), sem("h_copied")
    ln_stats, ln_aggr, ln_var, ln_rstd = sem("ln_stats"), sem("ln_aggr"), sem("ln_var"), sem("ln_rstd")
    z_ready, z2_ready = sem("z_ready"), sem("z2_ready")
    rope_parts, rope_done, hi_ready, lo_ready = sem("rope_parts"), sem("rope_done"), sem("hi_ready"), sem("lo_ready")
    score_full, square_done, factor_ready, y_done, y2_done = (
        sem("score_full"), sem("square_done"), sem("factor_ready"), sem("y_done"), sem("y2_done"))
    tanh_done, weight_ready, den_step = sem("tanh_done"), sem("weight_ready"), sem("den_step")

    table = timetable()
    spans = [steps_between(table, b * SPAN, (b + 1) * SPAN, b) for b in range(BATCHES)]
    begin, first, looped, before_last, last = (
        steps_between(table, -4 * SPAN, 0, 0), spans[0], spans[1], spans[-2], spans[-1])
    end = steps_between(table, BATCHES * SPAN, (BATCHES + 2) * SPAN, BATCHES - 1)
    LOOPS = BATCHES - 3
    assert all(span == looped for span in spans[1:1 + LOOPS])
    cut = [step[0] for step in begin].index("MM")
    opening, begin = begin[:cut], begin[cut:]
    f_open = fills(opening)
    f_begin = f_open + fills(begin)
    f_first = f_begin + fills(first)
    f_loop = fills(looped)
    assert f_loop % 2 == 0
    f_before_last = f_first + LOOPS * f_loop
    f_last = f_before_last + fills(before_last)
    f_end = f_last + fills(last)

    def run(emit, steps, half, odd, batch):
        for name, n, f, args in walk(steps, half, odd, batch):
            emit(name, n, f, args)

    def program(eng, emit):
        run(emit, begin, *divmod(f_open, 2), 0)
        run(emit, first, *divmod(f_begin, 2), 0)
        with eng.Fori(1, 1 + LOOPS) as b:
            run(emit, looped, (b - 1) * (f_loop // 2) + f_first // 2, f_first % 2, b)
        run(emit, before_last, *divmod(f_before_last, 2), BATCHES - 2)
        run(emit, last, *divmod(f_last, 2), BATCHES - 1)
        run(emit, end, *divmod(f_end, 2), BATCHES - 1)

    def moved(name, bank, k):
        if name == "XT":
            return xT[:], bank[:]
        if name == "QK":
            return qk[:, k, :], bank[:, 0:2 * D]
        if name == "V":
            return v32[:, k, :, 0:HD], bank[:, 0:D].rearrange("p (h i) -> p h i", i=HD)
        if name in ("TPQ", "TPK"):
            return (qT if name == "TPQ" else kT)[:, k % PAIR_RING, :], bank[:].bitcast(F16)[:, 0:SEQ]
        w = min(2, TILES - 2 * k)
        return (zT[:, :, 2 * k * P:(2 * k + w) * P].rearrange("p k (t n) -> p t k n", n=P),
                bank[0:HALF, 0:w * 2 * P].rearrange("p (t k n) -> p t k n", t=w, k=2))

    def wait_free(eng, f):
        for bank in range(2):
            wait(eng, misc_free[bank], f.of(bank))

    def wait(eng, s, value):
        if isinstance(value, int) and value <= 0:
            return
        eng.wait_ge(s, value)

    def norms_before(name, n):
        if name == "LN1":
            return 0 if isinstance(n, int) and n == 0 else n * 2 - 1
        return n * 2 + 1 if isinstance(n, int) and n == BATCHES - 1 else n * 2 + 2

    W_FILLS = CHUNKS * SUB
    block = ctx.enter_context(nc.Block())

    @block.sync
    def _(sp):
        def load_x(n, q):
            src = io["x"][bass.ds(n, 1)].rearrange("o (t p) c -> p (o t) c", p=P)
            if q < X_BLOCKS - 1:
                sp.dma_start(xraw[:], src[:, :, q * P:(q + 1) * P]).then_inc(x_loaded, 32)
            else:
                for side in range(2):
                    sp.dma_start(xraw[:, :, side * 64:(side + 1) * 64], src[:, :, CH - 64:CH]).then_inc(x_loaded, 16)

        def emit(name, n, f, args):
            if name == "XT":
                q = (args[0] + 1) % X_BLOCKS
                if q == 0 and isinstance(n, int) and n == BATCHES - 1:
                    return
                sp.wait_ge(misc_full, f.total + 1)
                load_x(n + (q == 0), q)
                if isinstance(n, int) and n == 0:
                    sp.wait_ge(fill_ready, 1)
                    sp.dma_start(io["xs_dram"].rearrange("(q p k n) d -> q p k (n d)", q=X_BLOCKS, p=P, n=2)[args[0]],
                                 h[:].rearrange("p t d -> p (t d)")[:, None, 0:2 * WIDE]
                                 .to_broadcast([P, SLOTS // P // 2 // X_BLOCKS, 2 * WIDE])).then_inc(slots_filled, 16)
            elif name == "COPYH":
                if isinstance(n, int) and n == BATCHES - 1:
                    return
                sp.wait_ge(h_copied, n + 1)
                sp.dma_start(hacc[:, IMG_TILES, :], io["txt"][bass.ds(n + 1, 1)].rearrange("o p d -> p (o d)"))\
                    .then_inc(txt_loaded, 16)
            elif name == "LN2":
                wait_free(sp, f)
                sp.dma_start(io["h_dram"][:, bass.ds(n * TILES, TILES), :], h[:]).then_inc(h_stored, 16)
                sp.wait_ge(z2_ready, n + 1)
                sp.dma_start(io["z2_dram"][:, bass.ds(n * TILES, TILES), :], z[:]).then_inc(z2_stored, 16)

        with nc.allow_non_contiguous_dma(reason="a few words of frequencies"):
            sp.dma_start(freq[:, 0:BANDS], io["freq"][None, :].to_broadcast([P, BANDS])).then_inc(freq_loaded, 16)
            for side in range(2):
                sp.dma_start(freq[64 * side:64 * side + 64, BANDS:BANDS + SUB],
                             io["freq"].rearrange("(i s) -> s i", s=2)[side:side + 1, :].to_broadcast([64, SUB]))\
                    .then_inc(freq_loaded, 16)
        load_x(0, 0)
        sp.dma_start(w_raw, io["W"].rearrange("(o p) f -> p o f", p=HALF)).then_inc(w_loaded, 16)
        run(emit, opening, 0, 0, 0)
        for raw, name in zip(attn_raw, ("Wq", "Wk", "Wv", "Wproj")):
            sp.dma_start(raw, io[name].rearrange("(o p) f -> p o f", p=HALF)).then_inc(small_loaded, 16)
        sp.dma_start(rope_cos[:], io["cos"]).then_inc(small_loaded, 16)
        sp.dma_start(rope_sin[:], io["sin"]).then_inc(small_loaded, 16)
        sp.dma_start(switch_w[:], io["switch_w"].rearrange("(k p) e -> p k e", p=HALF)).then_inc(small_loaded, 16)
        sp.dma_start(switch_b[:], io["switch_b"][None, :].to_broadcast([P, EXPERTS])).then_inc(small_loaded, 16)

        sp.wait_ge(at_free, 4)
        sp.dma_start(hacc[:, IMG_TILES, :], io["txt"][0]).then_inc(txt_loaded, 16)

        program(sp, emit)
        sp.wait_ge(h_stored, 16 * BATCHES)
        sp.wait_ge(z2_stored, 16 * BATCHES)

    @block.gpsimd
    def _(pool):
        pool.memset(ident[:], 0.0).then_inc(zero_ready, 1)
        pool.memset(ident16[:], 0.0).then_inc(zero_ready, 1)
        pool.memset(causal[:], 1.0).then_inc(zero_ready, 1)
        pool.memset(minus_half[:], -0.5).then_inc(const_ready, 1)
        pool.wait_ge(zero_ready, 3)
        for m in (ident, ident16):
            pool.affine_select(out=m[:], in_=m[:], compare_op=ALU.not_equal, fill=1.0, base=0,
                               pattern=[[-1, P]], channel_multiplier=1).then_inc(const_ready, 1)
        pool.memset(h[:], 1.0).then_inc(fill_ready, 1)
        pool.affine_select(out=causal[:], in_=causal[:], compare_op=ALU.is_ge, fill=0.0, base=0,
                           pattern=[[1, P]], channel_multiplier=-1).then_inc(const_ready, 1)

        def emit(name, n, f, args):
            if name == "YN":
                c, = args
                pool.wait_ge(turns_ready, n * CHUNKS + c + 1)
                pool.tensor_tensor(turns[c % RING][:], turns[c % RING][:], whole[c % RING][:],
                                   ALU.subtract).then_inc(frac_ready, 1)
            elif name in ("LN1", "LN2"):
                m = norms_before(name, n)
                pool.wait_ge(ln_var, m + 1)
                pool.tensor_tensor(rstd[:], var_eps[:], minus_half[:], ALU.pow).then_inc(ln_rstd, 1)
            elif name == "ROPE":
                t, = args
                done = n * TILES + t
                wait_free(pool, f)
                wait(pool, rope_done, done)
                shape = [P, 2 * HEADS, HD]
                q3, a3, b3 = (m.rearrange("p (h i) -> p h i", i=HD) for m in (qk[:, t, :], rope_a[:], rope_b[:]))
                pool.tensor_tensor(a3, q3, rope_cos[:, t, None, :].to_broadcast(shape), ALU.mult).then_inc(rope_parts, 1)
                half = [P, 2 * HEADS, HD // 2]
                for e in range(2):
                    pool.tensor_tensor(b3[:, :, e::2], q3[:, :, 1 - e::2],
                                       rope_sin[:, t, None, e::2].to_broadcast(half), ALU.mult).then_inc(rope_parts, 1)
                pool.wait_ge(rope_parts, 3 * done + 3)
                pool.tensor_tensor(qk[:, t, :], rope_a[:], rope_b[:], ALU.add).then_inc(rope_done, 1)
            elif name == "SPLIT":
                pool.wait_ge(hi_ready, 2 * n + 2)
                a4 = qk[:].rearrange("p t (h i) -> p t h i", i=HD)
                for w, at in ((0, 32), (1, 16)):
                    hs = slice(w * HEADS, (w + 1) * HEADS)
                    pool.tensor_tensor(split[:, :, hs, at:at + HD], a4[:, :, hs, :], split[:, :, hs, 0:HD],
                                       ALU.subtract).then_inc(lo_ready, 1)

        run(emit, opening, 0, 0, 0)
        program(pool, emit)

    @block.scalar
    def _(act):
        act.wait_ge(const_ready, 1)
        act.activation(den[:, 0:1], minus_half[:, 0:1], ACT.Silu).then_inc(ones_ready, 1)
        act.wait_ge(ones_ready, 5)

        def lay_out_weights():
            for k in range(0, W_FILLS, 2):
                act.wait_ge(wt_full, k + 1)
                act.activation(WT[:, 2 * k:2 * k + 2, :], score[:, (k % 4) * 512:(k % 4) * 512 + 2 * D], ACT.Copy).then_inc(wt_act, 1)

            act.wait_ge(ones_ready, 7)

        def emit(name, n, f, args):
            misc = shared[f.bank]
            if name in BY_DVE:
                if not BY_DVE[name][args[0]]:
                    if name == "XT":
                        wait(act, turns_ready, n * CHUNKS + 2 * args[0])
                    if name == "QK":
                        wait(act, lo_ready, 2 * n)
                    act.wait_ge(misc_full, f.total + 1)
                    act.activation(*moved(name, misc, args[0]), ACT.Copy).then_inc(misc_free[f.bank], 1)
            elif name == "TR":
                c, = args
                act.wait_ge(abs_ready, n * CHUNKS + c + 1)
                act.activation(turns[c % RING][:], turns[c % RING][:], ACT.Sin, scale=TWO_PI).then_inc(sine_ready, 1)
            elif name == "TC":
                c, = args
                act.wait_ge(abs_ready, n * CHUNKS + c + 1)
                act.activation(whole[c % RING][:], whole[c % RING][:], ACT.Sin, scale=-TWO_PI,
                               bias=keep["half_pi"][:, 0:1]).then_inc(cosine_ready, 1)
            elif name == "E1":
                i, = args
                H = n * HEADS + i
                A, B = weight[i % A_RING], factor
                for j, (a, b) in enumerate(HALVES):
                    act.wait_ge(score_full, 2 * H + j + 1)
                    act.activation(A[:, a:b], score[:, a:b], ACT.Square, scale=HD ** -0.5).then_inc(square_done, 1)
                wait(act, y2_done, H)
                for j, (a, b) in enumerate(HALVES):
                    act.wait_ge(square_done, 2 * H + j + 1)
                    act.activation(B[:, a:b], A[:, a:b], ACT.Square, bias=keep["erf_h1"][:, 0:1]).then_inc(factor_ready, 1)
            elif name == "E2":
                i, = args
                A = weight[i % A_RING]
                act.wait_ge(factor_ready, 3 * (n * HEADS + i) + 2)
                act.activation(A, A, ACT.Square, bias=keep["erf_h2"][:, 0:1]).then_inc(factor_ready, 1)
                if not (isinstance(n, int) and n == 0 and i == 0):
                    tanh(n, i - 1)
            elif name == "ELAST":
                tanh(n, HEADS - 1)
            elif name == "AV":
                g, part = args
                a, w = (0, 512) if part == 0 else (512, SEQ - 512)
                act.wait_ge(misc_full, f.total + 1)
                act.activation(yraw[:, a:a + w], misc[:, 0:w], ACT.Copy).then_inc(misc_free[f.bank], 1)

        def tanh(n, i):
            act.wait_ge(y2_done, n * HEADS + i + 1)
            A = weight[i % A_RING]
            act.activation(A, A, ACT.Tanh, scale=ERF_C * HD ** -0.5).then_inc(tanh_done, 1)

        run(emit, opening, 0, 0, 0)
        lay_out_weights()
        program(act, emit)

    @block.vector
    def _(dve):
        dve.memset(keep["half_pi"][:], HALF_PI).then_inc(ones_ready, 1)
        dve.memset(keep["erf_h1"][:], ERF_H1).then_inc(ones_ready, 1)
        dve.memset(keep["erf_h2"][:], ERF_H2).then_inc(ones_ready, 1)
        dve.memset(v32[:], 0.0).then_inc(ones_ready, 1)
        dve.wait_ge(freq_loaded, 48)

        def lay_out_weights():
            dve.wait_ge(ones_ready, 5)
            dve.memset(v32[:, :, :, HD:HD + 1], 1.0).then_inc(ones_ready, 1)
            dve.wait_ge(w_loaded, 16)
            for o in range(2):
                for s in range(2):
                    for i in range(SUB):
                        src = w_raw[:, o, (CH - 64) * 12:].rearrange("p (j k) -> p k j", k=12)[:, s * BANDS + 2 * i:s * BANDS + 2 * i + 2, :]
                        last = dve.tensor_copy(w_pairs[:, o, s, i, :].rearrange("p (k j) -> p k j", k=2), src)
            last.then_inc(pairs_ready, 1)
            for k in range(1, W_FILLS, 2):
                dve.wait_ge(wt_full, k + 1)
                dve.tensor_copy(WT[:, 2 * k:2 * k + 2, :],
                                score[:, (k % 4) * 512:(k % 4) * 512 + 2 * D].rearrange("p (t n) -> p t n", t=2)).then_inc(wt_dve, 1)
            dve.wait_ge(wt_full, W_FILLS)
            dve.memset(split[:], 0.0).then_inc(ones_ready, 1)
            for m in range(4):
                dve.wait_ge(at_full, m + 1)
                src = shared[0][0:HALF, 0:2 * D].rearrange("p (k n) -> p k n", k=2)
                dst = wqkvT[:, :, m * D:(m + 1) * D] if m < 3 else wpT[:]
                dve.tensor_copy(dst, src).then_inc(at_free, 1)
            dve.wait_ge(small_loaded, 16 * 8)
            dve.wait_ge(const_ready, 4)

        def norm(n, m, src, dst, done):
            for t in range(TILES):
                dve.bn_stats(stats[:, t, :], src[:, t, :]).then_inc(ln_stats, 1)
            dve.wait_ge(ln_stats, TILES * m + TILES)
            dve.memset(gate[:], 0.0)
            for t in range(TILES):
                dve.bn_aggr(moments[:, t, :], stats[:, t, :]).then_inc(ln_aggr, 1)
            dve.wait_ge(ln_aggr, TILES * m + TILES)
            dve.tensor_scalar(var_eps[:], moments[:, :, 1], 1e-5, None, ALU.add).then_inc(ln_var, 1)
            dve.wait_ge(ln_rstd, m + 1)
            for t in range(TILES):
                last = dve.tensor_scalar(dst[:, t, :], src[:, t, :], moments[:, t, 0:1], rstd[:, t:t + 1],
                                         ALU.subtract, ALU.mult)
            last.then_inc(done, 1)

        def emit(name, n, f, args):
            misc, free = shared[f.bank], misc_free[f.bank]
            if name in BY_DVE:
                if BY_DVE[name][args[0]]:
                    if name == "XT":
                        wait(dve, turns_ready, n * CHUNKS + 2 * args[0])
                    if name == "QK":
                        wait(dve, lo_ready, 2 * n)
                    dve.wait_ge(misc_full, f.total + 1)
                    dve.tensor_copy(*moved(name, misc, args[0])).then_inc(free, 1)
            elif name == "YN":
                c, = args
                K = n * CHUNKS + c
                if c % 2 == 0:
                    wait_free(dve, f)
                wait(dve, chunk_used, K - RING + 1)
                for i in range(SUB):
                    col = freq[:, BANDS + i:BANDS + i + 1] if c == CHUNKS - 1 else freq[:, SUB * (c % 2) + i:SUB * (c % 2) + i + 1]
                    src = xT[:]
                    cols = slice(i * IMG, (i + 1) * IMG)
                    last = dve.tensor_scalar(turns[c % RING][:, cols], src, col, None, ALU.mult)
                last.then_inc(turns_made, 1)
                dve.wait_ge(turns_made, K + 1)
                dve.tensor_scalar(whole[c % RING][:], turns[c % RING][:], ROUND, ROUND, ALU.add, ALU.subtract).then_inc(turns_ready, 1)
            elif name == "AB":
                c, = args
                dve.wait_ge(frac_ready, n * CHUNKS + c + 1)
                dve.tensor_scalar(whole[c % RING][:].bitcast(I32), turns[c % RING][:].bitcast(I32), 0x7FFFFFFF, None,
                                  ALU.bitwise_and).then_inc(abs_ready, 1)
            elif name == "HEVAC":
                dve.wait_ge(chunk_used, (n + 1) * CHUNKS)
                wait(dve, h_copied, n)
                for j in range(2):
                    last = dve.tensor_copy(hacc[:, 2 * j:2 * j + 2, :], acc[:, j, 0:2 * D].rearrange("p (t n) -> p t n", t=2))
                last.then_inc(hacc_ready, 1)
            elif name == "LN1":
                dve.wait_ge(txt_loaded, 16 * (n + 1))
                dve.wait_ge(hacc_ready, n + 1)
                if not (isinstance(n, int) and n <= 1):
                    dve.wait_ge(z2_stored, 16 * (n - 1))
                norm(n, norms_before(name, n), hacc, z, z_ready)
            elif name == "LN2":
                wait_free(dve, f)
                if isinstance(n, int) and n == BATCHES - 1:
                    dve.wait_ge(z2_stored, 16 * n)
                norm(n, norms_before(name, n), h, z, z2_ready)
            elif name == "SPLIT":
                dve.wait_ge(rope_done, (n + 1) * TILES)
                dve.wait_ge(misc_full, f.total)
                a4 = qk[:].rearrange("p t (h i) -> p t h i", i=HD)
                for w in range(2):
                    hs = slice(w * HEADS, (w + 1) * HEADS)
                    for e in range(2):
                        at = 16 * e if w == 0 else 32 * e
                        last = dve.tensor_copy(split[:, :, hs, at:at + HD], a4[:, :, hs, :])
                    last.then_inc(hi_ready, 1)
            elif name == "E2":
                i, = args
                H = n * HEADS + i
                B = factor
                for j, (a, b) in enumerate(HALVES):
                    dve.wait_ge(factor_ready, 3 * H + j + 1)
                    dve.scalar_tensor_tensor(B[:, a:b], B[:, a:b], ERF_K1, score[:, a:b], ALU.add, ALU.mult).then_inc(y_done, 1)
            elif name == "E3":
                i, = args
                H = n * HEADS + i
                A, B = weight[i % A_RING], factor
                dve.wait_ge(factor_ready, 3 * H + 3)
                dve.wait_ge(y_done, 2 * H + 2)
                dve.scalar_tensor_tensor(A, A, ERF_K2, B, ALU.add, ALU.mult).then_inc(y2_done, 1)
                if not (isinstance(n, int) and n == 0 and i == 0):
                    weights(n, i - 1)
            elif name == "ELAST":
                weights(n, HEADS - 1)
            elif name == "YT":
                g, part = args
                w = 4 if part == 0 else 1
                k = 2 * (2 * (n * (HEADS // GROUP) + g) + part)
                src = misc[:, 0:w * P].rearrange("p (t h i) -> p t h i", t=w, i=32)
                dn = den[:, 0:w * GROUP].rearrange("p (t h) -> p t h", t=w)
                dve.wait_ge(misc_full, f.total + 1)
                dve.tensor_scalar(dn, src[:, :, :, HD], 1e-6, None, ALU.max).then_inc(den_step, 1)
                dve.wait_ge(den_step, k + 1)
                dve.reciprocal(rden[:, 0:w * GROUP], den[:, 0:w * GROUP]).then_inc(den_step, 1)
                dve.wait_ge(den_step, k + 2)
                rd = rden[:, 0:w * GROUP].rearrange("p (t h) -> p t h", t=w)
                out = y_sb[:, 4 * part:4 * part + w, g * GROUP * HD:(g + 1) * GROUP * HD].rearrange("p t (h i) -> p t h i", i=HD)
                dve.tensor_tensor(out, src[:, :, :, 0:HD], rd[:, :, :, None].to_broadcast([P, w, GROUP, HD]),
                                  ALU.mult).then_inc(free, 1)
            elif name == "PJ":
                i, = args
                w = min(2, TILES - 2 * i)
                dve.wait_ge(misc_full, f.total + 1)
                if i == 0:
                    dve.wait_ge(h_copied, n + 1)
                ins = dve.tensor_tensor(h[:, 2 * i:2 * i + w, :], misc[:, 0:w * D].rearrange("p (t n) -> p t n", t=w),
                                        h[:, 2 * i:2 * i + w, :], ALU.add)
                ins.then_inc(free, 1)
            elif name == "RT":
                dve.wait_ge(misc_full, f.total + 1)
                dve.tensor_tensor(logits[:, bass.ds(n * TILES, TILES), :], misc[:, 0:TILES * EXPERTS].rearrange("p (t e) -> p t e", t=TILES),
                                  switch_b[:, None, :].to_broadcast([P, TILES, EXPERTS]), ALU.add).then_inc(free, 1)
            elif name == "COPYH":
                dve.wait_ge(slots_filled, 16 * X_BLOCKS)
                wait(dve, h_stored, 16 * n)
                wait(dve, z2_ready, n)
                dve.tensor_copy(h[:], hacc[:]).then_inc(h_copied, 1)

        def weights(n, i):
            A = weight[i % A_RING]
            dve.wait_ge(tanh_done, n * HEADS + i + 1)
            dg = A[:, 0:TILES * P].rearrange("p (t n) -> p t n", t=TILES)
            dve.scalar_tensor_tensor(dg, dg, 1.0, causal[:, None, :].to_broadcast([P, TILES, P]), ALU.add, ALU.mult)
            dve.tensor_scalar(A[:, TILES * P:TRI], A[:, TILES * P:TRI], 1.0, None, ALU.add).then_inc(weight_ready, 1)

        run(emit, opening, 0, 0, 0)
        lay_out_weights()
        program(dve, emit)

    @block.tensor
    def _(pe):
        pe.wait_ge(const_ready, 4)

        def lay_out_weights():
            pe.wait_ge(w_loaded, 16)
            for k in range(W_FILLS):
                if k >= 4:
                    pe.wait_ge(wt_dve if k % 2 else wt_act, (k - 4) // 2 + 1)
                if k == 0:
                    pe.wait_ge(pairs_ready, 1)
                c, i = divmod(k, SUB)
                for s in range(2):
                    for o in range(2):
                        if c < CHUNKS - 1:
                            band = SUB * (c % 2) + i
                            at = chunk_block(c) * P * 12 + s * BANDS + band
                            src = w_raw[:, o, at:at + 127 * 12 + 1:12]
                        else:
                            src = w_pairs[:, o, s, i, :]
                        at = (k % 4) * 512 + s * D + o * HALF
                        last = pe.transpose(score[:, at:at + HALF], src, ident[0:HALF, 0:HALF])
                last.then_inc(wt_full, 1)
            pe.wait_ge(small_loaded, 16 * 8)
            for m, raw in enumerate(attn_raw):
                if m:
                    pe.wait_ge(at_free, m)
                else:
                    pe.wait_ge(misc_free[0], Fills(0, f_open).of(0))
                for k in range(2):
                    for o in range(2):
                        last = pe.transpose(shared[0][0:HALF, k * D + o * HALF:k * D + (o + 1) * HALF],
                                            raw[:, o, k * HALF:(k + 1) * HALF], ident[0:HALF, 0:HALF])
                last.then_inc(at_full, 1)
            pe.wait_ge(at_free, 4)
            pe.wait_ge(wt_act, (W_FILLS + 1) // 2)
            pe.wait_ge(wt_dve, W_FILLS // 2)
            pe.wait_ge(ones_ready, 7)

        def emit(name, n, f, args):
            misc = shared[f.bank]
            if name in FILLS:
                wait(pe, misc_free[f.bank], f.of(f.bank))
            if name == "XT":
                q, = args
                pe.wait_ge(x_loaded, 32 * (n * X_BLOCKS + q + 1))
                for t in range(IMG_TILES):
                    last = pe.transpose(misc[:, t * P:(t + 1) * P], xraw[:, t, :], ident[:])
                last.then_inc(misc_full, 1)
            elif name == "MM":
                c, m = args
                s, i = divmod(m, SUB)
                K = n * CHUNKS + c
                if c == 0 and m == 0:
                    wait(pe, hacc_ready, n)
                if i == 0:
                    pe.wait_ge((sine_ready, cosine_ready)[s], K + 1)
                feat = (turns, whole)[s][c % RING]
                for t in range(IMG_TILES):
                    first = c == 0 and m == 0 and t % 2 == 0
                    end = c == CHUNKS - 1 and m == PIECES_OF_CHUNK - 1 and t % 2 == 1
                    last = pe.matmul(acc[:, t // 2, (t % 2) * D:(t % 2 + 1) * D],
                                     feat[:, i * IMG + t * P:i * IMG + (t + 1) * P],
                                     WT[:, 2 * (c * SUB + i) + s, :], start=first, stop=end)
                if m == PIECES_OF_CHUNK - 1:
                    last.then_inc(chunk_used, 1)
            elif name in ("ZT", "PT", "Z2T"):
                i, = args
                if name == "ZT" and i == 0:
                    pe.wait_ge(z_ready, n + 1)
                if name == "Z2T" and i == 0:
                    pe.wait_ge(z2_ready, n + 1)
                if name == "PT" and i == 0:
                    wait_free(pe, f)
                src = y_sb if name == "PT" else z
                for t in range(min(2, TILES - 2 * i)):
                    for k in range(2):
                        last = pe.transpose(misc[0:HALF, (2 * t + k) * P:(2 * t + k + 1) * P],
                                            src[:, 2 * i + t, k * HALF:(k + 1) * HALF], ident[:])
                last.then_inc(misc_full, 1)
            elif name in ("QK", "V"):
                t, = args
                cols = slice(0, 2 * D) if name == "QK" else slice(2 * D, 3 * D)
                w = cols.stop - cols.start
                if name == "QK" and t == 0:
                    wait_free(pe, f)
                for k in range(2):
                    last = pe.matmul(misc[:, 0:w], zT[:, k, t * P:(t + 1) * P], wqkvT[:, k, cols], start=k == 0, stop=k == 1)
                last.then_inc(misc_full, 1)
            elif name in ("TPQ", "TPK"):
                hp, = args
                pe.wait_ge(lo_ready, 2 * n + 2)
                at = 2 * hp + (HEADS if name == "TPK" else 0)
                for t in range(TILES):
                    last = pe.transpose(misc[:].bitcast(F16)[:, t * P:(t + 1) * P],
                                        split[:, t, at:at + 2, :].rearrange("p h i -> p (h i)"), ident16[:])
                last.then_inc(misc_full, 1)
            elif name == "S":
                i, = args
                H = n * HEADS + i
                if i % 2 == 0:
                    wait_free(pe, f)
                rows = slice(64 * (i % 2), 64 * (i % 2) + 64)
                for j, (a, b) in enumerate(HALVES):
                    wait(pe, y_done, 2 * (H - 1) + j + 1)
                    for at, t, q0, w in PIECES:
                        if not a <= at < b:
                            continue
                        last = pe.matmul(score[:, at:at + w], kT[rows, i // 2 % PAIR_RING, t * P:(t + 1) * P],
                                         qT[rows, i // 2 % PAIR_RING, q0:q0 + w], start=True, stop=True)
                    last.then_inc(score_full, 1)
            elif name == "AV":
                g, part = args
                pe.wait_ge(weight_ready, n * HEADS + GROUP * (g + 1))
                if g == 0 and part == 0:
                    wait_free(pe, f)
                lo, hi = (0, 512) if part == 0 else (512, SEQ)
                todo = []
                for at, t, q0, w in sorted(PIECES, key=lambda p: (p[1], p[2])):
                    a, b = max(lo, q0), min(hi, q0 + w)
                    if a < b:
                        todo.append((at + a - q0, t, a, b - a))
                for m, (at, t, q0, w) in enumerate(todo):
                    for r in range(GROUP):
                        head = GROUP * g + r
                        last = pe.matmul(misc[32 * r:32 * r + 32, q0 - lo:q0 - lo + w], v32[:, t, head, :],
                                         weight[head % A_RING][:, at:at + w], start=m == 0, stop=m == len(todo) - 1)
                last.then_inc(misc_full, 1)
            elif name == "YT":
                g, part = args
                if part == 0:
                    wait_free(pe, f)
                for t in range(4 if part == 0 else 1):
                    last = pe.transpose(misc[:, t * P:(t + 1) * P], yraw[:, (4 * part + t) * P:(4 * part + t + 1) * P], ident[:])
                last.then_inc(misc_full, 1)
            elif name == "PJ":
                i, = args
                if i == 0:
                    wait_free(pe, f)
                for t in range(min(2, TILES - 2 * i)):
                    for k in range(2):
                        last = pe.matmul(misc[:, t * D:(t + 1) * D], zT[:, k, (2 * i + t) * P:(2 * i + t + 1) * P],
                                         wpT[:, k, :], start=k == 0, stop=k == 1)
                last.then_inc(misc_full, 1)
            elif name == "RT":
                wait_free(pe, f)
                for t in range(TILES):
                    for k in range(2):
                        last = pe.matmul(misc[:, t * EXPERTS:(t + 1) * EXPERTS], zT[:, k, t * P:(t + 1) * P],
                                         switch_w[:, k, :], start=k == 0, stop=k == 1)
                last.then_inc(misc_full, 1)

        run(emit, opening, 0, 0, 0)
        lay_out_weights()
        program(pe, emit)


def experts(nc, ctx, io, keep):
    def sb(name, shape, dt=F32):
        return ctx.enter_context(nc.sbuf_tensor(name, shape, dt))

    def sem(name):
        return ctx.enter_context(nc.semaphore(name))

    ident, logits = keep["ident"], keep["logits"]
    sending = sb("sending", [P, ALL_TILES, WIDE])
    plain = sb("plain", [P, ALL_TILES, D])
    token = sb("token", [P, ALL_TILES], I32)
    top = sb("top", [P, ALL_TILES])
    below = sb("below", [P, ALL_TILES, EXPERTS])
    expo = sb("expo", [P, ALL_TILES, EXPERTS])
    number = sb("number", [P, EXPERTS])
    is_top = sb("is_top", [P, ALL_TILES, EXPERTS])
    route = sb("route", [P, ALL_TILES])
    onehot = sb("onehot", [P, ALL_TILES, EXPERTS])
    total = sb("total", [P, ALL_TILES])
    prob = sb("prob", [P, ALL_TILES])
    prob_e = sb("prob_e", [P, ALL_TILES, EXPERTS])
    level = sb("level", [P, LEVELS, EXPERTS])
    step_size = sb("step_size", [P, 1])
    tried = sb("tried", [P, LEVELS, EXPERTS])
    reached = sb("reached", [P, ALL_TILES, LEVELS * EXPERTS], F16)
    counts = sb("counts", [P, LEVELS * EXPERTS])
    passed = sb("passed", [P, LEVELS, EXPERTS])
    gain = sb("gain", [P, EXPERTS])
    threshold = sb("threshold", [P, EXPERTS])
    above = sb("above", [P, ALL_TILES, EXPERTS], F16)
    equal = sb("equal", [P, ALL_TILES, EXPERTS])
    tied = sb("tied", [P, ALL_TILES, EXPERTS], F16)
    room = sb("room", [P, EXPERTS])
    fits = sb("fits", [P, ALL_TILES, EXPERTS])
    kept = sb("kept", [P, ALL_TILES, EXPERTS], F16)
    first_slot = sb("first_slot", [P, EXPERTS])
    slot_e = sb("slot_e", [P, ALL_TILES, EXPERTS])
    place = sb("place", [P, ALL_TILES])
    gate = sb("pool_gate", [P, 2])
    lost = sb("lost", [P, ALL_TILES])
    slots = sb("slots", [P, ALL_TILES], U32)
    ones16 = sb("ones16", [P, P], F16)
    earlier = sb("earlier", [P, P], F16)
    b1_raw = sb("b1_raw", [EXPERTS * F_TILES, P])
    b1 = sb("b1", [P, EXPERTS * F_TILES])
    b2 = sb("b2", [BLOCK_P, EXPERTS, D])
    bias = [sb(f"bias{i}", [P, F_TILES]) for i in range(2)]
    w1 = [sb(f"w1_{i}", [P, 2, HIDDEN]) for i in range(2)]
    w2 = [sb(f"w2_{i}", [P, F_TILES, D]) for i in range(2)]
    rows = [sb(f"rows{i}", [BLOCK_P, ROWS, WIDE]) for i in range(ROWS_RING)]
    w1_hi, w1_lo = ([sb(f"w1_{half}{i}", [P, 2, HIDDEN], F16) for i in range(2)] for half in ("hi", "lo"))
    w2_hi, w2_lo = ([sb(f"w2_{half}{i}", [P, F_TILES, D], F16) for i in range(2)] for half in ("hi", "lo"))
    rows_hi = sb("rows_hi", [P, 2, BLOCK], F16)
    rows_lo = sb("rows_lo", [P, BLOCK], F16)
    hid = sb("hid", [P, 2, BLOCK])
    hid_hi, hid_lo = sb("hid_hi", [P, F_TILES, BLOCK], F16), sb("hid_lo", [P, F_TILES, BLOCK], F16)
    made = [sb(f"made{i}", [BLOCK_P, ROWS, D]) for i in range(2)]

    HB = 4
    hid_ps = ctx.enter_context(nc.psum_tensor("hid_ps", [P, HB, 512], F32))
    rowsT_ps = ctx.enter_context(nc.psum_tensor("rowsT_ps", [P, 2, 512], F32))
    made_ps = ctx.enter_context(nc.psum_tensor("made_ps", [P, 2, 512], F32))

    z_loaded, h_loaded, b1_loaded, b2_loaded = sem("z_loaded"), sem("h_loaded"), sem("b1_loaded"), sem("b2_loaded")
    token_loaded, sending_ready, sent, plain_ready, plain_stored = (
        sem("token_loaded"), sem("sending_ready"), sem("sent"), sem("plain_ready"), sem("plain_stored"))
    masks_ready, route_step, expo_ready = sem("masks_ready"), sem("route_step"), sem("expo_ready")
    try_ready, reached_ready, counted, count_read, passed_ready, gain_ready, threshold_ready, step_ready = (
        sem("try_ready"), sem("reached_ready"), sem("counted"), sem("count_read"), sem("passed_ready"),
        sem("gain_ready"), sem("threshold_ready"), sem("step_ready"))
    above_ready, tied_ready, above_counted, tied_before, kept_ready, kept_before = (
        sem("above_ready"), sem("tied_ready"), sem("above_counted"), sem("tied_before"), sem("kept_ready"), sem("kept_before"))
    slots_ready, b1_full, b1_ready = sem("slots_ready"), sem("b1_full"), sem("b1_ready")
    weights_loaded = [sem("weights_loaded0"), sem("weights_loaded1")]
    rows_loaded = [sem(f"rows_loaded{i}") for i in range(ROWS_RING)]
    made_stored = [sem("made_stored0"), sem("made_stored1")]
    rows_full, rows_hi_ready, rows_lo_ready = sem("rows_full"), sem("rows_hi_ready"), sem("rows_lo_ready")
    w_hi_ready, w_lo_ready, hid_lo_ready = sem("w_hi_ready"), sem("w_lo_ready"), sem("hid_lo_ready")
    hid_full, gelu_done, made_full, made_ready = sem("hid_full"), sem("gelu_done"), sem("made_full"), sem("made_ready")
    sum_ready, gate_ready = sem("sum_ready"), sem("gate_ready")

    SUMMED = 8
    MASKS = 2 * EXPERTS + LEVELS + 6
    block = ctx.enter_context(nc.Block())
    xs_blocks = io["xs_dram"].rearrange("(b p r) d -> b p r d", p=BLOCK_P, r=ROWS)
    out_rows = io["out"].rearrange("b s d -> (b s) d")
    STEP = 2 * PER_EXPERT
    TURNS = BLOCKS // STEP

    def wait(eng, s, value):
        if isinstance(value, int) and value <= 0:
            return
        eng.wait_ge(s, value)

    def program(eng, emit):
        for u in range(STEP):
            emit(0, u, False)
        with eng.Fori(1, TURNS - 1) as i:
            for u in range(STEP):
                emit(i, u, False)
        for u in range(STEP):
            emit(TURNS - 1, u, u == STEP - 1)

    @block.sync
    def _(sp):
        sp.dma_start(token[:], io["token"]).then_inc(token_loaded, 16)
        sp.dma_start(b1_raw[:], io["b1"].rearrange("e (f p) -> (e f) p", p=P)).then_inc(b1_loaded, 16)
        sp.dma_start(sending[:, :, 0:D], io["z2_dram"]).then_inc(z_loaded, 16)
        sp.dma_start(sending[:, :, AT_H:AT_H + D], io["h_dram"]).then_inc(h_loaded, 16)
        sp.dma_start(b2[:], io["b2"].rearrange("(o e) d -> o e d", o=1).to_broadcast([BLOCK_P, EXPERTS, D])).then_inc(b2_loaded, 16)

        def load_weights(e, side):
            of_expert = io["w1"][bass.ds(e, 1)].rearrange("o p f -> p (o f)")
            sp.dma_start(w1[side][:, 0, :], of_expert[0:P]).then_inc(weights_loaded[side], 16)
            for at in (0, REST):
                sp.dma_start(w1[side][at:at + REST, 1, :], of_expert[P:D]).then_inc(weights_loaded[side], 16)
            sp.dma_start(bias[side][:], b1[:, bass.ds(e * F_TILES, F_TILES)]).then_inc(weights_loaded[side], 16)
            sp.dma_start(w2[side][:], io["w2"][bass.ds(e, 1)].rearrange("o (f p) d -> p (o f) d", p=P)).then_inc(weights_loaded[side], 16)

        def load_rows(b, side):
            sp.dma_start(rows[side][:], xs_blocks[bass.ds(b, 1)].rearrange("o p r d -> p (o r) d")).then_inc(rows_loaded[side], 16)

        sp.wait_ge(b1_ready, 1)
        for e in range(2):
            load_weights(e, e)
        sp.wait_ge(sent, 16 * ALL_TILES)
        for b in range(2):
            load_rows(b, b)
        for b in range(BATCHES):
            sp.wait_ge(plain_ready, b + 1)
            sp.dma_start(io["out"][b].rearrange("(t p) d -> p t d", p=P), plain[:, b * TILES:(b + 1) * TILES, :]).then_inc(plain_stored, 16)

        def emit(i, u, last):
            b = i * STEP + u
            ends = isinstance(i, int) and i == TURNS - 1
            if not (ends and u >= STEP - 2):
                wait(sp, made_stored[u % 2], 16 * ROWS * (i * 2 + u // 2))
                load_rows(b + 2, (u + 2) % ROWS_RING)
            if u % PER_EXPERT == PER_EXPERT - 1 and not ends:
                sp.wait_ge(made_ready, 2 * b + 2)
                load_weights(i * 2 + u // PER_EXPERT + 2, u // PER_EXPERT)

        program(sp, emit)

    @block.gpsimd
    def _(pool):
        for e in range(EXPERTS):
            pool.memset(number[:, e:e + 1], float(e - EXPERTS)).then_inc(masks_ready, 1)
        pool.memset(earlier[:], 1.0).then_inc(masks_ready, 1)
        pool.wait_ge(masks_ready, EXPERTS + 1)
        pool.affine_select(out=earlier[:], in_=earlier[:], compare_op=ALU.is_ge, fill=0.0, base=-1,
                           pattern=[[1, P]], channel_multiplier=-1).then_inc(masks_ready, 1)
        pool.memset(ones16[:], 1.0).then_inc(masks_ready, 1)
        for e in range(EXPERTS):
            pool.memset(first_slot[:, e:e + 1], float(e * CAPACITY)).then_inc(masks_ready, 1)
        for k in range(LEVELS):
            pool.memset(level[:, k, :], float(k + 1)).then_inc(masks_ready, 1)
        pool.memset(step_size[:], 0.5).then_inc(masks_ready, 1)
        pool.memset(threshold[:], 0.0).then_inc(masks_ready, 1)
        pool.memset(gate[:], 0.0).then_inc(masks_ready, 1)
        pool.wait_ge(slots_ready, 1)
        pool.wait_ge(z_loaded, 16)
        pool.wait_ge(h_loaded, 16)
        pool.wait_ge(sending_ready, 2)
        for t in range(ALL_TILES):
            pool.indirect_dma_start(out=io["xs_dram"], out_offset=bass.IndirectOffsetOnAxis(ap=slots[:, t:t + 1], axis=0),
                                    in_=sending[:, t, :], in_offset=None, bounds_check=SLOTS - 1, oob_is_err=False).then_inc(sent, 16)
        pool.wait_ge(plain_stored, 16 * BATCHES)

        def emit(i, u, last):
            b = i * STEP + u
            wait(pool, gate_ready, b)
            pool.wait_ge(made_ready, 2 * b + 2)
            pool.tensor_tensor(gate[:, 1:2], gate[:, 0:1], gate[:, 0:1], ALU.mult).then_inc(gate_ready, 1)
            for r in range(ROWS):
                where = rows[u % ROWS_RING][:, r, AT_TOKEN:AT_TOKEN + 1].bitcast(U32)
                pool.indirect_dma_start(out=out_rows, out_offset=bass.IndirectOffsetOnAxis(ap=where, axis=0),
                                        in_=made[u % 2][:, r, :], in_offset=None, bounds_check=TOKENS - 1,
                                        oob_is_err=False).then_inc(made_stored[u % 2], 16)

        program(pool, emit)
        for side in range(2):
            pool.wait_ge(made_stored[side], 16 * ROWS * BLOCKS // 2)

    @block.scalar
    def _(act):
        act.wait_ge(route_step, 2)
        act.activation(expo[:], below[:], ACT.Exp).then_inc(expo_ready, 1)
        act.wait_ge(b1_full, 1)
        act.activation(b1[:], rowsT_ps[:, 0, 0:EXPERTS * F_TILES], ACT.Copy).then_inc(b1_ready, 1)

        def emit(i, u, last):
            b = i * STEP + u
            if isinstance(i, int) and b == 0:
                rows_high(0)
            for f in range(F_TILES):
                G = b * F_TILES + f
                act.wait_ge(hid_full, G + 1)
                if f == 0:
                    wait(act, made_full, 2 * b)
                wait(act, hid_lo_ready, G - 1)
                src, col = hid_ps[:, (u * F_TILES + f) % HB, 0:BLOCK], bias[u // PER_EXPERT][:, f:f + 1]
                act.activation(hid_hi[:, f, :], src, ACT.Gelu, scale=1 / W_SCALE, bias=col)
                act.activation(hid[:, f % 2, :], src, ACT.Gelu, scale=1 / W_SCALE, bias=col).then_inc(gelu_done, 1)
            if not last:
                rows_high(b + 1)

        def rows_high(b):
            act.wait_ge(rows_full, b + 1)
            act.activation(rows_hi[:], rowsT_ps[:, :, 0:BLOCK], ACT.Copy).then_inc(rows_hi_ready, 1)

        program(act, emit)

    @block.vector
    def _(dve):
        each = [P, ALL_TILES, EXPERTS]
        n = 0

        def step(ins):
            nonlocal n
            ins.then_inc(route_step, 1)
            n += 1
            dve.wait_ge(route_step, n)

        dve.wait_ge(masks_ready, MASKS)
        step(dve.tensor_reduce(top[:], logits[:], AX_X, ALU.max))
        step(dve.tensor_tensor(below[:], logits[:], top[:, :, None].to_broadcast(each), ALU.subtract))
        step(dve.scalar_tensor_tensor(is_top[:], below[:], 0.0, number[:, None, :].to_broadcast(each), ALU.is_ge, ALU.mult))
        step(dve.tensor_reduce(route[:], is_top[:], AX_X, ALU.min))
        step(dve.tensor_tensor(onehot[:], number[:, None, :].to_broadcast(each), route[:, :, None].to_broadcast(each), ALU.is_equal))
        dve.wait_ge(expo_ready, 1)
        step(dve.tensor_reduce(total[:], expo[:], AX_X, ALU.add))
        step(dve.reciprocal(prob[:], total[:]))
        step(dve.tensor_tensor(prob_e[:], onehot[:], prob[:, :, None].to_broadcast(each), ALU.mult))

        dve.wait_ge(token_loaded, 16)
        dve.tensor_copy(sending[:, :, AT_PROB], prob[:]).then_inc(sending_ready, 1)
        dve.tensor_copy(sending[:, :, AT_TOKEN].bitcast(I32), token[:]).then_inc(sending_ready, 1)

        def find(r):
            if not isinstance(r, int) or r > 0:
                dve.wait_ge(threshold_ready, r)
                dve.wait_ge(step_ready, r)
            dve.scalar_tensor_tensor(tried[:], level[:], step_size[:, 0:1],
                                     threshold[:, None, :].to_broadcast([P, LEVELS, EXPERTS]), ALU.mult, ALU.add)\
                .then_inc(try_ready, 1)
            dve.wait_ge(try_ready, r + 1)
            levels = [P, ALL_TILES, LEVELS, EXPERTS]
            dve.tensor_tensor(reached[:].rearrange("p t (k e) -> p t k e", e=EXPERTS),
                              prob_e[:, :, None, :].to_broadcast(levels), tried[:, None, :, :].to_broadcast(levels), ALU.is_ge)\
                .then_inc(reached_ready, 1)
            dve.wait_ge(counted, r + 1)
            dve.tensor_reduce(counts[:], made_ps[:, 0, 0:SUMMED * LEVELS * EXPERTS].rearrange("p (g m) -> p m g", g=SUMMED),
                              AX_X, ALU.add).then_inc(count_read, 1)
            dve.wait_ge(count_read, r + 1)
            dve.tensor_scalar(passed[:].rearrange("p k e -> p (k e)"), counts[:], float(CAPACITY), step_size[:, 0:1],
                              ALU.is_ge, ALU.mult).then_inc(passed_ready, 1)
            dve.wait_ge(passed_ready, r + 1)
            dve.tensor_scalar(step_size[:], step_size[:], 0.25, None, ALU.mult).then_inc(step_ready, 1)
            dve.tensor_reduce(gain[:], passed[:].rearrange("p k e -> p e k"), AX_X, ALU.add).then_inc(gain_ready, 1)
            dve.wait_ge(gain_ready, r + 1)
            dve.tensor_tensor(threshold[:], threshold[:], gain[:], ALU.add).then_inc(threshold_ready, 1)

        for u in range(2):
            find(u)
        with dve.Fori(1, ROUNDS // 2) as i:
            for u in range(2):
                find(2 * i + u)

        dve.wait_ge(threshold_ready, ROUNDS)
        limit = threshold[:, None, :].to_broadcast(each)
        dve.tensor_tensor(above[:], prob_e[:], limit, ALU.is_gt).then_inc(above_ready, 1)
        step(dve.tensor_tensor(equal[:], prob_e[:], limit, ALU.is_equal))
        dve.tensor_tensor(tied[:], equal[:], onehot[:], ALU.mult).then_inc(tied_ready, 1)
        dve.wait_ge(above_counted, 1)
        step(dve.tensor_reduce(room[:], made_ps[:, 0, 0:SUMMED * EXPERTS].rearrange("p (g e) -> p e g", g=SUMMED), AX_X, ALU.add))
        step(dve.tensor_scalar(room[:], room[:], -1.0, float(CAPACITY), ALU.mult, ALU.add))
        dve.wait_ge(tied_before, 1)
        before = made_ps[:, 1, 0:ALL_TILES * EXPERTS].rearrange("p (t e) -> p t e", e=EXPERTS)
        step(dve.tensor_tensor(fits[:], before, room[:, None, :].to_broadcast(each), ALU.is_lt))
        step(dve.tensor_tensor(fits[:], fits[:], tied[:], ALU.mult))
        dve.tensor_tensor(kept[:], fits[:], above[:], ALU.add).then_inc(kept_ready, 1)
        dve.wait_ge(kept_ready, 1)
        step(dve.tensor_reduce(lost[:], kept[:], AX_X, ALU.add))
        step(dve.tensor_scalar(lost[:], lost[:], -4.0 * SLOTS, 4.0 * SLOTS, ALU.mult, ALU.add))
        dve.wait_ge(kept_before, 1)
        before = made_ps[:, 0, 0:ALL_TILES * EXPERTS].rearrange("p (t e) -> p t e", e=EXPERTS)
        step(dve.tensor_tensor(slot_e[:], before, first_slot[:, None, :].to_broadcast(each), ALU.add))
        step(dve.tensor_tensor(slot_e[:], slot_e[:], kept[:], ALU.mult))
        step(dve.tensor_reduce(place[:], slot_e[:], AX_X, ALU.add))
        dve.tensor_tensor(slots[:], place[:], lost[:], ALU.add).then_inc(slots_ready, 1)
        dve.wait_ge(h_loaded, 16)
        dve.wait_ge(z_loaded, 16)
        for t in range(ALL_TILES):
            ins = dve.scalar_tensor_tensor(plain[:, t, :], sending[:, t, 0:D], prob[:, t:t + 1], sending[:, t, AT_H:AT_H + D],
                                           ALU.mult, ALU.add)
            if t % TILES == TILES - 1:
                ins.then_inc(plain_ready, 1)
        dve.wait_ge(b2_loaded, 16)

        def rows_low(b):
            dve.wait_ge(rows_hi_ready, b + 1)
            dve.tensor_tensor(rows_lo[:], rowsT_ps[:, 0, 0:BLOCK], rows_hi[:, 0, :], ALU.subtract)
            second = rows_hi[REST:P, 1, :]
            dve.tensor_tensor(second, rowsT_ps[REST:P, 1, 0:BLOCK], second, ALU.subtract).then_inc(rows_lo_ready, 1)

        def split_weights(e, side, round_):
            dve.wait_ge(weights_loaded[side], 80 * round_)
            for raw, hi in ((w1, w1_hi), (w2, w2_hi)):
                high = dve.tensor_scalar(hi[side][:], raw[side][:], W_SCALE, None, ALU.mult)
            high.then_inc(w_hi_ready, 1)
            dve.wait_ge(w_hi_ready, e + 1)
            for raw, hi, lo in ((w1, w1_hi, w1_lo), (w2, w2_hi, w2_lo)):
                low = dve.scalar_tensor_tensor(lo[side][:], raw[side][:], W_SCALE, hi[side][:], ALU.mult, ALU.subtract)
            low.then_inc(w_lo_ready, 1)

        def emit(i, u, last):
            b = i * STEP + u
            e = i * 2 + u // PER_EXPERT
            if isinstance(i, int) and b == 0:
                split_weights(0, 0, 1)
                rows_low(0)
            for f in range(F_TILES):
                G = b * F_TILES + f
                dve.wait_ge(gelu_done, G + 1)
                dve.tensor_tensor(hid_lo[:, f, :], hid[:, f % 2, :], hid_hi[:, f, :], ALU.subtract).then_inc(hid_lo_ready, 1)
            if not last:
                rows_low(b + 1)
            if u % PER_EXPERT == 0 and not (isinstance(i, int) and b + PER_EXPERT >= BLOCKS):
                side = 1 - u // PER_EXPERT
                split_weights(e + 1, side, i + 2 - side)
            for j in range(2):
                dve.wait_ge(made_full, 2 * b + j + 1)
                if j == 0:
                    wait(dve, made_stored[u % 2], (i * 2 + u // 2) * 16 * ROWS)
                half = made[u % 2][:, 2 * j:2 * j + 2, :]
                dve.scalar_tensor_tensor(half, made_ps[0:BLOCK_P, j, 0:2 * D].rearrange("p (r d) -> p r d", r=2), 1 / W_SCALE,
                                         b2[:, bass.ds(e, 1), :].to_broadcast([BLOCK_P, 2, D]), ALU.mult, ALU.add)\
                    .then_inc(sum_ready, 1)
                dve.wait_ge(sum_ready, 2 * b + j + 1)
                for r in (2 * j, 2 * j + 1):
                    row, result = rows[u % ROWS_RING], made[u % 2][:, r, :]
                    last_row = dve.scalar_tensor_tensor(result, result, row[:, r, AT_PROB:AT_PROB + 1], row[:, r, AT_H:AT_H + D],
                                                        ALU.mult, ALU.add)
                last_row.then_inc(made_ready, 1)

        program(dve, emit)

    @block.tensor
    def _(pe):
        pe.wait_ge(b1_loaded, 16)
        pe.transpose(rowsT_ps[:, 0, 0:EXPERTS * F_TILES], b1_raw[:], ident[0:EXPERTS * F_TILES, 0:EXPERTS * F_TILES]).then_inc(b1_full, 1)
        pe.wait_ge(masks_ready, MASKS)

        def count(bank, flags):
            width = flags.shape[2] * SUMMED
            for k in range(ALL_TILES // SUMMED):
                last = pe.matmul(made_ps[:, bank, 0:width], ones16[:],
                                 flags[:, k * SUMMED:(k + 1) * SUMMED, :].rearrange("p t m -> p (t m)"),
                                 start=k == 0, stop=k == ALL_TILES // SUMMED - 1)
            return last

        def before(bank, flags):
            out = made_ps[:, bank, 0:ALL_TILES * EXPERTS]
            pe.matmul(out, earlier[:], flags[:].rearrange("p t e -> p (t e)"), start=True, stop=False)
            for t in range(ALL_TILES - 1):
                rest = ALL_TILES - 1 - t
                last = pe.matmul(out[:, (t + 1) * EXPERTS:], ones16[:],
                                 flags[:, t:t + 1, :].to_broadcast([P, rest, EXPERTS]),
                                 start=False, stop=t == ALL_TILES - 2)
            return last

        with pe.Fori(0, ROUNDS // 2) as i:
            for u in range(2):
                pe.wait_ge(reached_ready, 2 * i + u + 1)
                count(0, reached).then_inc(counted, 1)
        pe.wait_ge(above_ready, 1)
        count(0, above).then_inc(above_counted, 1)
        pe.wait_ge(tied_ready, 1)
        before(1, tied).then_inc(tied_before, 1)
        pe.wait_ge(kept_ready, 1)
        before(0, kept).then_inc(kept_before, 1)
        pe.wait_ge(slots_ready, 1)

        def transpose_rows(side, round_, first):
            pe.wait_ge(rows_loaded[side], 16 * round_)
            if first:
                pe.wait_ge(b1_ready, 1)
            for r in range(ROWS):
                at = slice(r * BLOCK_P, (r + 1) * BLOCK_P)
                for out, cols in ((rowsT_ps[:, 0, at], slice(0, P)), (rowsT_ps[0:REST, 1, at], slice(P, D))):
                    pe.transpose(out, rows[side][:, r, cols], ident[0:BLOCK_P, 0:BLOCK_P])
                last = pe.matmul(rowsT_ps[REST:P, 1, at], rows[side][:, r, P:D], ident[0:BLOCK_P, 0:BLOCK_P],
                                 start=True, stop=True)
            last.then_inc(rows_full, 1)

        def emit(i, u, last):
            b = i * STEP + u
            side = u // PER_EXPERT
            if isinstance(i, int) and b == 0:
                transpose_rows(0, 1, True)
            pe.wait_ge(rows_lo_ready, b + 1)
            if u % PER_EXPERT == 0:
                pe.wait_ge(w_lo_ready, i * 2 + side + 1)
            for f in range(F_TILES):
                G = b * F_TILES + f
                wait(pe, gelu_done, G - HB + 1)
                cols = slice(f * P, (f + 1) * P)
                products = [(w1_hi[side][:, 0, cols], rows_hi[:, 0, :]), (w1_hi[side][:, 0, cols], rows_lo[:]),
                            (w1_lo[side][:, 0, cols], rows_hi[:, 0, :]), (w1_hi[side][:, 1, cols], rows_hi[:, 1, :]),
                            (w1_lo[side][0:REST, 1, cols], rows_hi[0:REST, 1, :])]
                for m, (w, x) in enumerate(products):
                    ins = pe.matmul(hid_ps[:, (u * F_TILES + f) % HB, 0:BLOCK], w, x, start=m == 0, stop=m == len(products) - 1)
                ins.then_inc(hid_full, 1)
            if not last:
                transpose_rows((u + 1) % ROWS_RING, i + (u + 1) // ROWS_RING + 1, False)
            wait(pe, sum_ready, 2 * b)
            for f in range(F_TILES):
                pe.wait_ge(hid_lo_ready, b * F_TILES + f + 1)
                for r in range(ROWS):
                    for x, w in ((hid_hi, w2_hi), (hid_hi, w2_lo), (hid_lo, w2_hi)):
                        first = r % 2 == 0 and f == 0 and x is hid_hi and w is w2_hi
                        ins = pe.matmul(made_ps[0:BLOCK_P, r // 2, (r % 2) * D:(r % 2 + 1) * D],
                                        x[:, f, r * BLOCK_P:(r + 1) * BLOCK_P], w[side][:, f, :],
                                        start=first, stop=r % 2 == 1 and f == F_TILES - 1 and x is hid_lo)
                    if r % 2 == 1 and f == F_TILES - 1:
                        ins.then_inc(made_full, 1)

        program(pe, emit)


def early_fusion_block(nc, x, txt, freq, W, Wq, Wk, Wv, Wproj, switch_w, switch_b, w1, b1, w2, b2, cos, sin, token, out):
    io = dict(x=x, txt=txt, freq=freq, W=W, Wq=Wq, Wk=Wk, Wv=Wv, Wproj=Wproj, switch_w=switch_w, switch_b=switch_b,
              w1=w1, b1=b1, w2=w2, b2=b2, cos=cos, sin=sin, token=token, out=out)
    io["h_dram"] = nc.dram_tensor("h_dram", [P, ALL_TILES, D], F32, kind="Internal").ap()
    io["z2_dram"] = nc.dram_tensor("z2_dram", [P, ALL_TILES, D], F32, kind="Internal").ap()
    io["xs_dram"] = nc.dram_tensor("xs_dram", [SLOTS, WIDE], F32, kind="Internal").ap()
    with ExitStack() as outer:
        def sb(name, shape):
            return outer.enter_context(nc.sbuf_tensor(name, shape, F32))
        keep = dict(ident=sb("ident", [P, P]), logits=sb("logits", [P, ALL_TILES, EXPERTS]),
                    half_pi=sb("half_pi", [P, 1]), erf_h1=sb("erf_h1", [P, 1]), erf_h2=sb("erf_h2", [P, 1]))
        with ExitStack() as ctx:
            transformer_block(nc, ctx, io, keep)
        with ExitStack() as ctx:
            experts(nc, ctx, io, keep)


def kernel(x, txt, L0_tok_freq_bands, L0_tok_W, L0_attn_Wq, L0_attn_Wk, L0_attn_Wv, L0_attn_Wproj, L0_ffn_switch_w,
           L0_ffn_switch_b, L0_ffn_w1, L0_ffn_b1, L0_ffn_w2, L0_ffn_b2):
    import numpy as _np
    import concourse.bacc as _bacc
    from concourse import mybir as _mybir
    from concourse.bass_utils import run_bass_kernel_spmd as _run

    half = HD // 2
    rate = _np.float32(1.0) / _np.float32(10000.0) ** (_np.arange(half, dtype=_np.float32) / _np.float32(half))
    angle = _np.arange(SEQ, dtype=_np.float32)[:, None] * rate[None, :]
    c, s = _np.cos(angle), _np.sin(angle)

    def tiled(a):
        return a.reshape(TILES, P, HD).transpose(1, 0, 2)

    arrays = [("x", x.reshape(BATCHES, IMG, CH)), ("txt", txt), ("freq", L0_tok_freq_bands), ("W", L0_tok_W),
              ("Wq", L0_attn_Wq), ("Wk", L0_attn_Wk), ("Wv", L0_attn_Wv), ("Wproj", L0_attn_Wproj),
              ("switch_w", L0_ffn_switch_w), ("switch_b", L0_ffn_switch_b),
              ("w1", L0_ffn_w1), ("b1", L0_ffn_b1), ("w2", L0_ffn_w2), ("b2", L0_ffn_b2),
              ("cos", tiled(_np.repeat(c, 2, axis=1))), ("sin", tiled(_np.stack([-s, s], axis=-1))),
              ("token", _np.arange(TOKENS, dtype=_np.int32).reshape(ALL_TILES, P).T)]
    nc = _bacc.Bacc("TRN2", target_bir_lowering=False, num_devices=1)
    feed, args = {}, []
    for name, a in arrays:
        a = _np.ascontiguousarray(a)
        feed[f"in_{name}"] = a
        args.append(nc.dram_tensor(f"in_{name}", a.shape, _mybir.dt.from_np(a.dtype), kind="ExternalInput").ap())
    args.append(nc.dram_tensor("out_0", (BATCHES, SEQ, D), _mybir.dt.float32, kind="ExternalOutput").ap())
    early_fusion_block(nc, *args)
    r = _run(nc, [feed], core_ids=[0])
    return r.results[0]["out_0"]
```
